# Optimizing a Trainium2 kernel written in Bass

```python
import numpy as np
import jax
import jax.numpy as jnp

def _softmax(x, axis=-1):
    return jax.nn.softmax(x, axis=axis)

def _gelu(x):
    return jax.nn.gelu(x, approximate=True)

def _silu(x):
    return jax.nn.silu(x)

def _sigmoid(x):
    return jax.nn.sigmoid(x)

def _layernorm(x, axis=-1, eps=1e-05):
    m = jnp.mean(x, axis=axis, keepdims=True)
    v = jnp.var(x, axis=axis, keepdims=True)
    return (x - m) / jnp.sqrt(v + eps)

def _scatter_add(tgt, idx, src, axis=0):
    return tgt.at[idx].add(src)

def _segment_sum(src, seg, n):
    return jax.ops.segment_sum(src, seg, n)
kernel_name = 'mk_gps_d2_gnn_r8_25d407'

def setup_inputs(seed: int=0):
    np.random.seed(seed)
    _w = jnp.asarray

    def _rec_inputs():
        import jax
        import jax.numpy as jnp
        _gk = jax.random.key(seed)
        x = -7.329e-05 + 0.9999 * jax.random.normal(jax.random.fold_in(_gk, 1), (1250, 1024), jnp.float32)
        src = jax.random.randint(jax.random.fold_in(_gk, 2), (20000,), 0, 1250, jnp.int32)
        dst = jax.random.randint(jax.random.fold_in(_gk, 3), (20000,), 0, 1250, jnp.int32)
        _o = jnp.argsort(dst, stable=True)
        src = src[_o]
        dst = dst[_o]
        edge_weight = -0.000130211 + 0.031236 * jax.random.normal(jax.random.fold_in(_gk, 12), (20000,), jnp.float32)
        return (x, src, dst, edge_weight)
    x, src, dst, edge_weight = _rec_inputs()

    def _L0_gnn_setup():
        import jax, jax.numpy as jnp
        import numpy as np
        INDIM = 1024
        OUTDIM = 1024
        NNZ = 8192
        N = 6250
        key = jax.random.key(seed)
        k1, k2, k3, k4, k5 = jax.random.split(key, 5)
        x = jax.random.normal(k1, (N, INDIM), dtype=jnp.float32)
        stdv = np.sqrt(6.0 / (INDIM + OUTDIM))
        nnz_weight = jax.random.uniform(k2, (NNZ,), dtype=jnp.float32, minval=-stdv, maxval=stdv)
        bias = jax.random.normal(k3, (OUTDIM,), dtype=jnp.float32) * 0.02
        row = jax.random.randint(k4, (NNZ,), 0, OUTDIM, dtype=jnp.int64)
        col = jax.random.randint(k5, (NNZ,), 0, INDIM, dtype=jnp.int64)
        edge_index = jnp.stack([row, col])
        return {'x': x, 'nnz_weight': nnz_weight, 'bias': bias, 'edge_index': edge_index}
    _L0_gnn_all = _L0_gnn_setup()
    _L0_gnn_in = {k: v for k, v in _L0_gnn_all.items() if k in ('bias',)}
    del _L0_gnn_all

    def _L0_mix_setup():
        import jax, jax.numpy as jnp
        import numpy as np
        B, N, D = (4, 512, 1024)
        H, DH = (16, 64)
        EPS = 1e-06
        key = jax.random.key(seed)
        ks = jax.random.split(key, 6)
        s = 1.0 / np.sqrt(D)
        return {'x': jax.random.normal(ks[0], (B, N, D), dtype=jnp.float32), 'Wq': jax.random.normal(ks[1], (D, H * DH), dtype=jnp.float32) * s, 'Wk': jax.random.normal(ks[2], (D, H * DH), dtype=jnp.float32) * s, 'Wv': jax.random.normal(ks[3], (D, H * DH), dtype=jnp.float32) * s, 'Wo': jax.random.normal(ks[4], (H * DH, D), dtype=jnp.float32) * s, 'bo': jnp.zeros((D,), dtype=jnp.float32)}
    _L0_mix_all = _L0_mix_setup()
    _L0_mix_in = {k: v for k, v in _L0_mix_all.items() if k in ('Wq', 'Wk', 'Wv', 'Wo', 'bo')}
    del _L0_mix_all

    def _L0_ffn_setup():
        import jax, jax.numpy as jnp
        import numpy as np
        INT8_MAX = 127.0

        def _absmax_scale(x, axes):
            amax = jnp.max(jnp.abs(x), axis=axes, keepdims=True)
            return jnp.maximum(amax, 1e-12) / INT8_MAX
        key = jax.random.key(seed)
        k1, k2 = jax.random.split(key)
        lhs = jax.random.normal(k1, (4, 1024, 1024), dtype=jnp.float32)
        rhs = jax.random.normal(k2, (1024, 1024), dtype=jnp.float32)
        return {'lhs': lhs, 'rhs': rhs}
    _L0_ffn_all = _L0_ffn_setup()
    _L0_ffn_in = {k: v for k, v in _L0_ffn_all.items() if k in ('rhs',)}
    del _L0_ffn_all

    def _L1_gnn_setup():
        import jax, jax.numpy as jnp
        import numpy as np
        N = 2500
        E = 40000
        D_IN = 1024
        D_OUT = 1024
        key = jax.random.key(seed)
        k1, k2, k3, k4 = jax.random.split(key, 4)
        x = jax.random.normal(k1, (N, D_IN), dtype=jnp.float32)
        edge_index = jax.random.randint(k2, (2, E), 0, N, dtype=jnp.int64)
        W = jax.random.normal(k3, (D_OUT, D_IN), dtype=jnp.float32) * (1.0 / np.sqrt(D_IN))
        b = jax.random.normal(k4, (D_OUT,), dtype=jnp.float32) * 0.01
        return {'x': x, 'edge_index': edge_index, 'W': W, 'b': b}
    _L1_gnn_all = _L1_gnn_setup()
    _L1_gnn_in = {k: v for k, v in _L1_gnn_all.items() if k in ('W', 'b')}
    del _L1_gnn_all

    def _L1_mix_setup():
        import jax, jax.numpy as jnp
        import numpy as np
        INV_SQRT_M = 1.0 / np.sqrt(256.0).astype(np.float32)

        def _kernel_features(x, random_matrix):
            x_proj = jnp.einsum('bhsd,dm->bhsm', x, random_matrix)
            return (jax.nn.elu(x_proj) + 1.0) * INV_SQRT_M
        key = jax.random.key(seed)
        ks = jax.random.split(key, 7)
        B, S, D, H, M = (4, 512, 1024, 16, 256)
        hd = D // H
        std = 1.0 / np.sqrt(D)
        return {'x': jax.random.normal(ks[0], (B, S, D), jnp.float32), 'Wq': jax.random.normal(ks[1], (D, D), jnp.float32) * std, 'bq': jnp.zeros((D,), jnp.float32), 'Wk': jax.random.normal(ks[2], (D, D), jnp.float32) * std, 'bk': jnp.zeros((D,), jnp.float32), 'Wv': jax.random.normal(ks[3], (D, D), jnp.float32) * std, 'bv': jnp.zeros((D,), jnp.float32), 'Wo': jax.random.normal(ks[4], (D, D), jnp.float32) * std, 'bo': jnp.zeros((D,), jnp.float32), 'random_matrix': jax.random.normal(ks[5], (hd, M), jnp.float32)}
    _L1_mix_all = _L1_mix_setup()
    _L1_mix_in = {k: v for k, v in _L1_mix_all.items() if k in ('Wq', 'bq', 'Wk', 'bk', 'Wv', 'bv', 'Wo', 'bo', 'random_matrix')}
    del _L1_mix_all

    def _L1_ffn_setup():
        import jax, jax.numpy as jnp
        import numpy as np
        D, F, E, K = (1024, 344, 8, 2)
        key = jax.random.key(seed)
        k0, k1, k2, k3, k4 = jax.random.split(key, 5)
        s = 0.02
        x = jax.random.normal(k0, (2, 512, D), jnp.float32)
        Ws = jax.random.normal(k1, (D, E), jnp.float32) * s
        bs = jnp.zeros((E,), jnp.float32)
        Wg = jax.random.normal(k2, (E, D, F), jnp.float32) * s
        Wu = jax.random.normal(k3, (E, D, F), jnp.float32) * s
        Wd = jax.random.normal(k4, (E, F, D), jnp.float32) * s
        return {'x': x, 'Ws': Ws, 'bs': bs, 'Wg': Wg, 'Wu': Wu, 'Wd': Wd}
    _L1_ffn_all = _L1_ffn_setup()
    _L1_ffn_in = {k: v for k, v in _L1_ffn_all.items() if k in ('Ws', 'bs', 'Wg', 'Wu', 'Wd')}
    del _L1_ffn_all
    return {'x': x, 'src': src, 'dst': dst, 'edge_weight': edge_weight, 'L0_gnn_bias': _L0_gnn_in['bias'], 'L0_mix_Wq': _L0_mix_in['Wq'], 'L0_mix_Wk': _L0_mix_in['Wk'], 'L0_mix_Wv': _L0_mix_in['Wv'], 'L0_mix_Wo': _L0_mix_in['Wo'], 'L0_mix_bo': _L0_mix_in['bo'], 'L0_ffn_rhs': _L0_ffn_in['rhs'], 'L1_gnn_W': _L1_gnn_in['W'], 'L1_gnn_b': _L1_gnn_in['b'], 'L1_mix_Wq': _L1_mix_in['Wq'], 'L1_mix_bq': _L1_mix_in['bq'], 'L1_mix_Wk': _L1_mix_in['Wk'], 'L1_mix_bk': _L1_mix_in['bk'], 'L1_mix_Wv': _L1_mix_in['Wv'], 'L1_mix_bv': _L1_mix_in['bv'], 'L1_mix_Wo': _L1_mix_in['Wo'], 'L1_mix_bo': _L1_mix_in['bo'], 'L1_mix_random_matrix': _L1_mix_in['random_matrix'], 'L1_ffn_Ws': _L1_ffn_in['Ws'], 'L1_ffn_bs': _L1_ffn_in['bs'], 'L1_ffn_Wg': _L1_ffn_in['Wg'], 'L1_ffn_Wu': _L1_ffn_in['Wu'], 'L1_ffn_Wd': _L1_ffn_in['Wd']}

def reference(x, src, dst, edge_weight, L0_gnn_bias, L0_mix_Wq, L0_mix_Wk, L0_mix_Wv, L0_mix_Wo, L0_mix_bo, L0_ffn_rhs, L1_gnn_W, L1_gnn_b, L1_mix_Wq, L1_mix_bq, L1_mix_Wk, L1_mix_bk, L1_mix_Wv, L1_mix_bv, L1_mix_Wo, L1_mix_bo, L1_mix_random_matrix, L1_ffn_Ws, L1_ffn_bs, L1_ffn_Wg, L1_ffn_Wu, L1_ffn_Wd):
    import jax
    import jax.numpy as jnp

    def _L0_gnn_ref(x, nnz_weight, bias, edge_index):
        import jax, jax.numpy as jnp
        import numpy as np
        INDIM = 1024
        OUTDIM = 1024
        NNZ = 8192
        N = 6250
        row, col = (edge_index[0], edge_index[1])
        W = jnp.zeros((OUTDIM, INDIM), dtype=nnz_weight.dtype).at[row, col].add(nnz_weight)
        return x @ W.T + bias

    def _L0_mix_ref(x, Wq, Wk, Wv, Wo, bo):
        import jax, jax.numpy as jnp
        import numpy as np
        B, N, D = (4, 512, 1024)
        H, DH = (16, 64)
        EPS = 1e-06

        def split_heads(t):
            b, n, _ = t.shape
            return t.reshape(b, n, H, DH).transpose(0, 2, 1, 3)
        q = split_heads(x @ Wq)
        k = split_heads(x @ Wk)
        v = split_heads(x @ Wv)
        q = jax.nn.elu(q) + 1.0
        k = jax.nn.elu(k) + 1.0
        k_sum = k.sum(axis=2)
        z = jnp.einsum('bhnd,bhd->bhn', q, k_sum)[..., None] + EPS
        kv = jnp.einsum('bhnd,bhne->bhde', k, v)
        out = jnp.einsum('bhnd,bhde->bhne', q, kv) / z
        out = out.transpose(0, 2, 1, 3).reshape(x.shape[0], x.shape[1], H * DH)
        return out @ Wo + bo

    def _L0_ffn_ref(lhs, rhs):
        import jax, jax.numpy as jnp
        import numpy as np
        INT8_MAX = 127.0

        def _absmax_scale(x, axes):
            amax = jnp.max(jnp.abs(x), axis=axes, keepdims=True)
            return jnp.maximum(amax, 1e-12) / INT8_MAX
        lhs_scale = _absmax_scale(lhs, (2,))
        rhs_scale = _absmax_scale(rhs, (0,))
        q_lhs = jnp.clip(jnp.round(lhs / lhs_scale), -INT8_MAX, INT8_MAX).astype(jnp.int8)
        q_rhs = jnp.clip(jnp.round(rhs / rhs_scale), -INT8_MAX, INT8_MAX).astype(jnp.int8)
        acc = jax.lax.dot_general(q_lhs, q_rhs, (((2,), (0,)), ((), ())), preferred_element_type=jnp.int32)
        return acc.astype(jnp.float32) * lhs_scale * rhs_scale

    def _L1_gnn_ref(x, edge_index, W, b):
        import jax, jax.numpy as jnp
        import numpy as np
        N = 2500
        E = 40000
        D_IN = 1024
        D_OUT = 1024
        num_nodes = x.shape[0]
        self_idx = jnp.arange(num_nodes, dtype=edge_index.dtype)
        ei = jnp.concatenate([edge_index, jnp.stack([self_idx, self_idx], axis=0)], axis=1)
        row, col = (ei[0], ei[1])
        h = jnp.einsum('nd,od->no', x, W) + b
        deg = jnp.zeros((num_nodes,), dtype=h.dtype).at[row].add(1.0)
        deg_inv_sqrt = deg ** (-0.5)
        norm = deg_inv_sqrt[row] * deg_inv_sqrt[col]
        msg = norm[:, None] * h[col]
        out = jax.ops.segment_sum(msg, row, num_segments=num_nodes)
        return out

    def _L1_mix_ref(x, Wq, bq, Wk, bk, Wv, bv, Wo, bo, random_matrix):
        import jax, jax.numpy as jnp
        import numpy as np
        INV_SQRT_M = 1.0 / np.sqrt(256.0).astype(np.float32)

        def _kernel_features(x, random_matrix):
            x_proj = jnp.einsum('bhsd,dm->bhsm', x, random_matrix)
            return (jax.nn.elu(x_proj) + 1.0) * INV_SQRT_M
        B, S, D = x.shape
        hd, M = random_matrix.shape
        H = D // hd
        q = (x @ Wq + bq).reshape(B, S, H, hd).transpose(0, 2, 1, 3)
        k = (x @ Wk + bk).reshape(B, S, H, hd).transpose(0, 2, 1, 3)
        v = (x @ Wv + bv).reshape(B, S, H, hd).transpose(0, 2, 1, 3)
        q_prime = _kernel_features(q, random_matrix)
        k_prime = _kernel_features(k, random_matrix)
        kv = jnp.einsum('bhsm,bhsd->bhmd', k_prime, v)
        k_sum = k_prime.sum(axis=2)
        out = jnp.einsum('bhsm,bhmd->bhsd', q_prime, kv)
        normalizer = jnp.einsum('bhsm,bhm->bhs', q_prime, k_sum)[..., None]
        normalizer = jnp.maximum(normalizer, 1e-06)
        out = out / normalizer
        out = out.transpose(0, 2, 1, 3).reshape(B, S, D)
        return out @ Wo + bo

    def _L1_ffn_ref(x, Ws, bs, Wg, Wu, Wd):
        import jax, jax.numpy as jnp
        import numpy as np
        D, F, E, K = (1024, 344, 8, 2)
        b, n, d = x.shape
        xt = x.reshape(-1, d)
        logits = xt @ Ws + bs
        topk_w, topk_idx = jax.lax.top_k(logits, K)
        topk_w = jax.nn.softmax(topk_w, axis=-1)
        combine = jnp.sum(jax.nn.one_hot(topk_idx, E, dtype=xt.dtype) * topk_w[..., None], axis=1)
        g = jnp.einsum('td,edf->tef', xt, Wg)
        u = jnp.einsum('td,edf->tef', xt, Wu)
        h = jax.nn.silu(g) * u
        y = jnp.einsum('tef,efd->ted', h, Wd)
        out = jnp.einsum('ted,te->td', y, combine)
        return out.reshape(b, n, d)
    edge_index = jnp.stack([src, dst])
    xn = _layernorm(x, axis=-1)
    x = x + _L0_gnn_ref(xn, edge_weight, L0_gnn_bias, edge_index) + _L0_mix_ref(xn[None], L0_mix_Wq, L0_mix_Wk, L0_mix_Wv, L0_mix_Wo, L0_mix_bo)[0]
    x = x + _L0_ffn_ref(_layernorm(x, axis=-1)[None], L0_ffn_rhs)[0]
    xn = _layernorm(x, axis=-1)
    x = x + _L1_gnn_ref(xn, edge_index, L1_gnn_W, L1_gnn_b) + _L1_mix_ref(xn[None], L1_mix_Wq, L1_mix_bq, L1_mix_Wk, L1_mix_bk, L1_mix_Wv, L1_mix_bv, L1_mix_Wo, L1_mix_bo, L1_mix_random_matrix)[0]
    x = x + _L1_ffn_ref(_layernorm(x, axis=-1)[None], L1_ffn_Ws, L1_ffn_bs, L1_ffn_Wg, L1_ffn_Wu, L1_ffn_Wd)[0]
    return x

_drawn_inputs = setup_inputs


def setup_inputs(seed=0):
    import zlib

    import numpy as np

    out = dict(_drawn_inputs(seed))
    spreads = {'L0_mix_bo': (0.0, 0.1),
     'L1_mix_bq': (0.0, 2.0),
     'L1_mix_bk': (0.0, 2.0),
     'L1_mix_bv': (0.0, 0.8),
     'L1_mix_bo': (0.0, 0.8),
     'L1_ffn_bs': (0.0, 0.8)}
    factors = {'L0_mix_Wq': 8.0,
     'L0_mix_Wk': 6.94,
     'L1_gnn_W': 6.671,
     'L1_gnn_b': 36.817,
     'L1_mix_Wq': 8.0,
     'L1_mix_Wk': 8.0,
     'L1_mix_Wv': 8.0,
     'L1_mix_Wo': 8.0,
     'L1_mix_random_matrix': 8.0,
     'L1_ffn_Ws': 8.0,
     'L1_ffn_Wg': 8.0,
     'L1_ffn_Wu': 8.0,
     'L1_ffn_Wd': 8.0}
    for name, (base, spread) in spreads.items():
        noise = np.random.default_rng([zlib.crc32(name.encode()), seed]).standard_normal(out[name].shape)
        drawn = base * np.exp(spread * noise) if base else spread * noise
        out[name] = jnp.asarray(drawn.astype(out[name].dtype))
    for name, factor in factors.items():
        out[name] = (out[name] * factor).astype(out[name].dtype)
    return out
```

```python
from contextlib import ExitStack

import numpy as np
import concourse.bass as bass
from concourse import mybir

F32, F32R, I32 = mybir.dt.float32, mybir.dt.float32r, mybir.dt.int32
ALU, ACT, AX = mybir.AluOpType, mybir.ActivationFunctionType, mybir.AxisListType
ds = bass.ds

P = 128
N = 1250
D = 1024
KT = D // P
CH = 418
NT = 3 * CH
TT = 10
NR = TT * P
E = 20000
EP = 125
ET = E // EP
H, HD = 16, 64
M = 256
NEXP, FF = 8, 344
FT = 22
ITEM = 1024
TOKS = [P] * 9 + [N - 9 * P]
VW = HD + 1
MAGIC = 1.5 * 2.0 ** 23

C_ID = 0
C_ONE = C_ID + P
C_MASK = C_ONE + P
C_IOTA8 = C_MASK + P
C_CNT = C_IOTA8 + 8
C_ALL = C_CNT


def cuts(j):
    lo, hi, out = P * j, min(P * (j + 1), NT), []
    while lo < hi:
        b = lo // CH
        end = min(hi, CH * (b + 1))
        out.append((b, lo - CH * b, lo - P * j, end - P * j))
        lo = end
    return out


def mm3(pe, out, lh, ll, rh, rl, first, last):
    pe.matmul(out, lh, rh, start=first, stop=False)
    pe.matmul(out, lh, rl, start=False, stop=False)
    return pe.matmul(out, ll, rh, start=False, stop=last)


def gps_kernel(nc, a, out):
    ctx = ExitStack()

    def sb(name, shape, dt):
        return ctx.enter_context(nc.sbuf_tensor(name, shape, dt))

    phase_sems = []

    def sem(name):
        phase_sems.append(nc.alloc_semaphore(name))
        return phase_sems[-1]

    def end_phase():
        nc.clear_and_free_semaphores(list(phase_sems))
        nc.all_engine_barrier()
        phase_sems.clear()

    def dram(name, shape):
        return nc.dram_tensor(name, shape, F32, kind="Internal").ap()

    with ctx:
        rh = sb("rh", [P, KT, NR], F32R)
        rl = sb("rl", [P, KT, NR], F32R)
        xres = sb("xres", [P, 10400], F32)
        raw = sb("raw", [P, 2, ITEM], F32)
        wh = sb("wh", [P, 4, ITEM], F32R)
        wl = sb("wl", [P, 4, ITEM], F32R)
        tmp = sb("tmp", [P, 4, NT], F32)
        cst = sb("cst", [P, C_ALL], F32)
        col = sb("col", [P, 6, TT], F32)
        bcol = sb("bcol", [P, 8, KT], F32)
        dcolq = sb("dcolq", [P, TT], F32)
        dcol = sb("dcol", [P, TT], F32)
        ps = ctx.enter_context(nc.psum_tensor("ps", [P, 8, 512], F32))
        x_t = xres[:, 0:KT * NT].rearrange("p (k t) -> p k t", k=KT)
        ident, ones, mask2 = cst[:, C_ID:C_ID + P], cst[:, C_ONE:C_ONE + P], cst[:, C_MASK:C_MASK + P]
        setA, setB = ps[:, 0:3, 0:CH], ps[:, 3:6, 0:CH]

        def rows(t):
            return t.rearrange("p (c t) -> p c t", c=3)

        cnt_s = dram("cnt_s", [TT, P, NT])
        wg_s = dram("wg_s", [KT, P, ITEM])
        att_s = dram("att_s", [KT, P, NT])
        x2_s = dram("x2_s", [P, KT, NT])
        h_s = dram("h_s", [KT * 2, P, 5 * P])

        consts_in = ctx.enter_context(nc.semaphore("consts_in"))

        spare = {}

        def high_of(k):
            return rh[:, k, 0:NT] if k < KT else spare["high"][:, k - KT, :]

        def low_of(k):
            return rl[:, k, 0:NT] if k < KT else spare["low"][:, k - KT, :]

        def with_two_more_tiles(name, phase):
            with nc.sbuf_tensor(name + "_more_high", [P, 2, NT], F32R) as spare["high"], \
                    nc.sbuf_tensor(name + "_more_low", [P, 2, NT], F32R) as spare["low"]:
                phase()

        def with_scratch(phase):
            with nc.sbuf_tensor("scratch", [P, 5120], F32) as spare["plain"]:
                phase()

        def setup():
            blk_cm = nc.Block("setup")
            with blk_cm as block:
                @block.sync
                def _(sp):
                    sp.dma_start(cst[:, :], a["consts"]).then_inc(consts_in, 16)
                    sp.dma_start(bcol[:, :, :], a["bias_cols"]).then_inc(consts_in, 16)
                    sp.wait_ge(consts_in, 32)

                @block.vector
                def _(dve):
                    dve.memset(col[:, :, :], 1.0)
                    dve.memset(dcolq[:, :], 1.0)
                    dve.memset(dcol[:, :], 1.0)
                    dve.memset(rh[:, :, NT:NR].bitcast(F32), 0.0)
                    dve.memset(rl[:, :, NT:NR].bitcast(F32), 0.0)

        def graph():
            onehot_src = rh[0:EP, 0:2, 0:NT]
            eye_slab = rh[:, 2, 0:NT]
            zeros = rl[:, 4, 0:512]
            onehot_dst = [rl[0:EP, s, 0:P] for s in range(2)]
            w_hi_dst = [rl[0:EP, s, P:2 * P] for s in range(2)]
            w_lo_dst = [rl[0:EP, s, 2 * P:3 * P] for s in range(2)]
            ident_r = rl[:, 2, 0:P]
            w_hi = rl[0:EP, 3, 0:ET]
            w_lo = rl[0:EP, 3, ET:2 * ET]
            iota = xres[:, 0:NR]
            srcf, dstf = xres[0:EP, 1280:1280 + ET], xres[0:EP, 1440:1440 + ET]
            dtile, wraw = xres[0:EP, 1600:1600 + ET], xres[0:EP, 1760:1760 + ET]
            dloc_all = xres[0:EP, 7900:7900 + TT * ET]
            hit = xres[0:EP, 2080:2080 + TT * ET]
            range_f = xres[0:1, 3680:3680 + TT * ET]
            idx = xres[0:EP, 5280:5280 + 2 * ET].bitcast(I32)
            rng_i = xres[0:1, 5600:5600 + 2 * TT].bitcast(I32)
            rng = xres[0:1, 5620:5620 + 4 * TT]
            steps = xres[0:1, 5660:5660 + ET]
            iota_col = xres[:, 5820:5821]
            tile_i = xres[0:EP, 5900:5900 + ET].bitcast(I32)
            got, prep, hits_up, ranges = sem("g_loads"), sem("g_prep"), sem("g_hits_counted"), sem("g_ranges")
            slot_free, onehots = sem("g_slot_free"), sem("g_onehots")
            eye, tile_done, tile_out = sem("g_eye"), sem("g_tile_done"), sem("g_tile_out")
            counts_out = [sem(f"g_counts_stored{s}") for s in range(2)]
            weights_out = [sem(f"g_weights_stored{s}") for s in range(2)]
            chain = sem("g_dve_chain")
            cnt_copied, deg_sqrt = sem("g_counts_copied"), sem("g_deg_sqrt")
            deg_seen = sem("g_degree_products")

            def spans(eng, table):
                vals = []
                for j in range(TT):
                    first = eng.value_load(table[0:1, 2 * j:2 * j + 1], min_val=0, max_val=ET // 2 - 1)
                    count = eng.value_load(table[0:1, 2 * j + 1:2 * j + 2], min_val=1, max_val=ET // 2)
                    vals.append((first, count))
                return vals

            with nc.Block("graph") as block:
                @block.sync
                def _(sp):
                    sp.dma_start(iota, a["iota"]).then_inc(got, 16)
                    sp.dma_start(idx[:, 0:ET], a["src"]).then_inc(got, 16)
                    sp.dma_start(idx[:, ET:2 * ET], a["dst"]).then_inc(got, 16)
                    sp.dma_start(wraw, a["edge_w"]).then_inc(got, 16)
                    sp.dma_start(iota_col, a["iota_col"]).then_inc(got, 16)

                @block.vector
                def _(dve):
                    link_n = [0]

                    def link(ins):
                        link_n[0] += 1
                        ins.then_inc(chain, 1)
                        dve.wait_ge(chain, link_n[0])

                    dve.wait_ge(got, 80)
                    dve.memset(zeros.bitcast(F32), 0.0).then_inc(prep, 1)
                    dve.tensor_copy(ident_r, ident).then_inc(prep, 1)
                    dve.tensor_copy(srcf, idx[:, 0:ET])
                    dve.tensor_copy(dstf, idx[:, ET:2 * ET])
                    link(dve.tensor_copy(w_hi, wraw))
                    dve.tensor_tensor(w_lo, wraw, w_hi.bitcast(F32), ALU.subtract)
                    link(dve.tensor_scalar(tile_i, idx[:, ET:2 * ET], 7, None, ALU.logical_shift_right))
                    link(dve.tensor_copy(dtile, tile_i))
                    for j in range(TT):
                        last = dve.tensor_scalar(hit[:, ET * j:ET * j + ET], dtile, float(j), None, ALU.is_equal)
                    last.then_inc(prep, 1)
                    for j in range(TT):
                        dve.tensor_scalar(dloc_all[:, ET * j:ET * j + ET], dstf, float(-P * j), None, ALU.add)
                    dve.tensor_scalar(steps, iota[0:1, 0:ET], 1.0, None, ALU.add)
                    dve.wait_ge(hits_up, 1)
                    link(dve.tensor_scalar(range_f.rearrange("p (b n) -> p b n", b=4), ps[0:1, 0:4, 0:400],
                                           1.0, None, ALU.min))
                    first_rev = xres[0:1, 6200:6200 + TT * ET]
                    r3 = range_f.rearrange("p (j t) -> p j t", j=TT)
                    f3 = first_rev.rearrange("p (j t) -> p j t", j=TT)
                    for j in range(TT):
                        last = dve.scalar_tensor_tensor(f3[:, j, :], steps, -1.0, r3[:, j, :], ALU.mult, ALU.mult)
                    link(last)
                    link(dve.scalar_tensor_tensor(first_rev, range_f, float(ET + 1), first_rev, ALU.mult, ALU.add))
                    for j in range(TT):
                        last = dve.tensor_tensor(r3[:, j, :], r3[:, j, :], steps, ALU.mult)
                    link(last)
                    link(dve.tensor_reduce(rng[:, 0:TT], f3, AX.X, ALU.max))
                    link(dve.tensor_reduce(rng[:, TT:2 * TT], r3, AX.X, ALU.max))
                    link(dve.tensor_scalar(rng[:, 0:TT], rng[:, 0:TT], -1.0, float(ET), ALU.mult, ALU.add))
                    link(dve.tensor_scalar(rng[:, 0:TT], rng[:, 0:TT], float(ET - 2), None, ALU.min))
                    link(dve.tensor_scalar(rng[:, TT:2 * TT], rng[:, TT:2 * TT], 1.0, None, ALU.add))
                    pairs = rng_i.rearrange("p (j c) -> p c j", c=2)
                    for c in range(2):
                        link(dve.tensor_copy(pairs[:, c, :], rng[:, c * TT:c * TT + TT]))
                    link(dve.tensor_scalar(rng_i, rng_i, 1, None, ALU.logical_shift_right))
                    link(dve.tensor_copy(rng.rearrange("p (a j c) -> p a c j", a=2, c=2)[:, 0], pairs))
                    f = rng[:, 0:2 * TT].rearrange("p (j c) -> p c j", c=2)
                    g = rng[:, 2 * TT:3 * TT]
                    link(dve.tensor_scalar(g, f[:, 0, :], 1.0, None, ALU.add))
                    link(dve.tensor_tensor(g, g, f[:, 1, :], ALU.max))
                    link(dve.tensor_tensor(g, g, f[:, 0, :], ALU.subtract))
                    dve.tensor_copy(pairs[:, 1, :], g).then_inc(ranges, 1)
                    dve.wait_ge(ranges, 1)
                    spans_d = spans(dve, rng_i)
                    base = 0
                    for j in range(TT):
                        first, count = spans_d[j]
                        dloc = xres[0:EP, 7900 + ET * j:7900 + ET * j + 2 * ET]
                        src_l = xres[0:EP, 1280:1280 + 2 * ET]
                        w_hi_l, w_lo_l = rl[0:EP, 3, 0:2 * ET], rl[0:EP, 3, ET:3 * ET]
                        if j:
                            dve.wait_ge(tile_done, j)
                        dve.tensor_scalar(eye_slab, iota[:, 0:NT], iota_col, float(P * j), ALU.subtract,
                                          ALU.is_equal).then_inc(eye, 1)
                        with dve.Fori(0, count) as i:
                            for s in range(2):
                                n = base + i * 2 + s
                                t = ds((first + i) * 2 + s, 1)
                                dve.wait_ge(slot_free, n + 1)
                                dve.tensor_scalar(onehot_src[:, s, :], iota[0:EP, 0:NT], src_l[:, t], None,
                                                  ALU.is_equal)
                                dve.tensor_scalar(onehot_dst[s], iota[0:EP, 0:P], dloc[:, t], None, ALU.is_equal)\
                                   .then_inc(onehots, 1) if j >= KT else \
                                    dve.tensor_scalar(onehot_dst[s], iota[0:EP, 0:P], dloc[:, t], None,
                                                      ALU.is_equal)
                                if j < KT:
                                    dve.tensor_scalar(w_hi_dst[s], iota[0:EP, 0:P], dloc[:, t],
                                                      w_hi_l[:, t].bitcast(F32), ALU.is_equal, ALU.mult)
                                    dve.tensor_scalar(w_lo_dst[s], iota[0:EP, 0:P], dloc[:, t],
                                                      w_lo_l[:, t].bitcast(F32), ALU.is_equal,
                                                      ALU.mult).then_inc(onehots, 1)
                        base = dve.snap(base + count * 2)
                    deg, y, v = col[:, 0, :], col[:, 1, :], col[:, 2, :]
                    dve.wait_ge(deg_sqrt, 1)
                    dve.tensor_copy(deg[:, 0:TT - 1], ps[:, 7, 0:TT - 1])
                    link(dve.tensor_copy(deg[0:NT - 9 * P, TT - 1:TT], ps[0:NT - 9 * P, 7, TT - 1:TT]))
                    link(dve.reciprocal(y, col[:, 3, :]))
                    newton(dve, link, y, deg, v)
                    link(dve.tensor_copy(dcol[:, :], y))

                @block.tensor
                def _(pe):
                    pe.sem_inc(slot_free, 2)
                    pe.wait_ge(prep, 3)
                    for b in range(4):
                        last = pe.matmul(ps[0:1, b, 0:400], ones[0:EP, 0:1], hit[:, 400 * b:400 * b + 400],
                                         start=True, stop=True)
                    last.then_inc(hits_up, 1)
                    pe.wait_ge(ranges, 1)
                    spans_p = spans(pe, rng_i)
                    base = 0
                    for j in range(TT):
                        first, count = spans_p[j]
                        pe.wait_ge(eye, j + 1)
                        if j:
                            pe.wait_ge(tile_out, 2 * j)
                        for n in range(3):
                            pe.matmul(ps[:, n, 0:CH], ident_r, eye_slab[:, CH * n:CH * n + CH],
                                      start=True, stop=False)
                        if j < KT:
                            for n in range(2):
                                pe.matmul(ps[:, 3 + n, :], zeros[:, 0:P], zeros, start=True, stop=False)
                        with pe.Fori(0, count) as i:
                            for s in range(2):
                                pe.wait_ge(onehots, base + i * 2 + s + 1)
                                for n in range(3):
                                    last = pe.matmul(ps[:, n, 0:CH], onehot_dst[s],
                                                     onehot_src[:, s, CH * n:CH * n + CH], start=False, stop=False)
                                if j < KT:
                                    for part in (w_hi_dst[s], w_lo_dst[s]):
                                        for n in range(2):
                                            last = pe.matmul(ps[:, 3 + n, :], part,
                                                             onehot_src[:, s, 512 * n:512 * n + 512],
                                                             start=False, stop=False)
                                last.then_inc(slot_free, 1)
                        base = pe.snap(base + count * 2)
                        for n in range(3):
                            last = pe.matmul(ps[:, n, 0:CH], zeros[:, 0:P], zeros[:, 0:CH], start=False, stop=True)
                        if j < KT:
                            for n in range(2):
                                last = pe.matmul(ps[:, 3 + n, :], zeros[:, 0:P], zeros, start=False, stop=True)
                        last.then_inc(tile_done, 1)
                        pe.wait_ge(cnt_copied, j + 1)
                        for r in range(TT):
                            w = min(P, NT - P * r)
                            last = pe.matmul(ps[0:w, 7, r:r + 1], tmp[:, j % 2, P * r:P * r + w], ones[:, 0:1],
                                             start=(j == 0 and r == 0), stop=(j == TT - 1),
                                             skip_group_check=True)
                        last.then_inc(deg_seen, 1)

                @block.scalar
                def _(act):
                    for j in range(TT):
                        act.wait_ge(tile_done, j + 1)
                        if j >= 2:
                            act.wait_ge(counts_out[j % 2], 16 * (j // 2))
                            act.wait_ge(deg_seen, j - 1)
                        if 2 <= j < KT:
                            act.wait_ge(weights_out[j % 2], 16 * (j // 2))
                        act.copy(rows(tmp[:, j % 2, :]), setA).then_inc(cnt_copied, 1)
                        act.wait_ge(cnt_copied, j + 1)
                        act.dma_start(cnt_s[j], tmp[:, j % 2, :]).then_inc(counts_out[j % 2], 16)
                        if j < KT:
                            act.copy(tmp[:, 2 + j % 2, 0:D].rearrange("p (c t) -> p c t", c=2),
                                     ps[:, 3:5, :]).then_inc(tile_out, 2)
                            act.wait_ge(tile_out, 2 * j + 2)
                            act.dma_start(wg_s[:, :, P * j:P * j + P].rearrange("m p f -> p m f"),
                                          tmp[:, 2 + j % 2, 0:D].rearrange("p (m f) -> p m f", m=KT))\
                               .then_inc(weights_out[j % 2], 16)
                        else:
                            act.sem_inc(tile_out, 2)
                    act.wait_ge(deg_seen, TT)
                    act.activation(col[:, 3, 0:TT - 1], ps[:, 7, 0:TT - 1], ACT.Sqrt)
                    act.activation(col[0:NT - 9 * P, 3, TT - 1:TT], ps[0:NT - 9 * P, 7, TT - 1:TT],
                                   ACT.Sqrt).then_inc(deg_sqrt, 1)
                    for s in range(2):
                        act.wait_ge(counts_out[s], 16 * TT // 2)
                        act.wait_ge(weights_out[s], 16 * KT // 2)

        def newton(dve, link, y, v, t):
            link(dve.tensor_tensor(t, y, y, ALU.mult))
            link(dve.tensor_tensor(t, t, v, ALU.mult))
            link(dve.tensor_scalar(t, t, -0.5, 1.5, ALU.mult, ALU.add))
            link(dve.tensor_tensor(y, y, t, ALU.mult))

        LEAD = 2
        SLOTS = 4

        class Chain:

            def __init__(self, eng, name, per=0):
                self.eng, self.sem, self.n, self.off, self.per = eng, sem(name), 0, 0, per

            def __call__(self, ins):
                self.n += 1
                ins.then_inc(self.sem, 1)
                self.eng.wait_ge(self.sem, self.off + self.n)

        def stream_load(sp, items, count, width, raw_in, split, unroll):
            with sp.Fori(0, count // unroll) as i:
                for q in range(unroll):
                    n = i * unroll + q
                    sp.wait_ge(split, n + 1)
                    sp.dma_start(raw[:, q % 2, 0:width], items[ds(n, 1)].rearrange("a p f -> (a p) f"))\
                      .then_inc(raw_in[q % 2], 16)

        def stream_split(pool, name, count, width, raw_in, split, used, used_of, unroll, slots=4):
            halves, claimed = sem(name + "_high_half"), sem(name + "_slot_claimed")
            pool.sem_inc(split, LEAD)
            with pool.Fori(0, count // unroll) as i:
                for q in range(unroll):
                    n = i * unroll + q
                    pool.wait_ge(raw_in[q % 2], (i * (unroll // 2) + q // 2 + 1) * 16)
                    pool.wait_ge(used, used_of(i, q))
                    pool.sem_inc(claimed, 1)
                    pool.tensor_copy(wh[:, q % slots, 0:width], raw[:, q % 2, 0:width]).then_inc(halves, 1)
                    pool.wait_ge(halves, n + 1)
                    pool.tensor_tensor(wl[:, q % slots, 0:width], raw[:, q % 2, 0:width],
                                       wh[:, q % slots, 0:width].bitcast(F32), ALU.subtract).then_inc(split, 1)

        def bank_sets(q):
            return setA if q % 2 == 0 else setB

        def broadcast_cols(pe, area, diag):
            last = None
            for j in range(TT):
                for b, c, lo, hi in cuts(j):
                    last = pe.matmul(area[:, b, c:c + hi - lo], ones, diag[:, P * j + lo:P * j + hi],
                                     start=True, stop=True)
            return last

        def node_sums(pe, bank, src, first=True, only=True):
            last = None
            for j in range(TT):
                w = min(P, NT - P * j)
                last = pe.matmul(ps[0:w, bank, j:j + 1], src[:, P * j:P * j + w], ones[:, 0:1],
                                 start=(first and j == 0), stop=only, skip_group_check=True)
            return last

        def node_cols(eng_op, dst, bank):
            eng_op(dst[:, 0:TT - 1], ps[:, bank, 0:TT - 1])
            w = NT - 9 * P
            return eng_op(dst[0:w, TT - 1:TT], ps[0:w, bank, TT - 1:TT])

        def diagonals(dve, dst, v):
            last = None
            for j in range(TT):
                w = min(P, NT - P * j)
                last = dve.tensor_scalar(dst[:, P * j:P * j + w], ident[:, 0:w], v[:, j:j + 1], None, ALU.mult)
            return last

        def layernorm(name, source=None, quantise=False):
            mean, var, rstd, std, t = (col[:, n, :] for n in range(5))
            scale = dcolq[:, :]
            top = raw[:, :, :].rearrange("p a b -> p (a b)")[:, 0:NT]
            loaded, summed, sums = sem(name + "_loaded"), sem(name + "_summed"), sem(name + "_sums")
            diag, wide = sem(name + "_diagonals"), sem(name + "_broadcast")
            centred, squared, sq_used = sem(name + "_centred"), sem(name + "_squared"), sem(name + "_squares_summed")
            rooted, var_in = sem(name + "_std"), sem(name + "_var")
            normed, high, low = sem(name + "_normed"), sem(name + "_high"), sem(name + "_low")
            turned, top_done = sem(name + "_turned"), sem(name + "_top_done")
            with nc.Block(name) as block:
                if source is not None:
                    @block.sync
                    def _(sp):
                        sp.dma_start(x_t, source).then_inc(loaded, 16)

                @block.vector
                def _(dve):
                    link = Chain(dve, name + "_chain")
                    if source is not None:
                        dve.wait_ge(loaded, 16)
                    link(dve.tensor_tensor(tmp[:, 0, :], x_t[:, 0, :], x_t[:, 1, :], ALU.add))
                    for k in range(2, KT):
                        ins = dve.tensor_tensor(tmp[:, 0, :], tmp[:, 0, :], x_t[:, k, :], ALU.add)
                        if k < KT - 1:
                            link(ins)
                        else:
                            ins.then_inc(summed, 1)
                    dve.wait_ge(sums, 1)
                    link(node_cols(lambda o, i: dve.tensor_scalar(o, i, 1.0 / D, None, ALU.mult), mean, 6))
                    diagonals(dve, tmp[:, 3, :], mean).then_inc(diag, 1)
                    if quantise:
                        link(dve.memset(top, 0.0))
                    dve.wait_ge(wide, 1)
                    for k in range(KT):
                        if k >= 2:
                            dve.wait_ge(squared, k - 1)
                        dve.tensor_tensor(rows(tmp[:, k % 2, :]), rows(x_t[:, k, :]), setA, ALU.subtract)\
                           .then_inc(centred, 1)
                        if quantise:
                            dve.wait_ge(centred, k + 1)
                            link(dve.tensor_tensor(top, tmp[:, k % 2, :], top, ALU.max))
                            link(dve.scalar_tensor_tensor(top, tmp[:, k % 2, :], -1.0, top, ALU.mult, ALU.max))
                    if quantise:
                        dve.sem_inc(top_done, 1)
                    dve.wait_ge(sq_used, KT)
                    node_cols(lambda o, i: dve.tensor_scalar(o, i, 1.0 / D, 1e-5, ALU.mult, ALU.add), var, 7)\
                        .then_inc(var_in, 1)
                    dve.wait_ge(rooted, 1)
                    link(dve.reciprocal(rstd, std))
                    newton(dve, link, rstd, var, t)
                    if quantise:
                        dve.wait_ge(turned, 1)
                        for b in range(3):
                            n = min(4, 9 - 4 * b)
                            dve.tensor_reduce(scale[:, 4 * b:4 * b + n],
                                              ps[:, 3 + b, 0:P * n].rearrange("p (j c) -> p j c", c=P), AX.X, ALU.max)
                        w = NT - 9 * P
                        link(dve.tensor_reduce(scale[0:w, 9:10], ps[0:w, 5, P:2 * P], AX.X, ALU.max))
                        link(dve.tensor_tensor(scale, scale, rstd, ALU.mult))
                        link(dve.tensor_scalar(scale, scale, 1e-12, 1.0 / 127.0, ALU.max, ALU.mult))
                        link(dve.reciprocal(t, scale))
                        link(dve.tensor_tensor(rstd, rstd, t, ALU.mult))
                    diagonals(dve, tmp[:, 3, :], rstd).then_inc(diag, 1)
                    dve.wait_ge(wide, 2)
                    for k in range(KT):
                        s = k % 3
                        if k >= 3 and not quantise:
                            dve.wait_ge(low, k - 2)
                        link(dve.tensor_tensor(rows(tmp[:, s, :]), rows(x_t[:, k, :]), setA, ALU.subtract))
                        ins = dve.tensor_tensor(rows(tmp[:, s, :]), rows(tmp[:, s, :]), setB, ALU.mult)
                        if quantise:
                            link(ins)
                            dve.tensor_scalar(rh[:, k, 0:NT], tmp[:, s, :], MAGIC, -MAGIC, ALU.add, ALU.add)
                        else:
                            ins.then_inc(normed, 1)

                @block.scalar
                def _(act):
                    for k in range(KT):
                        act.wait_ge(centred, k + 1)
                        if k < 2:
                            act.wait_ge(wide, 1)
                        else:
                            act.wait_ge(sq_used, k - 1)
                        act.activation(tmp[:, 2 + k % 2, :], tmp[:, k % 2, :], ACT.Square).then_inc(squared, 1)
                    act.wait_ge(var_in, 1)
                    act.activation(std, var, ACT.Sqrt).then_inc(rooted, 1)
                    if not quantise:
                        for k in range(KT):
                            act.wait_ge(normed, k + 1)
                            act.copy(rh[:, k, 0:NT], tmp[:, k % 3, :]).then_inc(high, 1)

                if not quantise:
                    @block.gpsimd
                    def _(pool):
                        for k in range(KT):
                            pool.wait_ge(high, k + 1)
                            pool.tensor_tensor(rl[:, k, 0:NT], tmp[:, k % 3, :], rh[:, k, 0:NT].bitcast(F32),
                                               ALU.subtract).then_inc(low, 1)

                @block.tensor
                def _(pe):
                    pe.wait_ge(summed, 1)
                    node_sums(pe, 6, tmp[:, 0, :]).then_inc(sums, 1)
                    pe.wait_ge(diag, 1)
                    broadcast_cols(pe, ps[:, 0:3, :], tmp[:, 3, :]).then_inc(wide, 1)
                    for k in range(KT):
                        pe.wait_ge(squared, k + 1)
                        node_sums(pe, 7, tmp[:, 2 + k % 2, :], first=(k == 0), only=(k == KT - 1))\
                            .then_inc(sq_used, 1)
                    if quantise:
                        pe.wait_ge(centred, KT)
                        pe.wait_ge(top_done, 1)
                        for j in range(TT):
                            w = min(P, NT - P * j)
                            last = pe.transpose(ps[0:w, 3 + j // 4, P * (j % 4):P * (j % 4) + P],
                                                top[:, P * j:P * j + w], ident)
                        last.then_inc(turned, 1)
                    pe.wait_ge(diag, 2)
                    broadcast_cols(pe, ps[:, 3:6, :], tmp[:, 3, :]).then_inc(wide, 1)

        def linear_kv():
            name = "lkv"
            kc = xres[:, 0:TT * 256].rearrange("p (j f) -> p j f", j=TT)
            vc = xres[:, 2560:2560 + TT * 260].rearrange("p (j h f) -> p j h f", j=TT, h=2)
            ex = xres[:, 7400:7912].rearrange("p (s f) -> p s f", s=2)
            raw_in = [sem(f"{name}_raw{s}") for s in range(2)]
            split, tiles = sem(name + "_split"), sem(name + "_tiles")
            freed, exped, k_in, v_in = sem(name + "_banks_free"), sem(name + "_exp"), sem(name + "_k"), sem(name + "_v")
            kv_done, kv_out, relued = sem(name + "_kv"), sem(name + "_kv_out"), sem(name + "_relu")
            v_ones = sem(name + "_ones")
            with nc.Block(name) as block:
                @block.sync
                def _(sp):
                    stream_load(sp, a["l0_kv"], 16, ITEM, raw_in, split, 4)

                @block.gpsimd
                def _(pool):
                    stream_split(pool, name, 16, ITEM, raw_in, split, tiles, lambda i, q: i * 20 + (q // 2) * 10 + 10, 4)

                @block.tensor
                def _(pe):
                    pe.sem_inc(tiles, 2 * TT)
                    pe.wait_ge(v_ones, 1)
                    with pe.Fori(0, 4) as i:
                        for half in range(2):
                            pe.wait_ge(split, i * 4 + 2 * half + 2 + LEAD)
                            for j in range(TT):
                                t = TT * half + j
                                pe.wait_ge(freed, i * 20 + t + 1)
                                for k in range(KT):
                                    s, c = 2 * half + k // 4, 256 * (k % 4)
                                    nodes = slice(P * j, P * j + P)
                                    last = mm3(pe, ps[:, t % 4, 0:256], rh[:, k, nodes], rl[:, k, nodes],
                                               wh[:, s, c:c + 256], wl[:, s, c:c + 256], k == 0, k == KT - 1)
                                last.then_inc(tiles, 1)
                        pe.wait_ge(k_in, i * 10 + 10)
                        pe.wait_ge(v_in, i * 10 + 10)
                        pe.wait_ge(kv_out, i * 4 + 1)
                        for p in range(2):
                            for j in range(TT):
                                w = TOKS[j]
                                last = pe.matmul(ps[:, 4 + p, 0:P + 1], kc[0:w, j, P * p:P * p + P],
                                                 vc[0:w, j, p, 0:P + 1], start=(j == 0), stop=(j == TT - 1))
                            last.then_inc(kv_done, 1)

                @block.scalar
                def _(act):
                    with act.Fori(0, 4) as i:
                        for j in range(TT):
                            act.wait_ge(consts_in, 32)
                            act.wait_ge(k_in, i * 10 + j)
                            act.wait_ge(tiles, i * 20 + j + 1 + 2 * TT)
                            act.activation(ex[:, j % 2, :], ps[:, j % 4, 0:256], ACT.Relu, scale=-1.0).then_inc(relued, 1)
                            act.wait_ge(consts_in, 32)
                            act.wait_ge(relued, i * 10 + j + 1)
                            act.activation(ex[:, j % 2, :], ex[:, j % 2, :], ACT.Exp, scale=-1.0).then_inc(exped, 1)
                        for j in range(TT):
                            act.wait_ge(kv_done, i * 2)
                            act.wait_ge(tiles, i * 20 + TT + j + 1 + 2 * TT)
                            act.copy(vc[:, j, :, 0:P], ps[:, (TT + j) % 4, 0:256].rearrange("p (h f) -> p h f", h=2))\
                               .then_inc(v_in, 1)

                @block.vector
                def _(dve):
                    dve.memset(vc[:, :, :, P:P + 2], 1.0).then_inc(v_ones, 1)
                    dve.sem_inc(freed, 4)
                    dve.sem_inc(kv_out, 1)
                    with dve.Fori(0, 4) as i:
                        for j in range(TT):
                            dve.wait_ge(kv_done, i * 2)
                            dve.wait_ge(exped, i * 10 + j + 1)
                            dve.scalar_tensor_tensor(kc[:, j, :], ps[:, j % 4, 0:256], 0.0, ex[:, j % 2, :],
                                                     ALU.max, ALU.add).then_inc(k_in, 1)
                            dve.wait_ge(k_in, i * 10 + j + 1)
                            dve.sem_inc(freed, 1)
                        for j in range(TT):
                            dve.wait_ge(v_in, i * 10 + j + 1)
                            dve.sem_inc(freed, 1)
                        for p in range(2):
                            dve.wait_ge(kv_done, i * 2 + p + 1)
                            dve.tensor_tensor(kvt[:, ds(2 * i + p, 1), 0:P].rearrange("p a f -> p (a f)"),
                                              ps[:, 4 + p, 0:P], mask2, ALU.mult).then_inc(kv_out, 1)
                            dve.tensor_scalar(kvt[:, ds(2 * i + p, 1), P:2 * P].rearrange("p a f -> p (a f)"),
                                              mask2, ps[:, 4 + p, P:P + 1], None, ALU.mult).then_inc(kv_out, 1)

        def linear_out():
            name = "lout"
            ex = xres[:, 7400:7400 + NT]
            zt = xres[:, 8700:8700 + 2 * CH].rearrange("p (s f) -> p s f", s=2)
            stage = xres[:, 9600:9600 + 512].rearrange("p (s f) -> p s f", s=2)
            raw_in = [sem(f"{name}_raw{s}") for s in range(2)]
            store2 = [sem(f"{name}_rows_stored{s}") for s in range(2)]
            split, used, freed = sem(name + "_split"), sem(name + "_items_used"), sem(name + "_sets_free")
            staged, relued, exped, q_in = (sem(name + x) for x in ("_staged", "_relu", "_exp", "_q"))
            num, z_in, recip, att, stored = (sem(name + x) for x in ("_num", "_z", "_recip", "_att", "_stored"))
            with nc.Block(name) as block:
                @block.sync
                def _(sp):
                    stream_load(sp, a["l0_q"], 8, ITEM, raw_in, split, 4)

                @block.gpsimd
                def _(pool):
                    stream_split(pool, name, 8, ITEM, raw_in, split, used, lambda i, q: i * 4 + q + 1, 4)

                @block.tensor
                def _(pe):
                    pe.sem_inc(used, SLOTS)

                    def attend(i, q, c):
                        n = i * 4 + q
                        cols = slice(CH * c, CH * c + CH)
                        if c == 0:
                            pe.wait_ge(q_in, n + 1)
                            pe.wait_ge(staged, n + 1)
                        pe.wait_ge(att, n * 3 + c)
                        pe.matmul(ps[:, 7, 0:CH], stage[:, q % 2, P:2 * P], tmp[:, q % 2, cols], start=True, stop=True)
                        pe.matmul(ps[:, 6, 0:CH], stage[:, q % 2, 0:P], tmp[:, q % 2, cols], start=True, stop=True)\
                          .then_inc(num, 1)

                    with pe.Fori(0, 2) as i:
                        for q in range(4):
                            pe.wait_ge(split, i * 4 + q + 1 + LEAD)
                            pe.wait_ge(freed, i * 4 + q + 1)
                            for c in range(3):
                                for k in range(KT):
                                    f, t = slice(P * k, P * k + P), slice(CH * c, CH * c + CH)
                                    last = mm3(pe, bank_sets(q)[:, c, :], wh[:, q, f], wl[:, q, f], rh[:, k, t], rl[:, k, t],
                                               k == 0, k == KT - 1)
                                if c == 2:
                                    last.then_inc(used, 1)
                                if q:
                                    attend(i, q - 1, c)
                        for c in range(3):
                            attend(i, 3, c)

                @block.scalar
                def _(act):
                    act.sem_inc(stored, 0) if False else None
                    with act.Fori(0, 2) as i:
                        for q in range(4):
                            n = i * 4 + q
                            act.wait_ge(att, i * 12 + (3 * (q - 1) if q else 0))
                            act.copy(stage[:, q % 2, :], kvt[:, ds(n, 1), :].rearrange("p a f -> p (a f)")).then_inc(staged, 1)
                            act.wait_ge(consts_in, 32)
                            act.wait_ge(q_in, n)
                            act.wait_ge(used, n + 1 + SLOTS)
                            act.activation(rows(ex), bank_sets(q), ACT.Relu, scale=-1.0).then_inc(relued, 1)
                            act.wait_ge(consts_in, 32)
                            act.wait_ge(relued, n + 1)
                            act.activation(ex, ex, ACT.Exp, scale=-1.0).then_inc(exped, 1)
                            for c in range(3):
                                act.wait_ge(consts_in, 32)
                                act.wait_ge(num, n * 3 + c + 1)
                                act.wait_ge(att, (n * 3 + c - 1) if q or c else i * 12)
                                act.activation(zt[:, (q * 3 + c) % 2, :], ps[:, 7, 0:CH], ACT.Copy, bias=1e-6)\
                                   .then_inc(z_in, 1)
                            act.wait_ge(att, n * 3 + 3)
                            act.dma_start(att_s[ds(n, 1)].rearrange("a p f -> (a p) f"), tmp[:, 2 + q % 2, :])\
                               .then_inc(store2[q % 2], 16)
                    for s in range(2):
                        act.wait_ge(store2[s], 64)

                @block.vector
                def _(dve):
                    dve.sem_inc(freed, LEAD)
                    with dve.Fori(0, 2) as i:
                        for q in range(4):
                            n = i * 4 + q
                            dve.wait_ge(exped, n + 1)
                            dve.scalar_tensor_tensor(rows(tmp[:, q % 2, :]), bank_sets(q), 0.0, rows(ex),
                                                     ALU.max, ALU.add).then_inc(q_in, 1)
                            dve.wait_ge(q_in, n + 1)
                            dve.sem_inc(freed, 1)
                            dve.wait_ge(store2[q % 2], i * 32 + (q // 2) * 16)
                            for c in range(3):
                                zs = zt[:, (q * 3 + c) % 2, :]
                                dve.wait_ge(z_in, n * 3 + c + 1)
                                dve.reciprocal(zs, zs).then_inc(recip, 1)
                                dve.wait_ge(recip, n * 3 + c + 1)
                                dve.tensor_tensor(tmp[:, 2 + q % 2, CH * c:CH * c + CH], ps[:, 6, 0:CH], zs, ALU.mult)\
                                   .then_inc(att, 1)

        def product(name, items, bias, k_tiles=KT, per=ITEM, parts=1, load=None, prep=None, passes=3, scales=None):
            raw_in = [sem(f"{name}_raw{s}") for s in range(2)]
            split, used, freed = sem(name + "_split"), sem(name + "_items_used"), sem(name + "_sets_free")
            ready, x_in = sem(name + "_resident"), sem(name + "_x_in")
            kp, count = k_tiles // parts, KT * parts
            with nc.Block(name) as block:
                @block.sync
                def _(sp):
                    if load is not None:
                        sp.dma_start(x_t, load).then_inc(x_in, 16)
                    stream_load(sp, items, count, per, raw_in, split, 4)

                @block.gpsimd
                def _(pool):
                    stream_split(pool, name, count, per, raw_in, split, used, lambda i, q: i * 4 + q + 1, 4)

                steps = prep(block, ready) if prep is not None else 0

                @block.tensor
                def _(pe):
                    if prep is not None and prep.tensor is not None:
                        prep.tensor(pe)
                    pe.sem_inc(used, SLOTS)
                    if prep is not None:
                        pe.wait_ge(ready, k_tiles)
                    with pe.Fori(0, count // 4) as i:
                        for q in range(4):
                            n = i * 4 + q
                            pe.wait_ge(split, n + 1 + LEAD)
                            m, part = q // parts, q % parts
                            if part == 0:
                                pe.wait_ge(freed, i * (4 // parts) + m + 1)
                            for k in range(kp):
                                kk = part * kp + k
                                for c in range(3):
                                    f, t = slice(P * k, P * k + P), slice(CH * c, CH * c + CH)
                                    last = mm3(pe, bank_sets(m)[:, c, :], wh[:, q, f], wl[:, q, f],
                                               high_of(kk)[:, t], low_of(kk)[:, t], kk == 0, kk == k_tiles - 1)
                            last.then_inc(used, 1)

                @block.vector
                def _(dve):
                    dve.sem_inc(freed, LEAD)
                    if prep is not None and prep.vector is not None:
                        prep.vector(dve)
                    if load is not None:
                        dve.wait_ge(x_in, 16)
                    with dve.Fori(0, count // 4) as i:
                        for m in range(4 // parts):
                            n = i * (4 // parts) + m
                            xm = x_t[:, ds(n, 1), :].rearrange("p a (c t) -> p (a c) t", c=3)
                            dve.wait_ge(used, i * 4 + (m + 1) * parts + SLOTS)
                            if bias is None:
                                ins = dve.tensor_tensor(xm, bank_sets(m), xm, ALU.add)
                            else:
                                ins = dve.scalar_tensor_tensor(xm, bank_sets(m), bcol[:, bias, ds(n, 1)], xm,
                                                               ALU.add, ALU.add)
                            ins.then_inc(freed, 1)

        class FromAttention:

            def __init__(self, name):
                self.name, self.tensor = name, None

            def __call__(self, block, ready):
                name = self.name
                got = [sem(f"{name}_rows{s}") for s in range(4)]
                high, low = sem(name + "_high"), ready

                @block.scalar
                def _(act):
                    for k in range(KT):
                        if k >= 4:
                            act.wait_ge(low, k - 3)
                        act.dma_start(tmp[:, k % 4, :], att_s[k]).then_inc(got[k % 4], 16)
                        if k >= 1:
                            j = k - 1
                            act.wait_ge(got[j % 4], 16 * (j // 4 + 1))
                            act.copy(rh[:, j, 0:NT], tmp[:, j % 4, :]).then_inc(high, 1)
                    act.wait_ge(got[3], 32)
                    act.copy(rh[:, KT - 1, 0:NT], tmp[:, 3, :]).then_inc(high, 1)

                def vector(dve):
                    for k in range(KT):
                        dve.wait_ge(high, k + 1)
                        dve.tensor_tensor(rl[:, k, 0:NT], tmp[:, k % 4, :], rh[:, k, 0:NT].bitcast(F32),
                                          ALU.subtract).then_inc(low, 1)

                self.vector = vector

        class FromCounts:

            def __init__(self, name):
                self.name = name

            def __call__(self, block, ready):
                name = self.name
                got = [sem(f"{name}_rows{s}") for s in range(3)]
                high, low, diag, wide, scaled = (sem(name + x) for x in ("_high", "_low", "_diag", "_wide", "_scaled"))
                low = ready

                @block.scalar
                def _(act):
                    for k in range(TT + 1):
                        if k < TT:
                            if k >= 3:
                                act.wait_ge(low, k - 2)
                            act.dma_start(tmp[:, k % 3, :], cnt_s[k]).then_inc(got[k % 3], 16)
                        if k >= 1:
                            j = k - 1
                            act.wait_ge(scaled, j + 1)
                            act.copy(high_of(j), tmp[:, j % 3, :]).then_inc(high, 1)

                def tensor(pe):
                    pe.wait_ge(diag, 1)
                    broadcast_cols(pe, ps[:, 0:3, :], tmp[:, 3, :]).then_inc(wide, 1)

                def vector(dve):
                    diagonals(dve, tmp[:, 3, :], dcol[:, :]).then_inc(diag, 1)
                    dve.wait_ge(wide, 1)
                    for k in range(TT + 1):
                        if k < TT:
                            dve.wait_ge(got[k % 3], 16 * (k // 3 + 1))
                            dve.scalar_tensor_tensor(rows(tmp[:, k % 3, :]), rows(tmp[:, k % 3, :]), dcol[:, k:k + 1],
                                                     setA, ALU.mult, ALU.mult).then_inc(scaled, 1)
                        if k >= 1:
                            j = k - 1
                            dve.wait_ge(high, j + 1)
                            dve.tensor_tensor(low_of(j), tmp[:, j % 3, :], high_of(j).bitcast(F32),
                                              ALU.subtract).then_inc(low, 1)

                self.vector, self.tensor = vector, tensor

        def int8_product():
            name = "ffn8"
            raw_in = [sem(f"{name}_raw{s}") for s in range(2)]
            diag, wide, slb = sem(name + "_scale_diag"), sem(name + "_scale_wide"), sem(name + "_scale_rows")
            topped, turned, colmax = sem(name + "_top"), sem(name + "_turned"), sem(name + "_colmax")
            inv_wide, quant, done, freed = (sem(name + x) for x in ("_inv_wide", "_quantised", "_products", "_free"))
            inv_diag, scaled, freed2 = sem(name + "_inv_diag"), sem(name + "_scaled"), sem(name + "_rows_added")
            scale_row, srow = tmp[:, 3, :], bcol[:, 7, :]
            part, dg, least = (tmp[:, 2, P * n:P * n + P] for n in range(3))
            with nc.Block(name) as block:
                @block.sync
                def _(sp):
                    for m in range(KT):
                        if m >= 2:
                            sp.wait_ge(quant, m - 1)
                        sp.dma_start(raw[:, m % 2, :], a["ffn_rhs"][m]).then_inc(raw_in[m % 2], 16)

                @block.vector
                def _(dve):
                    link = Chain(dve, name + "_chain")
                    diagonals(dve, scale_row, dcolq[:, :]).then_inc(diag, 1)
                    for m in range(KT + 1):
                        if m < KT:
                            w3 = raw[:, m % 2, :].rearrange("p (k f) -> p f k", k=KT)
                            wk = raw[:, m % 2, :].rearrange("p (k f) -> p k f", k=KT)
                            dve.wait_ge(raw_in[m % 2], 16 * (m // 2 + 1))
                            dve.tensor_reduce(part, w3, AX.X, ALU.max)
                            link(dve.tensor_reduce(least, w3, AX.X, ALU.min))
                            link(dve.scalar_tensor_tensor(part, least, -1.0, part, ALU.mult, ALU.max))
                            dve.sem_inc(topped, 1)
                            dve.wait_ge(turned, m + 1)
                            sc = srow[:, m:m + 1]
                            link(dve.tensor_reduce(sc, ps[:, 6, 0:P], AX.X, ALU.max))
                            link(dve.tensor_scalar(sc, sc, 1e-12, 1.0 / 127.0, ALU.max, ALU.mult))
                            link(dve.reciprocal(col[:, 0, 0:1], sc))
                            link(dve.tensor_scalar(dg, ident, col[:, 0, 0:1], None, ALU.mult))
                            dve.sem_inc(inv_diag, 1)
                            dve.wait_ge(inv_wide, m + 1)
                            for k in range(KT):
                                last = dve.tensor_tensor(wk[:, k, :], wk[:, k, :], ps[:, 7, 0:P], ALU.mult)
                            link(last)
                            dve.tensor_scalar(wh[:, m % 4, :], raw[:, m % 2, :], MAGIC, -MAGIC, ALU.add, ALU.add)\
                               .then_inc(quant, 1)
                        if m >= 1:
                            j = m - 1
                            dve.wait_ge(scaled, j + 1)
                            if j == 0:
                                dve.wait_ge(slb, 1)
                            link(dve.tensor_tensor(tmp[:, j % 2, :], tmp[:, j % 2, :], scale_row, ALU.mult))
                            dve.tensor_tensor(x_t[:, j, :], x_t[:, j, :], tmp[:, j % 2, :], ALU.add).then_inc(freed2, 1)

                @block.scalar
                def _(act):
                    act.wait_ge(wide, 1)
                    act.copy(rows(scale_row), setB).then_inc(slb, 1)
                    for m in range(KT):
                        act.wait_ge(done, m + 1)
                        if m >= 2:
                            act.wait_ge(freed2, m - 1)
                        act.activation(rows(tmp[:, m % 2, :]), bank_sets(m), ACT.Copy, scale=srow[:, m:m + 1])\
                           .then_inc(scaled, 1)

                @block.tensor
                def _(pe):
                    pe.wait_ge(diag, 1)
                    broadcast_cols(pe, ps[:, 3:6, :], scale_row).then_inc(wide, 1)
                    for m in range(KT + 1):
                        if m < KT:
                            pe.wait_ge(topped, m + 1)
                            pe.transpose(ps[:, 6, 0:P], part, ident).then_inc(turned, 1)
                            pe.wait_ge(inv_diag, m + 1)
                            pe.matmul(ps[:, 7, 0:P], ones, dg, start=True, stop=True).then_inc(inv_wide, 1)
                        if m >= 1:
                            j = m - 1
                            pe.wait_ge(quant, j + 1)
                            if j == 1:
                                pe.wait_ge(slb, 1)
                            if j >= 2:
                                pe.wait_ge(scaled, j - 1)
                            for c in range(3):
                                for k in range(KT):
                                    last = pe.matmul(bank_sets(j)[:, c, :], wh[:, j % 4, P * k:P * k + P],
                                                     rh[:, k, CH * c:CH * c + CH], start=(k == 0), stop=(k == KT - 1))
                            last.then_inc(done, 1)

        def node_major():
            name = "vh"
            v4 = v_all.rearrange("p j (h f) -> p j h f", h=H)
            brow = raw_extra[:, :]
            raw_in = [sem(f"{name}_raw{s}") for s in range(2)]
            split, tiles, freed = sem(name + "_split"), sem(name + "_tiles"), sem(name + "_banks_free")
            bias_in, chunk, x_out, v_ones = sem(name + "_bias"), sem(name + "_chunk"), sem(name + "_x_out"), sem(name + "_ones")
            h_out = [sem(f"{name}_h_stored{s}") for s in range(2)]
            hbuf = tmp[:, :, :].rearrange("p a b -> p (a b)")[:, 0:2560].rearrange("p (j f) -> p j f", j=TT)
            with nc.Block(name) as block:
                @block.sync
                def _(sp):
                    sp.dma_start(x2_s, x_t).then_inc(x_out, 16)
                    for first, used_for in ((0, 0), (8, 1)):
                        with sp.Fori(0, 2) as i:
                            for q in range(4):
                                n = i * 4 + q + first
                                if q % 2 == 0:
                                    sp.wait_ge(chunk, i * 2 + q // 2 + first // 2)
                                    sp.dma_start(brow, a["l1_vh_bias"][ds(i * 2 + q // 2 + first // 2, 1)]
                                                 .rearrange("a p f -> (a p) f")).then_inc(bias_in, 16)
                                sp.wait_ge(split, n + 1)
                                sp.dma_start(raw[:, q % 2, :], a["l1_vh"][ds(n, 1)].rearrange("a p f -> (a p) f"))\
                                  .then_inc(raw_in[q % 2], 16)

                @block.gpsimd
                def _(pool):
                    stream_split(pool, name, 16, ITEM, raw_in, split, tiles, lambda i, q: i * 20 + (q // 2) * 10 + 10, 4)

                @block.tensor
                def _(pe):
                    pe.sem_inc(tiles, 2 * TT)
                    with pe.Fori(0, 4) as i:
                        for half in range(2):
                            pe.wait_ge(split, i * 4 + 2 * half + 2 + LEAD)
                            for j in range(TT):
                                t = TT * half + j
                                pe.wait_ge(freed, i * 20 + t + 1)
                                for k in range(KT):
                                    s, c = 2 * half + k // 4, 256 * (k % 4)
                                    nodes = slice(P * j, P * j + P)
                                    last = mm3(pe, ps[:, t % 4, 0:256], rh[:, k, nodes], rl[:, k, nodes],
                                               wh[:, s, c:c + 256], wl[:, s, c:c + 256], k == 0, k == KT - 1)
                                last.then_inc(tiles, 1)

                @block.vector
                def _(dve):
                    dve.sem_inc(freed, 4)
                    dve.wait_ge(x_out, 16)
                    dve.memset(v4[:, :, :, HD:VW], 1.0)
                    for is_h in range(2):
                        with dve.Fori(0, 2) as i:
                            for half in range(2):
                                g = i * 2 + half + 4 * is_h
                                dve.wait_ge(bias_in, g * 16 + 16)
                                if is_h:
                                    dve.wait_ge(h_out[0], i * 64 + 32 * half)
                                    dve.wait_ge(h_out[1], i * 64 + 32 * half)
                                for j in range(TT):
                                    t = TT * half + j
                                    dve.wait_ge(tiles, g * TT + j + 1 + 2 * TT)
                                    if is_h:
                                        ins = dve.tensor_tensor(hbuf[:, j, :], ps[:, t % 4, 0:256], brow, ALU.add)
                                    else:
                                        dst = v4[:, j, ds((i * 2 + half) * 4, 4), 0:HD]
                                        ins = dve.tensor_tensor(dst, ps[:, t % 4, 0:256].rearrange(
                                            "p (h f) -> p h f", h=4), brow.rearrange("p (h f) -> p h f", h=4), ALU.add)
                                    ins.then_inc(freed, 1)
                                dve.wait_ge(freed, g * TT + TT + 4)
                                dve.sem_inc(chunk, 1)

                @block.scalar
                def _(act):
                    with act.Fori(0, 2) as i:
                        for half in range(2):
                            g = i * 2 + half
                            act.wait_ge(chunk, g + 5)
                            for u in range(2):
                                for part in range(2):
                                    act.dma_start(h_s[ds(g * 4 + 2 * u + part, 1)].rearrange("a p (k f) -> (a p) k f", k=5),
                                                  hbuf[:, 5 * part:5 * part + 5, P * u:P * u + P])\
                                       .then_inc(h_out[part], 16)
                    for part in range(2):
                        act.wait_ge(h_out[part], 128)

        def feature_attention():
            name = "fa"
            guard = float(np.float32(1e-6)) * M
            space_a, space_b = spare["plain"][:, 0:2560], spare["plain"][:, 2560:5120]
            kf = space_a[:, 0:1024].rearrange("p (s f) -> p s f", s=2)
            ex = space_a[:, 1024:2048].rearrange("p (s f) -> p s f", s=2)
            table = space_a[:, 2048:2560].rearrange("p (x f) -> p x f", x=4)
            qf = space_b[:, 0:4 * CH].rearrange("p (s f) -> p s f", s=4)
            ez = space_b[:, 4 * CH:5 * CH]
            rm = raw_extra[:, :]
            k_t, q_t = tmp[:, 0, :], tmp[:, 1, :]
            v4 = v_all.rearrange("p j (h f) -> p j h f", h=H)
            raw_in = [sem(f"{name}_raw{s}") for s in range(2)]
            stored = [sem(f"{name}_stored{s}") for s in range(2)]
            rm_in, split, used, k_in, q_in = (sem(name + x) for x in ("_rm_in", "_split", "_items_used", "_k", "_q"))
            kproj, kfeat, kv_used, tables = (sem(name + x) for x in ("_k_projected", "_k_features", "_kv", "_tables"))
            qproj, qfeat, outs, att = (sem(name + x) for x in ("_q_projected", "_q_features", "_outs", "_att"))
            relued, exped, ez_in, recip = (sem(name + x) for x in ("_relu", "_exp", "_norm", "_recip"))
            PIECES = 12
            ACTS = TT + PIECES

            def out_bank(c, h):
                return (3 if c % 2 == 0 else 1) + h

            def k_bank(w, j):
                b = (6, 1)[j % 2]
                return ps[0:w, b:b + 2, 0:M]

            def halves_of(t, w, j):
                return t[0:w, j % 2, :].rearrange("p (h f) -> p h f", h=2)

            def k_ex(w, j):
                return halves_of(ex, w, j)

            def q_bank(x):
                return ((6, 7), (0, 5))[x // 2 % 2][x % 2]

            with nc.Block(name) as block:
                @block.sync
                def _(sp):
                    sp.dma_start(rm, a["rm"]).then_inc(rm_in, 16)
                    stream_load(sp, a["l1_kq"], 16, ITEM, raw_in, split, 4)

                @block.gpsimd
                def _(pool):
                    stream_split(pool, name, 16, ITEM, raw_in, split, used, lambda i, q: i * 4 + q + 1, 4)

                @block.tensor
                def _(pe):
                    pe.sem_inc(used, SLOTS)
                    pe.wait_ge(rm_in, 16)

                    def gemm(area, slot):
                        for c in range(3):
                            for k in range(KT):
                                f, t = slice(P * k, P * k + P), slice(CH * c, CH * c + CH)
                                last = mm3(pe, area[:, c, :], wh[:, slot, f], wl[:, slot, f], rh[:, k, t], rl[:, k, t],
                                           k == 0, k == KT - 1)
                        last.then_inc(used, 1)

                    def kv_product(n, p, i, j):
                        w = TOKS[j]
                        pe.wait_ge(kfeat, n * TT + j + 1)
                        for x in range(4):
                            last = pe.matmul(ps[:, 0, VW * x:VW * x + VW], kf[0:w, j % 2, P * x:P * x + P],
                                             v4[0:w, j, ds(i * 4 + 2 * p + x // 2, 1), :].rearrange("p a f -> p (a f)"),
                                             start=(j == 0 and x == 0), stop=(j == TT - 1), skip_group_check=True)
                        last.then_inc(kv_used, 1)

                    def out_product(n, x):
                        c, mh, h = x // 4, x // 2 % 2, x % 2
                        pe.wait_ge(qfeat, n * PIECES + x + 1)
                        if x == 0:
                            pe.wait_ge(tables, n + 1)
                        if x == 8:
                            pe.wait_ge(att, n * 3 + 2)
                        pe.matmul(ps[:, out_bank(c, h), 0:CH], table[:, 2 * h + mh, :], qf[:, x % 4, :],
                                  start=(mh == 0), stop=(mh == 1)).then_inc(outs, 1)

                    with pe.Fori(0, 4) as i:
                        for p in range(2):
                            n = i * 2 + p
                            pe.wait_ge(split, i * 4 + 2 * p + 1 + LEAD)
                            pe.wait_ge(tables, n)
                            pe.wait_ge(att, n * 3)
                            gemm(setA, 2 * p)
                            pe.wait_ge(split, i * 4 + 2 * p + 2 + LEAD)
                            pe.wait_ge(att, n * 3 + 1)
                            gemm(setB, 2 * p + 1)
                            pe.wait_ge(k_in, n + 1)
                            for j in range(TT):
                                w = TOKS[j]
                                if j >= 2:
                                    pe.wait_ge(kfeat, n * TT + j - 1)
                                for h in range(2):
                                    r = slice(HD * h, HD * h + HD)
                                    last = pe.matmul(k_bank(w, j)[:, h, :], k_t[r, P * j:P * j + w],
                                                     rm[r, :], start=True, stop=True)
                                last.then_inc(kproj, 1)
                                if j:
                                    kv_product(n, p, i, j - 1)
                            kv_product(n, p, i, TT - 1)
                            pe.wait_ge(q_in, n + 1)
                            for y in range(PIECES // 2):
                                c, mh = y // 2, y % 2
                                if y == 1:
                                    pe.wait_ge(tables, n + 1)
                                if y >= 2:
                                    pe.wait_ge(qfeat, n * PIECES + 2 * y - 2)
                                for h in range(2):
                                    r = slice(HD * h, HD * h + HD)
                                    pe.matmul(ps[:, q_bank(2 * y + h), 0:CH], rm[r, P * mh:P * mh + P],
                                              q_t[r, CH * c:CH * c + CH], start=True, stop=True).then_inc(qproj, 1)
                                if y:
                                    out_product(n, 2 * y - 2)
                                    out_product(n, 2 * y - 1)
                            out_product(n, PIECES - 2)
                            out_product(n, PIECES - 1)

                @block.scalar
                def _(act):
                    def relu_exp(dst, src, count):
                        act.activation(dst, src, ACT.Relu, scale=-1.0).then_inc(relued, 1)
                        act.wait_ge(relued, count)
                        act.activation(dst, dst, ACT.Exp, scale=-1.0).then_inc(exped, 1)

                    with act.Fori(0, 4) as i:
                        for p in range(2):
                            n = i * 2 + p
                            for j in range(TT):
                                w = TOKS[j]
                                if j < 2:
                                    act.wait_ge(qfeat, n * PIECES)
                                else:
                                    act.wait_ge(kfeat, n * TT + j - 1)
                                act.wait_ge(kproj, n * TT + j + 1)
                                relu_exp(k_ex(w, j), k_bank(w, j), n * ACTS + j + 1)
                            for x in range(PIECES):
                                if x < 2:
                                    act.wait_ge(kfeat, n * TT + TT)
                                else:
                                    act.wait_ge(qfeat, n * PIECES + x - 1)
                                act.wait_ge(qproj, n * PIECES + x + 1)
                                relu_exp(ex[:, x % 2, 0:CH], ps[:, q_bank(x), 0:CH], n * ACTS + TT + x + 1)
                            act.wait_ge(att, n * 3 + 4)
                            act.dma_start(att_s[ds(n, 1)].rearrange("a p f -> (a p) f"), tmp[:, 2 + p, :])\
                               .then_inc(stored[p], 16)
                    for p in range(2):
                        act.wait_ge(stored[p], 64)

                @block.vector
                def _(dve):
                    dve.sem_inc(att, 1)
                    lo, hi = slice(0, HD), slice(HD, P)

                    def divide(n, p, c):
                        m, cols = n * 3 + c, slice(CH * c, CH * c + CH)
                        a_b, b_b = ps[:, out_bank(c, 0), 0:CH], ps[:, out_bank(c, 1), 0:CH]
                        dve.wait_ge(outs, n * PIECES + 4 * c + 4)
                        dve.wait_ge(att, m + 1)
                        dve.tensor_scalar(ez[lo, :], a_b[hi, :], guard, None, ALU.max).then_inc(ez_in, 1)
                        dve.tensor_scalar(ez[hi, :], b_b[lo, :], guard, None, ALU.max).then_inc(ez_in, 1)
                        dve.wait_ge(ez_in, m * 2 + 2)
                        dve.reciprocal(ez, ez).then_inc(recip, 1)
                        dve.wait_ge(recip, m + 1)
                        dve.tensor_tensor(tmp[lo, 2 + p, cols], a_b[lo, :], ez[lo, :], ALU.mult)
                        dve.tensor_tensor(tmp[hi, 2 + p, cols], b_b[hi, :], ez[hi, :], ALU.mult).then_inc(att, 1)

                    with dve.Fori(0, 4) as i:
                        for p in range(2):
                            n = i * 2 + p
                            for half, (area, dst, done, b) in enumerate(((setA, k_t, k_in, 2), (setB, q_t, q_in, 3))):
                                dve.wait_ge(used, i * 4 + 2 * p + half + 1 + SLOTS)
                                dve.tensor_scalar(rows(dst), area, bcol[:, b, ds(n, 1)], None, ALU.add)\
                                   .then_inc(done, 1)
                            for j in range(TT):
                                w = TOKS[j]
                                dve.wait_ge(kv_used, n * TT + max(j - 1, 0))
                                dve.wait_ge(exped, n * ACTS + j + 1)
                                dve.scalar_tensor_tensor(halves_of(kf, w, j), k_bank(w, j), 0.0, k_ex(w, j), ALU.max,
                                                         ALU.add).then_inc(kfeat, 1)
                            dve.wait_ge(kv_used, n * TT + TT)
                            kv = ps[:, 0, 0:4 * VW].rearrange("p (x f) -> p x f", x=4)
                            dve.tensor_copy(table[:, 0:2, lo], kv[:, 0:2, 0:HD])
                            dve.tensor_copy(table[:, 2:4, hi], kv[:, 2:4, 0:HD])
                            for x in range(4):
                                ins = dve.tensor_scalar(table[:, x, hi if x < 2 else lo], ones[:, 0:HD],
                                                        kv[:, x, HD:VW], None, ALU.mult)
                            ins.then_inc(tables, 1)
                            dve.wait_ge(stored[p], i * 16)
                            for x in range(PIECES):
                                dve.wait_ge(outs, n * PIECES + max(x - 3, 0))
                                dve.wait_ge(exped, n * ACTS + TT + x + 1)
                                dve.scalar_tensor_tensor(qf[:, x % 4, :], ps[:, q_bank(x), 0:CH], 0.0,
                                                         ex[:, x % 2, 0:CH], ALU.max, ALU.add).then_inc(qfeat, 1)
                                if x % 4 == 1 and x > 4:
                                    divide(n, p, x // 4 - 1)
                            divide(n, p, 2)

        def gating():
            name = "gate"
            ws = raw[:, 0, 0:KT * NEXP]
            bs = raw[:, 1, 0:TT * NEXP].rearrange("p (j e) -> p j e", j=TT)
            ws_h, ws_l = wh[:, 0, 0:KT * NEXP], wl[:, 0, 0:KT * NEXP]
            work = tmp[:, 0, :]

            def grid(n):
                return work[:, TT * NEXP * n:TT * NEXP * (n + 1)].rearrange("p (j e) -> p j e", j=TT)

            logits, is_top, first, second, rank = (grid(n) for n in range(5))
            t0 = TT * NEXP * 5
            top1, top2, pick, e2, total = (work[:, t0 + TT * n:t0 + TT * n + TT].rearrange("p (j o) -> p j o", o=1)
                                           for n in range(5))
            high = wh[:, 1, 0:TT * NEXP].rearrange("p (j e) -> p j e", j=TT)
            both = tmp[:, 1, 0:40 * TT].rearrange("p (j e) -> p j e", j=TT)
            loaded, halves, products, gap, ratio = (sem(name + x) for x in
                                                    ("_loaded", "_halves", "_logits", "_gap", "_ratio"))
            ready, turned, placed = sem(name + "_ready"), sem(name + "_turned"), sem(name + "_placed")
            with nc.Block(name) as block:
                @block.sync
                def _(sp):
                    sp.dma_start(ws, a["Ws"]).then_inc(loaded, 16)
                    sp.dma_start(bs, a["bs"].rearrange("p (j e) -> p j e", j=TT)).then_inc(loaded, 16)

                @block.tensor
                def _(pe):
                    pe.wait_ge(halves, 1)
                    for j in range(TT):
                        nodes = slice(P * j, P * j + P)
                        for k in range(KT):
                            e = slice(NEXP * k, NEXP * k + NEXP)
                            out = ps[:, 0, NEXP * j:NEXP * j + NEXP]
                            for n, (l, r) in enumerate(((rh, ws_h), (rh, ws_l), (rl, ws_h))):
                                last = pe.matmul(out, l[:, k, nodes], r[:, e], start=(j == 0 and k == 0 and n == 0),
                                                 stop=(k == KT - 1 and n == 2), skip_group_check=True)
                    last.then_inc(products, 1)
                    pe.wait_ge(ready, 1)
                    for j in range(TT):
                        last = pe.transpose(ps[0:40, 3 + j // 4, P * (j % 4):P * (j % 4) + P], both[:, j, :], ident)
                    last.then_inc(turned, 1)

                @block.vector
                def _(dve):
                    link = Chain(dve, name + "_chain")

                    def wide(fn, out, full, narrow, *ops):
                        f, n = bass.broadcast_tensor_aps(full, narrow)
                        return fn(out, f, n, *ops)

                    iota8 = cst[:, C_IOTA8:C_IOTA8 + NEXP].rearrange("p (o e) -> p o e", o=1)
                    dve.wait_ge(loaded, 32)
                    dve.memset(both, 0.0)
                    link(dve.tensor_copy(ws_h, ws))
                    dve.tensor_tensor(ws_l, ws, ws_h.bitcast(F32), ALU.subtract).then_inc(halves, 1)
                    dve.wait_ge(products, 1)
                    link(dve.tensor_tensor(logits, ps[:, 0, 0:TT * NEXP].rearrange("p (j e) -> p j e", j=TT), bs, ALU.add))

                    def choose(one_hot, top, best):
                        link(dve.tensor_reduce(top, logits, AX.X, ALU.max))
                        link(wide(dve.tensor_tensor, is_top, logits, top, ALU.is_equal))
                        link(wide(dve.tensor_tensor, rank, is_top, iota8, ALU.mult))
                        link(dve.tensor_reduce(best, rank, AX.X, ALU.max))
                        link(wide(dve.tensor_tensor, one_hot, rank, best, ALU.is_equal))

                    choose(first, top1, pick)
                    big = float(np.finfo(np.float32).max)
                    link(dve.tensor_scalar(is_top, first, -2.0, 1.0, ALU.mult, ALU.add))
                    link(dve.scalar_tensor_tensor(logits, is_top, big, logits, ALU.mult, ALU.min))
                    choose(second, top2, pick)
                    dve.tensor_tensor(e2, top2, top1, ALU.subtract).then_inc(gap, 1)
                    dve.wait_ge(ratio, 1)
                    link(dve.tensor_scalar(total, e2, 1.0, None, ALU.add))
                    link(dve.reciprocal(total, total))
                    link(dve.tensor_tensor(e2, e2, total, ALU.mult))
                    link(wide(dve.tensor_tensor, first, first, total, ALU.mult))
                    link(wide(dve.tensor_tensor, second, second, e2, ALU.mult))
                    link(dve.tensor_tensor(first, first, second, ALU.add))
                    link(dve.tensor_copy(high, first))
                    dve.tensor_copy(both[:, :, 0:NEXP], high.bitcast(F32))
                    dve.tensor_tensor(both[:, :, 32:32 + NEXP], first, high.bitcast(F32), ALU.subtract).then_inc(ready, 1)
                    dve.wait_ge(turned, 1)
                    dve.tensor_copy(wh[0:40, 3, 0:512], ps[0:40, 3, :])
                    dve.tensor_copy(wh[0:40, 3, 512:2 * CH], ps[0:40, 4, 0:2 * CH - 512])
                    dve.tensor_copy(wl[0:40, 3, 0:D - 2 * CH], ps[0:40, 4, 2 * CH - 512:512])
                    dve.tensor_copy(wl[0:40, 3, D - 2 * CH:CH], ps[0:40, 5, 0:NT - D]).then_inc(placed, 1)

                @block.scalar
                def _(act):
                    act.wait_ge(gap, 1)
                    act.activation(e2, e2, ACT.Exp).then_inc(ratio, 1)

        def experts():
            name = "moe"
            raw_in = [sem(f"{name}_raw{s}") for s in range(2)]
            split, used, sel_in, sel_set = (sem(name + x) for x in ("_split", "_items_used", "_sel_in", "_selector"))
            wide, gated, weighed, hidden = (sem(name + x) for x in ("_wide", "_gated", "_weighed", "_hidden"))
            high, low, y_done, added = (sem(name + x) for x in ("_high", "_low", "_y_products", "_y_added"))
            sel = wl[0:40, 3, 512:512 + 2 * P]
            sel_raw = raw_extra[0:40, :]
            STEPS, YS = FT // 2, 2 * KT

            def weights_of(c):
                return wh[0:40, 3, CH * c:CH * c + CH] if c < 2 else wl[0:40, 3, 0:CH]

            with nc.Block(name) as block:
                @block.sync
                def _(sp):
                    stream_load(sp, a["moe"], 6 * STEPS, ITEM, raw_in, split, 6)

                @block.gpsimd
                def _(pool):
                    stream_split(pool, name, 6 * STEPS, ITEM, raw_in, split, used, lambda i, q: i * 6 + q + 1, 6, slots=3)

                @block.tensor
                def _(pe):
                    pe.sem_inc(used, 3)

                    def gemm(area, slot, c):
                        for k in range(KT):
                            f, t = slice(P * k, P * k + P), slice(CH * c, CH * c + CH)
                            last = mm3(pe, area[:, c, :], wh[:, slot, f], wl[:, slot, f], rh[:, k, t], rl[:, k, t],
                                       k == 0, k == KT - 1)
                        return last

                    def spread(x, c):
                        pe.matmul(ps[:, 6 + c % 2, 0:CH], sel[:, P * x:P * x + P], weights_of(c), start=True, stop=True)\
                          .then_inc(wide, 1)

                    with pe.Fori(0, STEPS) as i:
                        for x in range(2):
                            pe.wait_ge(split, i * 6 + 2 * x + 1 + LEAD)
                            if x == 0:
                                pe.wait_ge(added, i * YS + 1)
                            else:
                                pe.wait_ge(gated, i * 2 + 1)
                            gemm(setA, 2 * x % 3, 0)
                            gemm(setA, 2 * x % 3, 1)
                            gemm(setA, 2 * x % 3, 2).then_inc(used, 1)
                            pe.wait_ge(sel_set, i + 1)
                            pe.wait_ge(weighed, i * 6 + 3 * x)
                            spread(x, 0)
                            spread(x, 1)
                            pe.wait_ge(split, i * 6 + 2 * x + 2 + LEAD)
                            if x == 0:
                                pe.wait_ge(added, i * YS + 2)
                            else:
                                pe.wait_ge(hidden, i * 2 + 1)
                            gemm(setB, (2 * x + 1) % 3, 0)
                            gemm(setB, (2 * x + 1) % 3, 1)
                            pe.wait_ge(weighed, i * 6 + 3 * x + 1)
                            spread(x, 2)
                            gemm(setB, (2 * x + 1) % 3, 2).then_inc(used, 1)
                        for n in range(YS):
                            x, m = n // KT, n % KT
                            if m == 0:
                                pe.wait_ge(split, i * 6 + 5 + x + LEAD)
                                pe.wait_ge(low, i * 2 + x + 1)
                            if n == 0:
                                pe.wait_ge(gated, i * 2 + 2)
                            elif n == 1:
                                pe.wait_ge(hidden, i * 2 + 2)
                            else:
                                pe.wait_ge(added, i * YS + n + 1)
                            for c in range(3):
                                f, t = slice(P * m, P * m + P), slice(CH * c, CH * c + CH)
                                last = mm3(pe, bank_sets(m)[:, c, :], wh[:, 1 + x, f], wl[:, 1 + x, f],
                                           high_of(KT + x)[:, t], low_of(KT + x)[:, t], True, True)
                            last.then_inc(y_done, 1)
                            if m == KT - 1:
                                pe.wait_ge(y_done, i * YS + n + 1)
                                pe.sem_inc(used, 1)

                @block.scalar
                def _(act):
                    with act.Fori(0, STEPS) as i:
                        act.wait_ge(sel_set, i)
                        act.dma_start(sel_raw, a["sel"][ds(i, 1)].rearrange("a p f -> (a p) f")).then_inc(sel_in, 16)
                        act.wait_ge(sel_in, i * 16 + 16)
                        act.wait_ge(weighed, i * 6)
                        act.copy(sel, sel_raw).then_inc(sel_set, 1)
                        for x in range(2):
                            act.wait_ge(used, i * 6 + 2 * x + 1 + 3)
                            act.wait_ge(low, i * 2 + x)
                            act.activation(rows(tmp[:, x, :]), setA, ACT.Silu).then_inc(gated, 1)
                            act.wait_ge(hidden, i * 2 + x + 1)
                            act.copy(high_of(KT + x), tmp[:, 2 + x, :]).then_inc(high, 1)

                @block.vector
                def _(dve):
                    dve.sem_inc(added, 2)
                    with dve.Fori(0, STEPS) as i:
                        def low_half(x):
                            dve.wait_ge(high, i * 2 + x + 1)
                            dve.tensor_tensor(low_of(KT + x), tmp[:, 2 + x, :], high_of(KT + x).bitcast(F32),
                                              ALU.subtract).then_inc(low, 1)

                        def add(n):
                            dve.wait_ge(y_done, i * YS + n + 1)
                            xm = rows(x_t[:, n % KT, :])
                            dve.tensor_tensor(xm, bank_sets(n), xm, ALU.add).then_inc(added, 1)

                        for x in range(2):
                            dve.wait_ge(gated, i * 2 + x + 1)
                            for c in range(3):
                                s = tmp[:, x, CH * c:CH * c + CH]
                                dve.wait_ge(wide, i * 6 + 3 * x + c + 1)
                                dve.tensor_tensor(s, s, ps[:, 6 + c % 2, 0:CH], ALU.mult).then_inc(weighed, 1)
                            dve.wait_ge(used, i * 6 + 2 * x + 2 + 3)
                            dve.wait_ge(weighed, i * 6 + 3 * x + 3)
                            dve.tensor_tensor(rows(tmp[:, 2 + x, :]), rows(tmp[:, x, :]), setB, ALU.mult)\
                               .then_inc(hidden, 1)
                            if x:
                                add(0)
                            low_half(x)
                        for n in range(1, YS):
                            add(n)

        def finish():
            stored = sem("out_stored")
            with nc.Block("finish") as block:
                @block.sync
                def _(sp):
                    sp.dma_start(out, x_t).then_inc(stored, 16)
                    sp.wait_ge(stored, 16)

        raw_extra = sb("bias_rows", [P, 256], F32)
        v_all = xres[:, 0:TT * H * VW].rearrange("p (j f) -> p j f", j=TT)
        kvt = xres[:, 5200:5200 + 8 * 256].rearrange("p (m f) -> p m f", m=8)
        setup()
        end_phase()
        graph()
        end_phase()
        layernorm("ln0", source=a["x_t"])
        end_phase()
        linear_kv()
        end_phase()
        linear_out()
        end_phase()
        product("sparse", wg_s, 0, load=a["x_t"])
        end_phase()
        product("out0", a["l0_o"], 1, prep=FromAttention("out0_prep"))
        end_phase()
        layernorm("ln1", quantise=True)
        end_phase()
        int8_product()
        end_phase()
        layernorm("ln2")
        end_phase()
        node_major()
        end_phase()
        with_scratch(feature_attention)
        end_phase()
        with_two_more_tiles("gcn", lambda: product("gcn", h_s, None, k_tiles=TT, per=5 * P, parts=2, load=x2_s, prep=FromCounts("gcn_prep")))
        end_phase()
        product("out1", a["l1_o"], 4, prep=FromAttention("out1_prep"))
        end_phase()
        layernorm("ln3")
        end_phase()
        gating()
        end_phase()
        with_two_more_tiles("moe", experts)
        end_phase()
        finish()
        end_phase()


def layout(v):
    f = np.float32
    x_t = np.zeros((P, KT, NT), f)
    x_t[:, :, :N] = v["x"].T.reshape(KT, P, N).transpose(1, 0, 2)

    def stat(w):
        k, m = w.shape
        return np.ascontiguousarray(w.reshape(k // P, P, m // P, P).transpose(2, 1, 0, 3)).reshape(m // P, P, k)

    def mov(w):
        k, m = w.shape
        return np.ascontiguousarray(w.reshape(2, 4, P, m // 256, 256).transpose(3, 0, 2, 1, 4)).reshape(-1, P, ITEM)

    def bc(b):
        return b.reshape(-1, P).T

    consts = np.zeros((P, C_ALL), f)
    consts[:, C_ID:C_ID + P] = np.eye(P)
    consts[:, C_ONE:C_ONE + P] = 1
    consts[:64, C_MASK:C_MASK + 64] = 1
    consts[64:, C_MASK + 64:C_MASK + P] = 1
    consts[:, C_IOTA8:C_IOTA8 + 8] = 8 - np.arange(8)
    bias_cols = np.zeros((P, 8, KT), f)
    for n, name in enumerate(["L0_gnn_bias", "L0_mix_bo", "L1_mix_bk", "L1_mix_bq", "L1_mix_bo"]):
        bias_cols[:, n, :] = bc(v[name])
    o = {
        "consts": consts, "bias_cols": bias_cols, "x_t": x_t,
        "iota": np.tile(np.arange(NR, dtype=f), (P, 1)), "iota_col": np.arange(P, dtype=f).reshape(P, 1),
        "src": np.ascontiguousarray(v["src"].reshape(ET, EP).T), "dst": np.ascontiguousarray(v["dst"].reshape(ET, EP).T),
        "edge_w": np.ascontiguousarray(v["edge_weight"].reshape(ET, EP).T),
    }
    def pairs(*ws):
        return np.ascontiguousarray(np.stack([w.reshape(4, -1, P, ITEM) for w in ws], 1)).reshape(-1, P, ITEM)

    o["l0_kv"] = pairs(mov(v["L0_mix_Wk"]), mov(v["L0_mix_Wv"]))
    o["l0_q"] = stat(v["L0_mix_Wq"])
    o["l0_o"] = stat(v["L0_mix_Wo"])
    o["ffn_rhs"] = stat(v["L0_ffn_rhs"])
    o["l1_vh"] = np.concatenate([mov(v["L1_mix_Wv"]), mov(np.ascontiguousarray(v["L1_gnn_W"].T))])
    vh = np.concatenate([v["L1_mix_bv"], v["L1_gnn_b"]]).reshape(8, 1, 256)
    o["l1_vh_bias"] = np.ascontiguousarray(np.broadcast_to(vh, (8, P, 256)))
    kq = np.stack([stat(v["L1_mix_Wk"]), stat(v["L1_mix_Wq"])], 1)
    o["l1_kq"] = np.ascontiguousarray(kq).reshape(2 * KT, P, ITEM)
    o["l1_o"] = stat(v["L1_mix_Wo"])
    ws = v["L1_ffn_Ws"].reshape(KT, P, NEXP).transpose(1, 0, 2)
    o["Ws"] = np.ascontiguousarray(ws).reshape(P, KT * NEXP)
    o["bs"] = np.tile(v["L1_ffn_bs"], (P, TT))
    hid = NEXP * FF
    gu = np.zeros((2, D, FT * P), f)
    gu[0, :, :hid] = v["L1_ffn_Wg"].transpose(1, 0, 2).reshape(D, hid)
    gu[1, :, :hid] = v["L1_ffn_Wu"].transpose(1, 0, 2).reshape(D, hid)
    down = np.zeros((FT * P, D), f)
    down[:hid] = v["L1_ffn_Wd"].reshape(hid, D)
    moe = np.zeros((FT // 2, 6, P, ITEM), f)
    moe[:, 0:4:2] = stat(gu[0]).reshape(FT // 2, 2, P, ITEM)
    moe[:, 1:4:2] = stat(gu[1]).reshape(FT // 2, 2, P, ITEM)
    moe[:, 4:6] = down.reshape(FT // 2, 2, P, ITEM)
    o["moe"] = moe.reshape(-1, P, ITEM)
    owner = (np.arange(FT * P) // FF).reshape(FT // 2, 1, 2 * P)
    sel = np.zeros((FT // 2, 40, 2 * P), f)
    sel[:, 0:NEXP] = sel[:, 32:32 + NEXP] = owner == np.arange(NEXP).reshape(1, NEXP, 1)
    o["sel"] = sel
    o["rm"] = np.tile(v["L1_mix_random_matrix"], (2, 1))
    return o


def kernel(**inputs):
    from concourse import bacc
    from concourse.bass_utils import run_bass_kernel_spmd

    arrays = layout({k: np.asarray(v) for k, v in inputs.items()})
    nc = bacc.Bacc("TRN2", target_bir_lowering=False, num_devices=1)
    a = {k: nc.dram_tensor(k, v.shape, mybir.dt.from_np(v.dtype), kind="ExternalInput").ap() for k, v in arrays.items()}
    out = nc.dram_tensor("out", (P, KT, NT), F32, kind="ExternalOutput").ap()
    gps_kernel(nc, a, out)
    got = run_bass_kernel_spmd(nc, [arrays], core_ids=[0]).results[0]["out"]
    return np.ascontiguousarray(got.transpose(1, 0, 2).reshape(D, NT)[:, :N].T)
```

```python
from contextlib import ExitStack

import numpy as np
import concourse.bass as bass
from concourse import mybir

F32, F32R, I32 = mybir.dt.float32, mybir.dt.float32r, mybir.dt.int32
ALU, ACT, AX = mybir.AluOpType, mybir.ActivationFunctionType, mybir.AxisListType
ds = bass.ds

P = 128
N = 1250
D = 1024
KT = D // P
CH = 418
NT = 3 * CH
TT = 10
NR = TT * P
E = 20000
EP = 125
ET = E // EP
H, HD = 16, 64
M = 256
NEXP, FF = 8, 344
FT = 22
ITEM = 1024
TOKS = [P] * 9 + [N - 9 * P]
VW = HD + 1
MAGIC = 1.5 * 2.0 ** 23

C_ID = 0
C_ONE = C_ID + P
C_MASK = C_ONE + P
C_IOTA8 = C_MASK + P
C_CNT = C_IOTA8 + 8
C_ALL = C_CNT


def cuts(j):
    lo, hi, out = P * j, min(P * (j + 1), NT), []
    while lo < hi:
        b = lo // CH
        end = min(hi, CH * (b + 1))
        out.append((b, lo - CH * b, lo - P * j, end - P * j))
        lo = end
    return out


def mm3(pe, out, lh, ll, rh, rl, first, last):
    pe.matmul(out, lh, rh, start=first, stop=False)
    pe.matmul(out, lh, rl, start=False, stop=False)
    return pe.matmul(out, ll, rh, start=False, stop=last)


def gps_kernel(nc, a, out):
    ctx = ExitStack()

    def sb(name, shape, dt):
        return ctx.enter_context(nc.sbuf_tensor(name, shape, dt))

    phase_sems = []

    def sem(name):
        phase_sems.append(nc.alloc_semaphore(name))
        return phase_sems[-1]

    def end_phase():
        nc.clear_and_free_semaphores(list(phase_sems))
        nc.all_engine_barrier()
        phase_sems.clear()

    def dram(name, shape):
        return nc.dram_tensor(name, shape, F32, kind="Internal").ap()

    with ctx:
        rh = sb("rh", [P, KT, NR], F32R)
        rl = sb("rl", [P, KT, NR], F32R)
        xres = sb("xres", [P, 10400], F32)
        raw = sb("raw", [P, 2, ITEM], F32)
        wh = sb("wh", [P, 4, ITEM], F32R)
        wl = sb("wl", [P, 4, ITEM], F32R)
        tmp = sb("tmp", [P, 4, NT], F32)
        cst = sb("cst", [P, C_ALL], F32)
        col = sb("col", [P, 6, TT], F32)
        bcol = sb("bcol", [P, 8, KT], F32)
        dcolq = sb("dcolq", [P, TT], F32)
        dcol = sb("dcol", [P, TT], F32)
        ps = ctx.enter_context(nc.psum_tensor("ps", [P, 8, 512], F32))
        x_t = xres[:, 0:KT * NT].rearrange("p (k t) -> p k t", k=KT)
        ident, ones, mask2 = cst[:, C_ID:C_ID + P], cst[:, C_ONE:C_ONE + P], cst[:, C_MASK:C_MASK + P]
        setA, setB = ps[:, 0:3, 0:CH], ps[:, 3:6, 0:CH]

        def rows(t):
            return t.rearrange("p (c t) -> p c t", c=3)

        cnt_s = dram("cnt_s", [TT, P, NT])
        wg_s = dram("wg_s", [KT, P, ITEM])
        att_s = dram("att_s", [KT, P, NT])
        x2_s = dram("x2_s", [P, KT, NT])
        h_s = dram("h_s", [KT * 2, P, 5 * P])

        consts_in = ctx.enter_context(nc.semaphore("consts_in"))

        spare = {}

        def high_of(k):
            return rh[:, k, 0:NT] if k < KT else spare["high"][:, k - KT, :]

        def low_of(k):
            return rl[:, k, 0:NT] if k < KT else spare["low"][:, k - KT, :]

        def with_two_more_tiles(name, phase):
            with nc.sbuf_tensor(name + "_more_high", [P, 2, NT], F32R) as spare["high"], \
                    nc.sbuf_tensor(name + "_more_low", [P, 2, NT], F32R) as spare["low"]:
                phase()

        def with_scratch(name, phase, size=5120):
            with nc.sbuf_tensor(name + "_scratch", [P, size], F32) as spare["plain"]:
                phase()

        def with_gate(phase):
            with nc.sbuf_tensor("gate", [P, (KT + TT) * NEXP], F32) as spare["gate"], \
                    nc.sbuf_tensor("gate_halves", [P, (2 * KT + TT) * NEXP], F32R) as spare["gate_halves"]:
                with_two_more_tiles("moe", phase)

        def with_kept_rows(phases):
            with nc.sbuf_tensor("kept_rows", [P, 4, NT], F32) as spare["kept"]:
                phases()

        def setup():
            blk_cm = nc.Block("setup")
            with blk_cm as block:
                @block.sync
                def _(sp):
                    sp.dma_start(cst[:, :], a["consts"]).then_inc(consts_in, 16)
                    sp.dma_start(bcol[:, :, :], a["bias_cols"]).then_inc(consts_in, 16)
                    sp.wait_ge(consts_in, 32)

                @block.vector
                def _(dve):
                    dve.memset(col[:, :, :], 1.0)
                    dve.memset(dcolq[:, :], 1.0)
                    dve.memset(dcol[:, :], 1.0)
                    dve.memset(rh[:, :, NT:NR].bitcast(F32), 0.0)
                    dve.memset(rl[:, :, NT:NR].bitcast(F32), 0.0)

        def graph():
            onehot_src = rh[0:EP, 0:2, 0:NT]
            zeros = rl[:, 4, 0:512]
            onehot_dst = [rl[0:EP, s, 0:P] for s in range(2)]
            w_hi_dst = [rl[0:EP, s, P:2 * P] for s in range(2)]
            w_lo_dst = [rl[0:EP, s, 2 * P:3 * P] for s in range(2)]
            ident_r = rl[:, 2, 0:P]
            w_hi = rl[0:EP, 3, 0:ET]
            w_lo = rl[0:EP, 3, ET:2 * ET]
            pieces = spare["plain"][:, 2 * NT:]

            def piece(size, at=[0]):
                at[0] += size
                return pieces[:, at[0] - size:at[0]]

            def thin(row, size):
                return tmp[0:1, row:row + 2, :].rearrange("p a b -> p (a b)")[:, 0:size]

            hit = piece(TT * ET)[0:EP, :]
            dloc_all = hit
            srcf, dstf, dtile, wraw = (piece(ET)[0:EP, :] for _ in range(4))
            src_l = pieces[0:EP, TT * ET:(TT + 2) * ET]
            iota = piece(NR)
            idx = raw[0:EP, 0, 0:2 * ET].bitcast(I32)
            rng_i, rng = piece(2 * TT)[0:1, :].bitcast(I32), piece(4 * TT)[0:1, :]
            steps = dtile[0:1, :]
            tile_i = idx[:, ET:2 * ET]
            range_f, first_rev = thin(0, TT * ET), thin(2, TT * ET)
            got, prep, hits_up, ranges = sem("g_loads"), sem("g_prep"), sem("g_hits_counted"), sem("g_ranges")
            slot_free, onehots = sem("g_slot_free"), sem("g_onehots")
            tile_done, tile_out = sem("g_tile_done"), sem("g_tile_out")
            counts_out = [sem(f"g_counts_stored{s}") for s in range(2)]
            weights_out = [sem(f"g_weights_stored{s}") for s in range(2)]
            chain = sem("g_dve_chain")
            cnt_copied, deg_sqrt = sem("g_counts_copied"), sem("g_deg_sqrt")
            deg_seen = sem("g_degree_products")

            col_sums = ps[:, 0, :]
            total = spare["plain"][:, 0:NT]
            x_sum, x_in, x_added = spare["plain"][:, NT:2 * NT], sem("g_x_in"), sem("g_x_added")
            added = sem("g_counts_added")

            def counts_area(j):
                return setA if j % 2 == 0 else ps[:, 5:8, 0:CH]

            def spans(eng, table):
                vals = []
                for j in range(TT):
                    first = eng.value_load(table[0:1, 2 * j:2 * j + 1], min_val=0, max_val=ET // 2 - 1)
                    count = eng.value_load(table[0:1, 2 * j + 1:2 * j + 2], min_val=1, max_val=ET // 2)
                    vals.append((first, count))
                return vals

            with nc.Block("graph") as block:
                @block.sync
                def _(sp):
                    sp.dma_start(iota, a["iota"]).then_inc(got, 16)
                    sp.dma_start(idx[:, 0:ET], a["src"]).then_inc(got, 16)
                    sp.dma_start(idx[:, ET:2 * ET], a["dst"]).then_inc(got, 16)
                    sp.dma_start(wraw, a["edge_w"]).then_inc(got, 16)
                    sp.dma_start(x_t, a["x_t"]).then_inc(x_in, 16)
                    sp.wait_ge(x_in, 16)

                @block.vector
                def _(dve):
                    link_n = [0]

                    def link(ins):
                        link_n[0] += 1
                        ins.then_inc(chain, 1)
                        dve.wait_ge(chain, link_n[0])

                    dve.wait_ge(got, 64)
                    dve.memset(total, 0.0).then_inc(added, 1)
                    dve.memset(zeros.bitcast(F32), 0.0).then_inc(prep, 1)
                    dve.tensor_copy(ident_r, ident).then_inc(prep, 1)
                    dve.tensor_copy(srcf, idx[:, 0:ET])
                    link(dve.tensor_copy(w_hi, wraw))
                    dve.tensor_tensor(w_lo, wraw, w_hi.bitcast(F32), ALU.subtract)
                    link(dve.tensor_copy(dstf, idx[:, ET:2 * ET]))
                    link(dve.tensor_scalar(tile_i, idx[:, ET:2 * ET], 7, None, ALU.logical_shift_right))
                    link(dve.tensor_copy(dtile, tile_i))
                    for j in range(TT):
                        last = dve.tensor_scalar(hit[:, ET * j:ET * j + ET], dtile, float(j), None, ALU.is_equal)
                    last.then_inc(prep, 1)
                    dve.wait_ge(prep, 3)
                    dve.wait_ge(hits_up, 1)
                    dve.tensor_scalar(steps, iota[0:1, 0:ET], 1.0, None, ALU.add)
                    for j in range(TT):
                        dve.tensor_scalar(dloc_all[:, ET * j:ET * j + ET], dstf, float(-P * j), None, ALU.add)
                    link(dve.tensor_scalar(range_f.rearrange("p (b n) -> p b n", b=4), ps[0:1, 0:4, 0:400],
                                           1.0, None, ALU.min))
                    r3 = range_f.rearrange("p (j t) -> p j t", j=TT)
                    f3 = first_rev.rearrange("p (j t) -> p j t", j=TT)
                    for j in range(TT):
                        last = dve.scalar_tensor_tensor(f3[:, j, :], steps, -1.0, r3[:, j, :], ALU.mult, ALU.mult)
                    link(last)
                    link(dve.scalar_tensor_tensor(first_rev, range_f, float(ET + 1), first_rev, ALU.mult, ALU.add))
                    for j in range(TT):
                        last = dve.tensor_tensor(r3[:, j, :], r3[:, j, :], steps, ALU.mult)
                    link(last)
                    link(dve.tensor_reduce(rng[:, 0:TT], f3, AX.X, ALU.max))
                    link(dve.tensor_reduce(rng[:, TT:2 * TT], r3, AX.X, ALU.max))
                    link(dve.tensor_scalar(rng[:, 0:TT], rng[:, 0:TT], -1.0, float(ET), ALU.mult, ALU.add))
                    link(dve.tensor_scalar(rng[:, 0:TT], rng[:, 0:TT], float(ET - 2), None, ALU.min))
                    link(dve.tensor_scalar(rng[:, TT:2 * TT], rng[:, TT:2 * TT], 1.0, None, ALU.add))
                    pairs = rng_i.rearrange("p (j c) -> p c j", c=2)
                    for c in range(2):
                        link(dve.tensor_copy(pairs[:, c, :], rng[:, c * TT:c * TT + TT]))
                    link(dve.tensor_scalar(rng_i, rng_i, 1, None, ALU.logical_shift_right))
                    link(dve.tensor_copy(rng.rearrange("p (a j c) -> p a c j", a=2, c=2)[:, 0], pairs))
                    f = rng[:, 0:2 * TT].rearrange("p (j c) -> p c j", c=2)
                    g = rng[:, 2 * TT:3 * TT]
                    link(dve.tensor_scalar(g, f[:, 0, :], 1.0, None, ALU.add))
                    link(dve.tensor_tensor(g, g, f[:, 1, :], ALU.max))
                    link(dve.tensor_tensor(g, g, f[:, 0, :], ALU.subtract))
                    dve.tensor_copy(pairs[:, 1, :], g).then_inc(ranges, 1)
                    dve.wait_ge(ranges, 1)
                    spans_d = spans(dve, rng_i)
                    base = 0
                    for j in range(TT):
                        first, count = spans_d[j]
                        dloc = pieces[0:EP, ET * j:ET * j + 2 * ET]
                        w_hi_l, w_lo_l = rl[0:EP, 3, 0:2 * ET], rl[0:EP, 3, ET:3 * ET]
                        with dve.Fori(0, count) as i:
                            for s in range(2):
                                n = base + i * 2 + s
                                t = ds((first + i) * 2 + s, 1)
                                dve.wait_ge(slot_free, n + 1)
                                dve.tensor_scalar(onehot_src[:, s, :], iota[0:EP, 0:NT], src_l[:, t], None,
                                                  ALU.is_equal)
                                dve.tensor_scalar(onehot_dst[s], iota[0:EP, 0:P], dloc[:, t], None, ALU.is_equal)\
                                   .then_inc(onehots, 1) if j >= KT else \
                                    dve.tensor_scalar(onehot_dst[s], iota[0:EP, 0:P], dloc[:, t], None,
                                                      ALU.is_equal)
                                if j < KT:
                                    dve.tensor_scalar(w_hi_dst[s], iota[0:EP, 0:P], dloc[:, t],
                                                      w_hi_l[:, t].bitcast(F32), ALU.is_equal, ALU.mult)
                                    dve.tensor_scalar(w_lo_dst[s], iota[0:EP, 0:P], dloc[:, t],
                                                      w_lo_l[:, t].bitcast(F32), ALU.is_equal,
                                                      ALU.mult).then_inc(onehots, 1)
                        base = dve.snap(base + count * 2)
                    deg, y, v = col[:, 0, :], col[:, 1, :], col[:, 2, :]
                    dve.wait_ge(deg_sqrt, 1)
                    dve.tensor_copy(deg[:, 0:TT - 1], col_sums[:, 0:TT - 1])
                    link(dve.tensor_copy(deg[0:NT - 9 * P, TT - 1:TT], col_sums[0:NT - 9 * P, TT - 1:TT]))
                    link(dve.reciprocal(y, col[:, 3, :]))
                    newton(dve, link, y, deg, v)
                    link(dve.tensor_copy(dcol[:, :], y))

                @block.tensor
                def _(pe):
                    pe.sem_inc(slot_free, 2)
                    pe.wait_ge(prep, 3)
                    for b in range(4):
                        last = pe.matmul(ps[0:1, b, 0:400], ones[0:EP, 0:1], hit[:, 400 * b:400 * b + 400],
                                         start=True, stop=True)
                    last.then_inc(hits_up, 1)
                    pe.wait_ge(ranges, 1)
                    spans_p = spans(pe, rng_i)
                    base = 0
                    for j in range(TT):
                        first, count = spans_p[j]
                        if j >= 2:
                            pe.wait_ge(cnt_copied, j - 1)
                        for n in range(3):
                            pe.matmul(counts_area(j)[:, n, :], zeros[:, 0:P], zeros[:, 0:CH], start=True, stop=False)
                        for b, c, lo, hi in cuts(j):
                            pe.matmul(counts_area(j)[:, b, c:c + hi - lo], ident_r, ident_r[:, lo:hi], start=False, stop=False)
                        if 1 <= j < KT:
                            pe.wait_ge(tile_out, j)
                        if j < KT:
                            for n in range(2):
                                pe.matmul(ps[:, 3 + n, :], zeros[:, 0:P], zeros, start=True, stop=False)
                        with pe.Fori(0, count) as i:
                            for s in range(2):
                                pe.wait_ge(onehots, base + i * 2 + s + 1)
                                for n in range(3):
                                    last = pe.matmul(counts_area(j)[:, n, :], onehot_dst[s],
                                                     onehot_src[:, s, CH * n:CH * n + CH], start=False, stop=False)
                                if j < KT:
                                    for part in (w_hi_dst[s], w_lo_dst[s]):
                                        for n in range(2):
                                            last = pe.matmul(ps[:, 3 + n, :], part,
                                                             onehot_src[:, s, 512 * n:512 * n + 512],
                                                             start=False, stop=False)
                                last.then_inc(slot_free, 1)
                        base = pe.snap(base + count * 2)
                        for n in range(3):
                            last = pe.matmul(counts_area(j)[:, n, :], zeros[:, 0:P], zeros[:, 0:CH], start=False, stop=True)
                        if j < KT:
                            for n in range(2):
                                last = pe.matmul(ps[:, 3 + n, :], zeros[:, 0:P], zeros, start=False, stop=True)
                        last.then_inc(tile_done, 1)
                    pe.wait_ge(added, TT + 1)
                    node_sums(pe, 0, total).then_inc(deg_seen, 1)

                @block.gpsimd
                def _(pool):
                    pool.wait_ge(x_in, 16)
                    pool.tensor_tensor(x_sum, x_t[:, 0, :], x_t[:, 1, :], ALU.add).then_inc(x_added, 1)
                    for k in range(2, KT):
                        pool.wait_ge(x_added, k - 1)
                        pool.tensor_tensor(x_sum, x_sum, x_t[:, k, :], ALU.add).then_inc(x_added, 1)
                    for j in range(TT):
                        pool.wait_ge(cnt_copied, j + 1)
                        pool.wait_ge(added, j + 1)
                        pool.tensor_tensor(total, total, tmp[:, j % 2, :], ALU.add).then_inc(added, 1)

                @block.scalar
                def _(act):
                    for j in range(TT):
                        act.wait_ge(tile_done, j + 1)
                        if j >= 2:
                            act.wait_ge(counts_out[j % 2], 16 * (j // 2))
                            act.wait_ge(added, j)
                        if 2 <= j < KT:
                            act.wait_ge(weights_out[j % 2], 16 * (j // 2))
                        if j < KT:
                            act.copy(tmp[:, 2 + j % 2, 0:D].rearrange("p (c t) -> p c t", c=2),
                                     ps[:, 3:5, :]).then_inc(tile_out, 1)
                        act.copy(rows(tmp[:, j % 2, :]), counts_area(j)).then_inc(cnt_copied, 1)
                        act.wait_ge(cnt_copied, j + 1)
                        act.dma_start(cnt_s[j], tmp[:, j % 2, :]).then_inc(counts_out[j % 2], 16)
                        if j < KT:
                            act.wait_ge(tile_out, j + 1)
                            act.dma_start(wg_s[:, :, P * j:P * j + P].rearrange("m p f -> p m f"),
                                          tmp[:, 2 + j % 2, 0:D].rearrange("p (m f) -> p m f", m=KT))\
                               .then_inc(weights_out[j % 2], 16)
                    act.wait_ge(deg_seen, 1)
                    act.activation(col[:, 3, 0:TT - 1], col_sums[:, 0:TT - 1], ACT.Sqrt)
                    act.activation(col[0:NT - 9 * P, 3, TT - 1:TT], col_sums[0:NT - 9 * P, TT - 1:TT],
                                   ACT.Sqrt).then_inc(deg_sqrt, 1)
                    for s in range(2):
                        act.wait_ge(counts_out[s], 16 * TT // 2)
                        act.wait_ge(weights_out[s], 16 * KT // 2)

        def newton(dve, link, y, v, t):
            link(dve.tensor_tensor(t, y, y, ALU.mult))
            link(dve.tensor_tensor(t, t, v, ALU.mult))
            link(dve.tensor_scalar(t, t, -0.5, 1.5, ALU.mult, ALU.add))
            link(dve.tensor_tensor(y, y, t, ALU.mult))

        LEAD = 2
        SLOTS = 4

        class Chain:

            def __init__(self, eng, name, per=0):
                self.eng, self.sem, self.n, self.off, self.per = eng, sem(name), 0, 0, per

            def __call__(self, ins):
                self.n += 1
                ins.then_inc(self.sem, 1)
                self.eng.wait_ge(self.sem, self.off + self.n)

        def stream_load(sp, items, count, width, raw_in, split, unroll):
            with sp.Fori(0, count // unroll) as i:
                for q in range(unroll):
                    n = i * unroll + q
                    sp.wait_ge(split, n + 1)
                    sp.dma_start(raw[:, q % 2, 0:width], items[ds(n, 1)].rearrange("a p f -> (a p) f"))\
                      .then_inc(raw_in[q % 2], 16)

        def stream_split(pool, name, count, width, raw_in, split, used, used_of, unroll, slots=4, before=()):
            halves, claimed = sem(name + "_high_half"), sem(name + "_slot_claimed")

            def one(i, q):
                n = i * unroll + q
                pool.wait_ge(raw_in[q % 2], (i * (unroll // 2) + q // 2 + 1) * 16)
                pool.wait_ge(used, used_of(i, q))
                pool.sem_inc(claimed, 1)
                pool.tensor_copy(wh[:, q % slots, 0:width], raw[:, q % 2, 0:width]).then_inc(halves, 1)
                pool.wait_ge(halves, n + 1)
                pool.tensor_tensor(wl[:, q % slots, 0:width], raw[:, q % 2, 0:width],
                                   wh[:, q % slots, 0:width].bitcast(F32), ALU.subtract).then_inc(split, 1)

            pool.sem_inc(split, LEAD)
            start = 0
            if before:
                start = 1
                for q in range(unroll):
                    if q == slots - 1:
                        for stage in before:
                            stage.run("gpsimd", pool)
                    one(0, q)
            with pool.Fori(start, count // unroll) as i:
                for q in range(unroll):
                    one(i, q)

        def bank_sets(q):
            return setA if q % 2 == 0 else setB

        def broadcast_cols(pe, area, diag):
            last = None
            for j in range(TT):
                for b, c, lo, hi in cuts(j):
                    last = pe.matmul(area[:, b, c:c + hi - lo], ones, diag[:, P * j + lo:P * j + hi],
                                     start=True, stop=True)
            return last

        def node_sums(pe, bank, src, first=True, only=True):
            last = None
            for j in range(TT):
                w = min(P, NT - P * j)
                last = pe.matmul(ps[0:w, bank, j:j + 1], src[:, P * j:P * j + w], ones[:, 0:1],
                                 start=(first and j == 0), stop=only, skip_group_check=True)
            return last

        def node_cols(eng_op, dst, bank):
            eng_op(dst[:, 0:TT - 1], ps[:, bank, 0:TT - 1])
            w = NT - 9 * P
            return eng_op(dst[0:w, TT - 1:TT], ps[0:w, bank, TT - 1:TT])

        def diagonals(dve, dst, v):
            last = None
            for j in range(TT):
                w = min(P, NT - P * j)
                last = dve.tensor_scalar(dst[:, P * j:P * j + w], ident[:, 0:w], v[:, j:j + 1], None, ALU.mult)
            return last

        class Stage:

            def __init__(self, done, **programs):
                self.done, self.programs = done, programs

            def run(self, name, eng):
                if self.programs.get(name) is not None:
                    self.programs[name](eng)

        sum_row = tmp[:, 2, :]

        def layernorm(name, sums_at=None, quantise=False):
            mean, var, rstd, std, t = (col[:, n, :] for n in range(5))
            scale = dcolq[:, :]
            top = spare["plain"][:, 3 * P:3 * P + NT] if quantise else None
            sums = sem(name + "_sums")
            diag, wide = sem(name + "_diagonals"), sem(name + "_broadcast")
            centred, squared, sq_used = sem(name + "_centred"), sem(name + "_squared"), sem(name + "_squares_summed")
            rooted, var_in, paired = sem(name + "_std"), sem(name + "_var"), sem(name + "_paired")
            normed, high, low = sem(name + "_normed"), sem(name + "_high"), sem(name + "_low")
            turned, top_done = sem(name + "_turned"), sem(name + "_top_done")
            def vector(dve):
                link = Chain(dve, name + "_chain")
                dve.wait_ge(sums, 1)
                link(node_cols(lambda o, i: dve.tensor_scalar(o, i, 1.0 / D, None, ALU.mult), mean, 6))
                diagonals(dve, tmp[:, 3, :], mean).then_inc(diag, 1)
                if quantise:
                    link(dve.memset(top, 0.0))
                dve.wait_ge(wide, 1)
                def pair(g):
                    dve.wait_ge(squared, 2 * g + 2)
                    dve.tensor_tensor(tmp[:, 2, :], tmp[:, 2, :], tmp[:, 3, :], ALU.add).then_inc(paired, 1)

                for k in range(KT):
                    if k >= 2:
                        dve.wait_ge(squared, k - 1)
                    dve.tensor_tensor(rows(tmp[:, k % 2, :]), rows(x_t[:, k, :]), setA, ALU.subtract)\
                       .then_inc(centred, 1)
                    if k % 2 == 0 and k:
                        pair(k // 2 - 1)
                    if quantise:
                        dve.wait_ge(centred, k + 1)
                        link(dve.tensor_tensor(top, tmp[:, k % 2, :], top, ALU.max))
                        link(dve.scalar_tensor_tensor(top, tmp[:, k % 2, :], -1.0, top, ALU.mult, ALU.max))
                pair(KT // 2 - 1)
                if quantise:
                    dve.sem_inc(top_done, 1)
                dve.wait_ge(sq_used, KT // 2)
                node_cols(lambda o, i: dve.tensor_scalar(o, i, 1.0 / D, 1e-5, ALU.mult, ALU.add), var, 7)\
                    .then_inc(var_in, 1)
                dve.wait_ge(rooted, 1)
                link(dve.reciprocal(rstd, std))
                newton(dve, link, rstd, var, t)
                if quantise:
                    dve.wait_ge(turned, 1)
                    for b in range(3):
                        n = min(4, 9 - 4 * b)
                        dve.tensor_reduce(scale[:, 4 * b:4 * b + n],
                                          ps[:, 3 + b, 0:P * n].rearrange("p (j c) -> p j c", c=P), AX.X, ALU.max)
                    w = NT - 9 * P
                    link(dve.tensor_reduce(scale[0:w, 9:10], ps[0:w, 5, P:2 * P], AX.X, ALU.max))
                    link(dve.tensor_tensor(scale, scale, rstd, ALU.mult))
                    link(dve.tensor_scalar(scale, scale, 1e-12, 1.0 / 127.0, ALU.max, ALU.mult))
                    link(dve.reciprocal(t, scale))
                    link(dve.tensor_tensor(rstd, rstd, t, ALU.mult))
                diagonals(dve, tmp[:, 3, :], rstd).then_inc(diag, 1)
                dve.wait_ge(wide, 2)
                for k in range(KT):
                    s = k % 3
                    if k >= 3 and not quantise:
                        dve.wait_ge(low, k - 2)
                    link(dve.tensor_tensor(rows(tmp[:, s, :]), rows(x_t[:, k, :]), setA, ALU.subtract))
                    ins = dve.tensor_tensor(rows(tmp[:, s, :]), rows(tmp[:, s, :]), setB, ALU.mult)
                    if quantise:
                        link(ins)
                        dve.tensor_scalar(rh[:, k, 0:NT], tmp[:, s, :], MAGIC, -MAGIC, ALU.add, ALU.add)
                    else:
                        ins.then_inc(normed, 1)

            def scalar(act):
                for k in range(KT):
                    act.wait_ge(centred, k + 1)
                    if k < 2:
                        act.wait_ge(wide, 1)
                    elif k % 2 == 0:
                        act.wait_ge(sq_used, k // 2)
                    act.activation(tmp[:, 2 + k % 2, :], tmp[:, k % 2, :], ACT.Square).then_inc(squared, 1)
                act.wait_ge(var_in, 1)
                act.activation(std, var, ACT.Sqrt).then_inc(rooted, 1)
                if not quantise:
                    for k in range(KT):
                        act.wait_ge(normed, k + 1)
                        act.copy(rh[:, k, 0:NT], tmp[:, k % 3, :]).then_inc(high, 1)

            if not quantise:
                def gpsimd(pool):
                    for k in range(KT):
                        pool.wait_ge(high, k + 1)
                        pool.tensor_tensor(rl[:, k, 0:NT], tmp[:, k % 3, :], rh[:, k, 0:NT].bitcast(F32),
                                           ALU.subtract).then_inc(low, 1)

            def tensor(pe):
                node_sums(pe, 6, sum_row if sums_at is None else sums_at).then_inc(sums, 1)
                pe.wait_ge(diag, 1)
                broadcast_cols(pe, ps[:, 0:3, :], tmp[:, 3, :]).then_inc(wide, 1)
                for g in range(KT // 2):
                    pe.wait_ge(paired, g + 1)
                    node_sums(pe, 7, tmp[:, 2, :], first=(g == 0), only=(g == KT // 2 - 1)).then_inc(sq_used, 1)
                if quantise:
                    pe.wait_ge(centred, KT)
                    pe.wait_ge(top_done, 1)
                    for j in range(TT):
                        w = min(P, NT - P * j)
                        last = pe.transpose(ps[0:w, 3 + j // 4, P * (j % 4):P * (j % 4) + P],
                                            top[:, P * j:P * j + w], ident)
                    last.then_inc(turned, 1)
                pe.wait_ge(diag, 2)
                broadcast_cols(pe, ps[:, 3:6, :], tmp[:, 3, :]).then_inc(wide, 1)
            return Stage(vector=vector, scalar=scalar, tensor=tensor, gpsimd=None if quantise else gpsimd,
                         done=None if quantise else low)

        def linear_kv(*before):
            name = "lkv"
            kc = xres[:, 0:TT * 256].rearrange("p (j f) -> p j f", j=TT)
            vc = xres[:, 2560:2560 + TT * 260].rearrange("p (j h f) -> p j h f", j=TT, h=2)
            ex = xres[:, 7400:7912].rearrange("p (s f) -> p s f", s=2)
            raw_in = [sem(f"{name}_raw{s}") for s in range(2)]
            split, tiles = sem(name + "_split"), sem(name + "_tiles")
            freed, exped, k_in, v_in = sem(name + "_banks_free"), sem(name + "_exp"), sem(name + "_k"), sem(name + "_v")
            kv_done, kv_out, relued = sem(name + "_kv"), sem(name + "_kv_out"), sem(name + "_relu")
            v_ones = sem(name + "_ones")
            with nc.Block(name) as block:
                @block.sync
                def _(sp):
                    for stage in before:
                        stage.run("sync", sp)
                    stream_load(sp, a["l0_kv"], 16, ITEM, raw_in, split, 4)

                @block.gpsimd
                def _(pool):
                    stream_split(pool, name, 16, ITEM, raw_in, split, tiles, lambda i, q: i * 20 + (q // 2) * 10 + 10, 4,
                                 before=before)

                @block.tensor
                def _(pe):
                    pe.sem_inc(kv_done, 1)
                    pe.sem_inc(tiles, 2 * TT)
                    for stage in before:
                        stage.run("tensor", pe)
                        if stage.done is not None:
                            pe.wait_ge(stage.done, KT if stage.programs.get("gpsimd") else 1)
                    pe.wait_ge(v_ones, 1)
                    with pe.Fori(0, 4) as i:
                        for half in range(2):
                            pe.wait_ge(split, i * 4 + 2 * half + 2 + LEAD)
                            for j in range(TT):
                                t = TT * half + j
                                pe.wait_ge(freed, i * 20 + t + 1)
                                for k in range(KT):
                                    s, c = 2 * half + k // 4, 256 * (k % 4)
                                    nodes = slice(P * j, P * j + P)
                                    last = mm3(pe, ps[:, t % 4, 0:256], rh[:, k, nodes], rl[:, k, nodes],
                                               wh[:, s, c:c + 256], wl[:, s, c:c + 256], k == 0, k == KT - 1)
                                last.then_inc(tiles, 1)
                        pe.wait_ge(k_in, i * 10 + 10 + 1)
                        pe.wait_ge(v_in, i * 10 + 10)
                        pe.wait_ge(kv_out, i * 4 + 1)
                        for p in range(2):
                            for j in range(TT):
                                w = TOKS[j]
                                last = pe.matmul(ps[:, 4 + p, 0:P + 1], kc[0:w, j, P * p:P * p + P],
                                                 vc[0:w, j, p, 0:P + 1], start=(j == 0), stop=(j == TT - 1))
                            last.then_inc(kv_done, 1)

                @block.scalar
                def _(act):
                    for stage in before:
                        stage.run("scalar", act)
                    with act.Fori(0, 4) as i:
                        for j in range(TT):
                            act.wait_ge(consts_in, 32)
                            act.wait_ge(k_in, i * 10 + j + 1)
                            act.wait_ge(tiles, i * 20 + j + 1 + 2 * TT)
                            act.activation(ex[:, j % 2, :], ps[:, j % 4, 0:256], ACT.Relu, scale=-1.0).then_inc(relued, 1)
                            act.wait_ge(consts_in, 32)
                            act.wait_ge(relued, i * 10 + j + 1)
                            act.activation(ex[:, j % 2, :], ex[:, j % 2, :], ACT.Exp, scale=-1.0).then_inc(exped, 1)
                        for j in range(TT):
                            act.wait_ge(kv_done, i * 2 + 1)
                            act.wait_ge(tiles, i * 20 + TT + j + 1 + 2 * TT)
                            act.copy(vc[:, j, :, 0:P], ps[:, (TT + j) % 4, 0:256].rearrange("p (h f) -> p h f", h=2))\
                               .then_inc(v_in, 1)

                @block.vector
                def _(dve):
                    for stage in before:
                        stage.run("vector", dve)
                    dve.sem_inc(k_in, 1)
                    dve.memset(vc[:, :, :, P:P + 2], 1.0).then_inc(v_ones, 1)
                    dve.sem_inc(freed, 4)
                    dve.sem_inc(kv_out, 1)
                    with dve.Fori(0, 4) as i:
                        for j in range(TT):
                            dve.wait_ge(kv_done, i * 2 + 1)
                            dve.wait_ge(exped, i * 10 + j + 1)
                            dve.scalar_tensor_tensor(kc[:, j, :], ps[:, j % 4, 0:256], 0.0, ex[:, j % 2, :],
                                                     ALU.max, ALU.add).then_inc(k_in, 1)
                            dve.wait_ge(k_in, i * 10 + j + 1 + 1)
                            dve.sem_inc(freed, 1)
                        for j in range(TT):
                            dve.wait_ge(v_in, i * 10 + j + 1)
                            dve.sem_inc(freed, 1)
                        for p in range(2):
                            dve.wait_ge(kv_done, i * 2 + p + 1 + 1)
                            dve.tensor_tensor(kvt[:, ds(2 * i + p, 1), 0:P].rearrange("p a f -> p (a f)"),
                                              ps[:, 4 + p, 0:P], mask2, ALU.mult).then_inc(kv_out, 1)
                            dve.tensor_scalar(kvt[:, ds(2 * i + p, 1), P:2 * P].rearrange("p a f -> p (a f)"),
                                              mask2, ps[:, 4 + p, P:P + 1], None, ALU.mult).then_inc(kv_out, 1)

        def linear_out():
            name = "lout"
            ex = xres[:, 7400:7400 + NT]
            zt = xres[:, 8700:8700 + 2 * CH].rearrange("p (s f) -> p s f", s=2)
            stage = xres[:, 9600:9600 + 512].rearrange("p (s f) -> p s f", s=2)
            raw_in = [sem(f"{name}_raw{s}") for s in range(2)]
            store2 = [sem(f"{name}_rows_stored{s}") for s in range(2)]
            split, used, freed = sem(name + "_split"), sem(name + "_items_used"), sem(name + "_sets_free")
            staged, relued, exped, q_in = (sem(name + x) for x in ("_staged", "_relu", "_exp", "_q"))
            num, z_in, recip, att, stored = (sem(name + x) for x in ("_num", "_z", "_recip", "_att", "_stored"))
            with nc.Block(name) as block:
                @block.sync
                def _(sp):
                    stream_load(sp, a["l0_q"], 8, ITEM, raw_in, split, 2)

                @block.gpsimd
                def _(pool):
                    stream_split(pool, name, 8, ITEM, raw_in, split, used, lambda i, q: i * 2 + q + 1, 2, slots=2)

                @block.tensor
                def _(pe):
                    pe.sem_inc(used, 2)

                    def attend(n, q, c):
                        cols = slice(CH * c, CH * c + CH)
                        if c == 0:
                            pe.wait_ge(q_in, n + 1 + 1)
                            pe.wait_ge(staged, n + 1)
                        pe.wait_ge(att, n * 3 + c + 1)
                        pe.matmul(ps[:, 7, 0:CH], stage[:, q % 2, P:2 * P], tmp[:, q % 2, cols], start=True, stop=True)
                        pe.matmul(ps[:, 6, 0:CH], stage[:, q % 2, 0:P], tmp[:, q % 2, cols], start=True, stop=True)\
                          .then_inc(num, 1)

                    AFTER = (8, 13, 18)

                    def gemm(n, q, attends):
                        pe.wait_ge(split, n + 1 + LEAD)
                        pe.wait_ge(freed, n + 1)
                        for c in range(3):
                            for k in range(KT):
                                f, t = slice(P * k, P * k + P), slice(CH * c, CH * c + CH)
                                last = mm3(pe, bank_sets(q)[:, c, :], wh[:, q, f], wl[:, q, f], rh[:, k, t], rl[:, k, t],
                                           k == 0, k == KT - 1)
                                if c == 2 and k == KT - 1:
                                    last.then_inc(used, 1)
                                if attends and c * KT + k + 1 in AFTER:
                                    attend(n - 1, 1 - q, AFTER.index(c * KT + k + 1))

                    gemm(0, 0, False)
                    with pe.Fori(0, KT // 2 - 1) as i:
                        gemm(i * 2 + 1, 1, True)
                        gemm(i * 2 + 2, 0, True)
                    gemm(KT - 1, 1, True)
                    for c in range(3):
                        attend(KT - 1, 1, c)

                @block.scalar
                def _(act):
                    for s in range(2):
                        act.sem_inc(store2[s], 16)
                    with act.Fori(0, 2) as i:
                        for q in range(4):
                            n = i * 4 + q
                            act.wait_ge(att, (i * 12 + (3 * (q - 1) if q else 0)) + 1)
                            act.copy(stage[:, q % 2, :], kvt[:, ds(n, 1), :].rearrange("p a f -> p (a f)")).then_inc(staged, 1)
                            act.wait_ge(consts_in, 32)
                            act.wait_ge(q_in, n + 1)
                            act.wait_ge(used, n + 1 + 2)
                            act.activation(rows(ex), bank_sets(q), ACT.Relu, scale=-1.0).then_inc(relued, 1)
                            act.wait_ge(consts_in, 32)
                            act.wait_ge(relued, n + 1)
                            act.activation(ex, ex, ACT.Exp, scale=-1.0).then_inc(exped, 1)
                            for c in range(3):
                                act.wait_ge(consts_in, 32)
                                act.wait_ge(num, n * 3 + c + 1)
                                act.wait_ge(att, (n * 3 + c - 1) if q or c else i * 12 + 1)
                                act.activation(zt[:, (q * 3 + c) % 2, :], ps[:, 7, 0:CH], ACT.Copy, bias=1e-6)\
                                   .then_inc(z_in, 1)
                            act.wait_ge(att, n * 3 + 3 + 1)
                            act.dma_start(att_s[ds(n, 1)].rearrange("a p f -> (a p) f"), tmp[:, 2 + q % 2, :])\
                               .then_inc(store2[q % 2], 16)
                    for s in range(2):
                        act.wait_ge(store2[s], 64 + 16)

                @block.vector
                def _(dve):
                    dve.sem_inc(q_in, 1)
                    dve.sem_inc(att, 1)
                    dve.sem_inc(freed, LEAD)
                    with dve.Fori(0, 2) as i:
                        for q in range(4):
                            n = i * 4 + q
                            dve.wait_ge(exped, n + 1)
                            dve.scalar_tensor_tensor(rows(tmp[:, q % 2, :]), bank_sets(q), 0.0, rows(ex),
                                                     ALU.max, ALU.add).then_inc(q_in, 1)
                            dve.wait_ge(q_in, n + 1 + 1)
                            dve.sem_inc(freed, 1)
                            dve.wait_ge(store2[q % 2], i * 32 + (q // 2) * 16 + 16)
                            for c in range(3):
                                zs = zt[:, (q * 3 + c) % 2, :]
                                dve.wait_ge(z_in, n * 3 + c + 1)
                                dve.reciprocal(zs, zs).then_inc(recip, 1)
                                dve.wait_ge(recip, n * 3 + c + 1)
                                dve.tensor_tensor(tmp[:, 2 + q % 2, CH * c:CH * c + CH], ps[:, 6, 0:CH], zs, ALU.mult)\
                                   .then_inc(att, 1)

        def att_row(k, early):
            return spare["kept"][:, k - 4, :] if early == KT and k >= 4 else tmp[:, k % 4, :]

        def product(name, items, bias, k_tiles=KT, per=ITEM, parts=1, load=None, prep=None,
                    fetch=0, sums=False):
            raw_in = [sem(f"{name}_raw{s}") for s in range(2)]
            split, used, freed = sem(name + "_split"), sem(name + "_items_used"), sem(name + "_sets_free")
            ready, x_in, fetched = sem(name + "_resident"), sem(name + "_x_in"), sem(name + "_rows_fetched")
            summed = sem(name + "_summed")
            kp, count = k_tiles // parts, KT * parts
            if prep is not None:
                prep.begin(ready)
            with nc.Block(name) as block:
                @block.sync
                def _(sp):
                    stream_load(sp, items, count, per, raw_in, split, 4)

                @block.gpsimd
                def _(pool):
                    stream_split(pool, name, count, per, raw_in, split, used, lambda i, q: i * 4 + q + 1, 4)

                if prep is not None or load is not None:
                    @block.scalar
                    def _(act):
                        if prep is not None:
                            prep.scalar(act)
                        if load is not None:
                            act.wait_ge(split, 2 + LEAD)
                            act.dma_start(x_t, load).then_inc(x_in, 16)
                        if fetch:
                            if prep is not None:
                                act.wait_ge(ready, k_tiles)
                            for k in range(fetch):
                                act.dma_start(att_row(k, fetch), att_s[k]).then_inc(fetched, 16)
                            act.wait_ge(fetched, 16 * fetch)

                @block.tensor
                def _(pe):
                    if prep is not None:
                        prep.tensor(pe)
                    pe.sem_inc(used, SLOTS)
                    with pe.Fori(0, count // 4) as i:
                        for q in range(4):
                            n = i * 4 + q
                            pe.wait_ge(split, n + 1 + LEAD)
                            m, part = q // parts, q % parts
                            if part == 0:
                                pe.wait_ge(freed, i * (4 // parts) + m + 1)
                            for k in range(kp):
                                kk = part * kp + k
                                if prep is not None:
                                    pe.wait_ge(ready, kk + 1)
                                for c in range(3):
                                    f, t = slice(P * k, P * k + P), slice(CH * c, CH * c + CH)
                                    last = mm3(pe, bank_sets(m)[:, c, :], wh[:, q, f], wl[:, q, f],
                                               high_of(kk)[:, t], low_of(kk)[:, t], kk == 0, kk == k_tiles - 1)
                            last.then_inc(used, 1)

                @block.vector
                def _(dve):
                    dve.sem_inc(freed, 1)
                    if prep is not None:
                        prep.vector(dve)
                    dve.sem_inc(freed, 1)
                    if load is not None:
                        dve.wait_ge(x_in, 16)
                    if sums:
                        dve.wait_ge(ready, k_tiles)
                        dve.memset(sum_row, 0.0).then_inc(summed, 1)
                    with dve.Fori(0, count // 4) as i:
                        for m in range(4 // parts):
                            n = i * (4 // parts) + m
                            xm = x_t[:, ds(n, 1), :].rearrange("p a (c t) -> p (a c) t", c=3)
                            dve.wait_ge(used, i * 4 + (m + 1) * parts + SLOTS)
                            if bias is None:
                                ins = dve.tensor_tensor(xm, bank_sets(m), xm, ALU.add)
                            else:
                                ins = dve.scalar_tensor_tensor(xm, bank_sets(m), bcol[:, bias, ds(n, 1)], xm,
                                                               ALU.add, ALU.add)
                            ins.then_inc(freed, 1)
                            if sums:
                                dve.wait_ge(freed, n + 1 + LEAD)
                                dve.wait_ge(summed, n + 1)
                                dve.tensor_tensor(rows(sum_row), rows(sum_row), xm, ALU.add).then_inc(summed, 1)

        class FromAttention:

            def __init__(self, name, early):
                self.name, self.early = name, early

            def begin(self, ready):
                self.got = [sem(f"{self.name}_rows{s}") for s in range(4)]
                self.high, self.low = sem(self.name + "_high"), ready

            def scalar(self, act):
                for k in range(KT):
                    if k >= self.early:
                        act.wait_ge(self.got[k % 4], 16)
                    act.copy(rh[:, k, 0:NT], att_row(k, self.early)).then_inc(self.high, 1)
                    if 1 <= k and k + 3 >= self.early and k + 3 < KT:
                        act.wait_ge(self.low, k)
                        act.dma_start(att_row(k + 3, self.early), att_s[k + 3]).then_inc(self.got[(k + 3) % 4], 16)

            def vector(self, dve):
                for k in range(KT):
                    dve.wait_ge(self.high, k + 1)
                    dve.tensor_tensor(rl[:, k, 0:NT], att_row(k, self.early), rh[:, k, 0:NT].bitcast(F32),
                                      ALU.subtract).then_inc(self.low, 1)

            def tensor(self, pe):
                pass

        class FromCounts:

            def __init__(self, name):
                self.name = name

            def begin(self, ready):
                self.got = [sem(f"{self.name}_rows{s}") for s in range(3)]
                self.high, self.diag, self.wide, self.scaled = (sem(self.name + x) for x in
                                                                ("_high", "_diag", "_wide", "_scaled"))
                self.low = ready

            def scalar(self, act):
                for k in range(3):
                    act.dma_start(tmp[:, k, :], cnt_s[k]).then_inc(self.got[k], 16)
                for k in range(TT):
                    act.wait_ge(self.scaled, k + 1)
                    act.copy(high_of(k), tmp[:, k % 3, :]).then_inc(self.high, 1)
                    if 1 <= k <= TT - 3:
                        act.wait_ge(self.low, k)
                        act.dma_start(tmp[:, (k + 2) % 3, :], cnt_s[k + 2]).then_inc(self.got[(k + 2) % 3], 16)

            def tensor(self, pe):
                pe.wait_ge(self.diag, 1)
                broadcast_cols(pe, ps[:, 3:6, :], tmp[:, 3, :]).then_inc(self.wide, 1)

            def vector(self, dve):
                diagonals(dve, tmp[:, 3, :], dcol[:, :]).then_inc(self.diag, 1)
                dve.wait_ge(self.wide, 1)
                for k in range(TT + 1):
                    if k < TT:
                        dve.wait_ge(self.got[k % 3], 16 * (k // 3 + 1))
                        dve.scalar_tensor_tensor(rows(tmp[:, k % 3, :]), rows(tmp[:, k % 3, :]), dcol[:, k:k + 1],
                                                 setB, ALU.mult, ALU.mult).then_inc(self.scaled, 1)
                    if k >= 1:
                        j = k - 1
                        dve.wait_ge(self.high, j + 1)
                        dve.tensor_tensor(low_of(j), tmp[:, j % 3, :], high_of(j).bitcast(F32),
                                          ALU.subtract).then_inc(self.low, 1)

        def int8_product(*before):
            name = "ffn8"
            raw_in = [sem(f"{name}_raw{s}") for s in range(2)]
            diag, wide, slb = sem(name + "_scale_diag"), sem(name + "_scale_wide"), sem(name + "_scale_rows")
            topped, turned, colmax = sem(name + "_top"), sem(name + "_turned"), sem(name + "_colmax")
            inv_wide, quant, done, freed = (sem(name + x) for x in ("_inv_wide", "_quantised", "_products", "_free"))
            inv_diag, scaled, freed2 = sem(name + "_inv_diag"), sem(name + "_scaled"), sem(name + "_rows_added")
            by_node, cleared, sum_added = sem(name + "_scaled_by_node"), sem(name + "_sums_cleared"), sem(name + "_sum_added")
            scale_row, srow = tmp[:, 3, :], bcol[:, 7, :]
            part, dg, least = (spare["plain"][:, P * n:P * n + P] for n in range(3))
            with nc.Block(name) as block:
                @block.sync
                def _(sp):
                    for stage in before:
                        stage.run("sync", sp)
                    for m in range(KT):
                        if m >= 2:
                            sp.wait_ge(quant, m - 1)
                        sp.dma_start(raw[:, m % 2, :], a["ffn_rhs"][m]).then_inc(raw_in[m % 2], 16)

                @block.vector
                def _(dve):
                    for stage in before:
                        stage.run("vector", dve)
                    link = Chain(dve, name + "_chain")
                    diagonals(dve, scale_row, dcolq[:, :]).then_inc(diag, 1)
                    dve.memset(sum_row, 0.0).then_inc(cleared, 1)
                    for m in range(KT + 2):
                        if m < KT:
                            w3 = raw[:, m % 2, :].rearrange("p (k f) -> p f k", k=KT)
                            wk = raw[:, m % 2, :].rearrange("p (k f) -> p k f", k=KT)
                            dve.wait_ge(raw_in[m % 2], 16 * (m // 2 + 1))
                            dve.tensor_reduce(part, w3, AX.X, ALU.max)
                            link(dve.tensor_reduce(least, w3, AX.X, ALU.min))
                            link(dve.scalar_tensor_tensor(part, least, -1.0, part, ALU.mult, ALU.max))
                            dve.sem_inc(topped, 1)
                            dve.wait_ge(turned, m + 1)
                            sc = srow[:, m:m + 1]
                            link(dve.tensor_reduce(sc, ps[:, 6, 0:P], AX.X, ALU.max))
                            link(dve.tensor_scalar(sc, sc, 1e-12, 1.0 / 127.0, ALU.max, ALU.mult))
                            link(dve.reciprocal(col[:, 0, 0:1], sc))
                            link(dve.tensor_scalar(dg, ident, col[:, 0, 0:1], None, ALU.mult))
                            dve.sem_inc(inv_diag, 1)
                            dve.wait_ge(inv_wide, m + 1)
                            full, inv = bass.broadcast_tensor_aps(wk, ps[:, 7, 0:P].rearrange("p (o f) -> p o f", o=1))
                            link(dve.tensor_tensor(wk, full, inv, ALU.mult))
                            dve.tensor_scalar(wh[:, m % 4, :], raw[:, m % 2, :], MAGIC, -MAGIC, ALU.add, ALU.add)\
                               .then_inc(quant, 1)
                        if m >= 2:
                            j = m - 2
                            dve.wait_ge(by_node, j + 1)
                            dve.tensor_tensor(x_t[:, j, :], x_t[:, j, :], tmp[:, j % 2, :], ALU.add).then_inc(freed2, 1)

                @block.gpsimd
                def _(pool):
                    pool.wait_ge(slb, 1)
                    pool.wait_ge(cleared, 1)
                    for m in range(KT):
                        pool.wait_ge(scaled, m + 1)
                        pool.tensor_tensor(tmp[:, m % 2, :], tmp[:, m % 2, :], scale_row, ALU.mult).then_inc(by_node, 1)
                        if m:
                            pool.wait_ge(freed2, m)
                            if m > 1:
                                pool.wait_ge(sum_added, m - 1)
                            pool.tensor_tensor(sum_row, sum_row, x_t[:, m - 1, :], ALU.add).then_inc(sum_added, 1)
                    pool.wait_ge(freed2, KT)
                    pool.wait_ge(sum_added, KT - 1)
                    pool.tensor_tensor(sum_row, sum_row, x_t[:, KT - 1, :], ALU.add)

                @block.scalar
                def _(act):
                    for stage in before:
                        stage.run("scalar", act)
                    act.wait_ge(wide, 1)
                    act.copy(rows(scale_row), setB).then_inc(slb, 1)
                    for m in range(KT):
                        act.wait_ge(done, m + 1)
                        if m >= 2:
                            act.wait_ge(freed2, m - 1)
                        act.activation(rows(tmp[:, m % 2, :]), bank_sets(m), ACT.Copy, scale=srow[:, m:m + 1])\
                           .then_inc(scaled, 1)

                @block.tensor
                def _(pe):
                    for stage in before:
                        stage.run("tensor", pe)
                        if stage.done is not None:
                            pe.wait_ge(stage.done, KT if stage.programs.get("gpsimd") else 1)
                    pe.wait_ge(diag, 1)
                    broadcast_cols(pe, ps[:, 3:6, :], scale_row).then_inc(wide, 1)
                    for m in range(KT + 1):
                        if m < KT:
                            pe.wait_ge(topped, m + 1)
                            pe.transpose(ps[:, 6, 0:P], part, ident).then_inc(turned, 1)
                            pe.wait_ge(inv_diag, m + 1)
                            pe.matmul(ps[:, 7, 0:P], ones, dg, start=True, stop=True).then_inc(inv_wide, 1)
                        if m >= 1:
                            j = m - 1
                            pe.wait_ge(quant, j + 1)
                            if j == 1:
                                pe.wait_ge(slb, 1)
                            if j >= 2:
                                pe.wait_ge(scaled, j - 1)
                            for c in range(3):
                                for k in range(KT):
                                    last = pe.matmul(bank_sets(j)[:, c, :], wh[:, j % 4, P * k:P * k + P],
                                                     rh[:, k, CH * c:CH * c + CH], start=(k == 0), stop=(k == KT - 1))
                            last.then_inc(done, 1)

        def node_major(*before):
            name = "vh"
            v4 = v_all.rearrange("p j (h f) -> p j h f", h=H)
            biases = spare["plain"][:, 0:2 * D].rearrange("p (g f) -> p g f", f=256)
            raw_in = [sem(f"{name}_raw{s}") for s in range(2)]
            split, tiles, freed = sem(name + "_split"), sem(name + "_tiles"), sem(name + "_banks_free")
            bias_in, h_ready, x_out = sem(name + "_bias"), sem(name + "_h_ready"), sem(name + "_x_out")
            h_out = [sem(f"{name}_h_stored{s}") for s in range(2)]
            hbuf = tmp[:, :, :].rearrange("p a b -> p (a b)")[:, 0:2560].rearrange("p (j f) -> p j f", j=TT)
            hbufs = (hbuf, spare["plain"][:, 2 * D:2 * D + 2560].rearrange("p (j f) -> p j f", j=TT))
            with nc.Block(name) as block:
                @block.sync
                def _(sp):
                    for stage in before:
                        stage.run("sync", sp)
                    stream_load(sp, a["l1_vh"], 16, ITEM, raw_in, split, 4)

                @block.gpsimd
                def _(pool):
                    stream_split(pool, name, 16, ITEM, raw_in, split, tiles, lambda i, q: i * 20 + (q // 2) * 10 + 10, 4,
                                 before=before)

                @block.tensor
                def _(pe):
                    pe.sem_inc(tiles, 2 * TT)
                    for stage in before:
                        stage.run("tensor", pe)
                        if stage.done is not None:
                            pe.wait_ge(stage.done, KT if stage.programs.get("gpsimd") else 1)
                    with pe.Fori(0, 4) as i:
                        for half in range(2):
                            pe.wait_ge(split, i * 4 + 2 * half + 2 + LEAD)
                            for j in range(TT):
                                t = TT * half + j
                                pe.wait_ge(freed, i * 20 + t + 1)
                                for k in range(KT):
                                    s, c = 2 * half + k // 4, 256 * (k % 4)
                                    nodes = slice(P * j, P * j + P)
                                    last = mm3(pe, ps[:, t % 4, 0:256], rh[:, k, nodes], rl[:, k, nodes],
                                               wh[:, s, c:c + 256], wl[:, s, c:c + 256], k == 0, k == KT - 1)
                                last.then_inc(tiles, 1)

                @block.vector
                def _(dve):
                    for stage in before:
                        stage.run("vector", dve)
                    dve.sem_inc(freed, 4)
                    dve.wait_ge(bias_in, 16)
                    with dve.Fori(0, 2) as i:
                        for half in range(2):
                            dve.wait_ge(h_out[half], i * 64 + 16)
                            brow = biases[:, ds(i * 2 + half, 1), :].rearrange("p a f -> p (a f)")
                            for j in range(TT):
                                dve.wait_ge(tiles, (i * 2 + half) * TT + j + 1 + 2 * TT)
                                dve.tensor_tensor(hbufs[half][:, j, :], ps[:, (TT * half + j) % 4, 0:256], brow,
                                                  ALU.add).then_inc(freed, 1)
                            dve.wait_ge(freed, (i * 2 + half) * TT + TT + 4)
                            dve.sem_inc(h_ready, 1)
                    dve.wait_ge(x_out, 16)
                    dve.memset(v4[:, :, :, HD:VW], 1.0)
                    with dve.Fori(0, 2) as i:
                        for half in range(2):
                            brow = biases[:, ds(i * 2 + half + 4, 1), :].rearrange("p a (h f) -> p (a h) f", h=4)
                            for j in range(TT):
                                dve.wait_ge(tiles, (i * 2 + half + 4) * TT + j + 1 + 2 * TT)
                                dve.tensor_tensor(v4[:, j, ds((i * 2 + half) * 4, 4), 0:HD],
                                                  ps[:, (TT * half + j) % 4, 0:256].rearrange("p (h f) -> p h f", h=4),
                                                  brow, ALU.add).then_inc(freed, 1)

                @block.scalar
                def _(act):
                    for stage in before:
                        stage.run("scalar", act)
                    for half in range(2):
                        act.sem_inc(h_out[half], 16)
                    act.dma_start(biases, a["l1_vh_bias"].rearrange("g p f -> p g f")).then_inc(bias_in, 16)
                    act.wait_ge(split, 4 + LEAD)
                    act.dma_start(x2_s, x_t).then_inc(x_out, 16)
                    with act.Fori(0, 2) as i:
                        for half in range(2):
                            g = i * 2 + half
                            act.wait_ge(h_ready, g + 1)
                            for u in range(2):
                                for part in range(2):
                                    act.dma_start(h_s[ds(g * 4 + 2 * u + part, 1)].rearrange("a p (k f) -> (a p) k f", k=5),
                                                  hbufs[half][:, 5 * part:5 * part + 5, P * u:P * u + P])\
                                       .then_inc(h_out[half], 16)
                    for half in range(2):
                        act.wait_ge(h_out[half], 128 + 16)

        def feature_attention():
            name = "fa"
            guard = float(np.float32(1e-6)) * M
            space_a, space_b = spare["plain"][:, 0:7 * 512], spare["plain"][:, 7 * 512:]
            kf = space_a[:, 0:3 * 512].rearrange("p (s f) -> p s f", s=3)
            ex = space_a[:, 3 * 512:6 * 512].rearrange("p (s f) -> p s f", s=3)
            table = space_a[:, 6 * 512:7 * 512].rearrange("p (x f) -> p x f", x=4)
            qf = space_b[:, 0:4 * CH].rearrange("p (s f) -> p s f", s=4)
            ez = space_b[:, 4 * CH:5 * CH]
            rm = raw_extra[:, :]
            k_t, q_t = tmp[:, 0, :], tmp[:, 1, :]
            v4 = v_all.rearrange("p j (h f) -> p j h f", h=H)
            raw_in = [sem(f"{name}_raw{s}") for s in range(2)]
            stored = [sem(f"{name}_stored{s}") for s in range(2)]
            rm_in, split, used, k_in, q_in = (sem(name + x) for x in ("_rm_in", "_split", "_items_used", "_k", "_q"))
            kproj, kfeat, kv_used, tables = (sem(name + x) for x in ("_k_projected", "_k_features", "_kv", "_tables"))
            qproj, qfeat, outs, att = (sem(name + x) for x in ("_q_projected", "_q_features", "_outs", "_att"))
            relued, exped, ez_in, recip = (sem(name + x) for x in ("_relu", "_exp", "_norm", "_recip"))
            PIECES = 12
            ACTS = TT + PIECES

            def out_bank(c, h):
                return (3 if c % 2 == 0 else 1) + h

            def k_bank(w, j):
                b = (6, 1, 3)[j % 3]
                return ps[0:w, b:b + 2, 0:M]

            def halves_of(t, w, j):
                return t[0:w, j % 3, :].rearrange("p (h f) -> p h f", h=2)

            def k_ex(w, j):
                return halves_of(ex, w, j)

            def q_bank(x):
                return ((6, 7), (0, 5))[x // 2 % 2][x % 2]

            with nc.Block(name) as block:
                @block.sync
                def _(sp):
                    sp.dma_start(rm, a["rm"]).then_inc(rm_in, 16)
                    stream_load(sp, a["l1_kq"], 16, ITEM, raw_in, split, 4)

                @block.gpsimd
                def _(pool):
                    stream_split(pool, name, 16, ITEM, raw_in, split, used, lambda i, q: i * 4 + q + 1, 4)

                @block.tensor
                def _(pe):
                    pe.sem_inc(outs, 1)
                    pe.sem_inc(kv_used, 1)
                    pe.sem_inc(used, SLOTS)
                    pe.wait_ge(rm_in, 16)

                    def gemm(area, slot):
                        for c in range(3):
                            for k in range(KT):
                                f, t = slice(P * k, P * k + P), slice(CH * c, CH * c + CH)
                                last = mm3(pe, area[:, c, :], wh[:, slot, f], wl[:, slot, f], rh[:, k, t], rl[:, k, t],
                                           k == 0, k == KT - 1)
                        last.then_inc(used, 1)

                    def kv_product(n, p, i, j):
                        w = TOKS[j]
                        pe.wait_ge(kfeat, n * TT + j + 1)
                        for x in range(4):
                            last = pe.matmul(ps[:, 0, VW * x:VW * x + VW], kf[0:w, j % 3, P * x:P * x + P],
                                             v4[0:w, j, ds(i * 4 + 2 * p + x // 2, 1), :].rearrange("p a f -> p (a f)"),
                                             start=(j == 0 and x == 0), stop=(j == TT - 1), skip_group_check=True)
                        last.then_inc(kv_used, 1)

                    def out_product(n, x):
                        c, mh, h = x // 4, x // 2 % 2, x % 2
                        pe.wait_ge(qfeat, n * PIECES + x + 1 + 1)
                        if x == 0:
                            pe.wait_ge(tables, n + 1 + 1)
                        if x == 8:
                            pe.wait_ge(att, n * 3 + 2 + 1)
                        pe.matmul(ps[:, out_bank(c, h), 0:CH], table[:, 2 * h + mh, :], qf[:, x % 4, :],
                                  start=(mh == 0), stop=(mh == 1)).then_inc(outs, 1)

                    with pe.Fori(0, 4) as i:
                        for p in range(2):
                            n = i * 2 + p
                            pe.wait_ge(split, i * 4 + 2 * p + 1 + LEAD)
                            pe.wait_ge(tables, n + 1)
                            pe.wait_ge(att, n * 3 + 1)
                            gemm(setA, 2 * p)
                            pe.wait_ge(split, i * 4 + 2 * p + 2 + LEAD)
                            pe.wait_ge(att, n * 3 + 1 + 1)
                            gemm(setB, 2 * p + 1)
                            pe.wait_ge(k_in, n + 1)
                            for j in range(TT):
                                w = TOKS[j]
                                if j == 2:
                                    pe.wait_ge(q_in, n + 1)
                                if j >= 3:
                                    pe.wait_ge(kfeat, n * TT + j - 2)
                                for h in range(2):
                                    r = slice(HD * h, HD * h + HD)
                                    last = pe.matmul(k_bank(w, j)[:, h, :], k_t[r, P * j:P * j + w],
                                                     rm[r, :], start=True, stop=True)
                                last.then_inc(kproj, 1)
                                if j >= 2:
                                    kv_product(n, p, i, j - 2)
                            kv_product(n, p, i, TT - 2)
                            kv_product(n, p, i, TT - 1)
                            pe.wait_ge(q_in, n + 1)
                            for y in range(PIECES // 2):
                                c, mh = y // 2, y % 2
                                if y == 1:
                                    pe.wait_ge(tables, n + 1 + 1)
                                if y >= 2:
                                    pe.wait_ge(qfeat, n * PIECES + 2 * y - 2 + 1)
                                for h in range(2):
                                    r = slice(HD * h, HD * h + HD)
                                    pe.matmul(ps[:, q_bank(2 * y + h), 0:CH], rm[r, P * mh:P * mh + P],
                                              q_t[r, CH * c:CH * c + CH], start=True, stop=True).then_inc(qproj, 1)
                                if y:
                                    out_product(n, 2 * y - 2)
                                    out_product(n, 2 * y - 1)
                            out_product(n, PIECES - 2)
                            out_product(n, PIECES - 1)

                @block.scalar
                def _(act):
                    for p in range(2):
                        act.sem_inc(stored[p], 16)
                    def relu_exp(dst, src, count):
                        act.activation(dst, src, ACT.Relu, scale=-1.0).then_inc(relued, 1)
                        act.wait_ge(relued, count)
                        act.activation(dst, dst, ACT.Exp, scale=-1.0).then_inc(exped, 1)

                    with act.Fori(0, 4) as i:
                        for p in range(2):
                            n = i * 2 + p
                            for j in range(TT):
                                w = TOKS[j]
                                if j < 3:
                                    act.wait_ge(qfeat, n * PIECES + 1)
                                else:
                                    act.wait_ge(kfeat, n * TT + j - 2)
                                act.wait_ge(kproj, n * TT + j + 1)
                                relu_exp(k_ex(w, j), k_bank(w, j), n * ACTS + j + 1)
                            for x in range(PIECES):
                                if x < 3:
                                    act.wait_ge(kfeat, n * TT + TT)
                                else:
                                    act.wait_ge(qfeat, n * PIECES + x - 2 + 1)
                                act.wait_ge(qproj, n * PIECES + x + 1)
                                relu_exp(ex[:, x % 3, 0:CH], ps[:, q_bank(x), 0:CH], n * ACTS + TT + x + 1)
                            act.wait_ge(att, n * 3 + 4 + 1)
                            act.dma_start(att_s[ds(n, 1)].rearrange("a p f -> (a p) f"), tmp[:, 2 + p, :])\
                               .then_inc(stored[p], 16)
                    for p in range(2):
                        act.wait_ge(stored[p], 64 + 16)

                @block.vector
                def _(dve):
                    dve.sem_inc(qfeat, 1)
                    dve.sem_inc(tables, 1)
                    dve.sem_inc(att, 2)
                    lo, hi = slice(0, HD), slice(HD, P)

                    def divide(n, p, c):
                        m, cols = n * 3 + c, slice(CH * c, CH * c + CH)
                        a_b, b_b = ps[:, out_bank(c, 0), 0:CH], ps[:, out_bank(c, 1), 0:CH]
                        dve.wait_ge(outs, n * PIECES + 4 * c + 4 + 1)
                        dve.wait_ge(att, m + 1 + 1)
                        dve.tensor_scalar(ez[lo, :], a_b[hi, :], guard, None, ALU.max).then_inc(ez_in, 1)
                        dve.tensor_scalar(ez[hi, :], b_b[lo, :], guard, None, ALU.max).then_inc(ez_in, 1)
                        dve.wait_ge(ez_in, m * 2 + 2)
                        dve.reciprocal(ez, ez).then_inc(recip, 1)
                        dve.wait_ge(recip, m + 1)
                        dve.tensor_tensor(tmp[lo, 2 + p, cols], a_b[lo, :], ez[lo, :], ALU.mult)
                        dve.tensor_tensor(tmp[hi, 2 + p, cols], b_b[hi, :], ez[hi, :], ALU.mult).then_inc(att, 1)

                    with dve.Fori(0, 4) as i:
                        for p in range(2):
                            n = i * 2 + p
                            for half, (area, dst, done, b) in enumerate(((setA, k_t, k_in, 2), (setB, q_t, q_in, 3))):
                                dve.wait_ge(used, i * 4 + 2 * p + half + 1 + SLOTS)
                                dve.tensor_scalar(rows(dst), area, bcol[:, b, ds(n, 1)], None, ALU.add)\
                                   .then_inc(done, 1)
                            for j in range(TT):
                                w = TOKS[j]
                                dve.wait_ge(kv_used, n * TT + max(j - 2, 0) + 1)
                                dve.wait_ge(exped, n * ACTS + j + 1)
                                dve.scalar_tensor_tensor(halves_of(kf, w, j), k_bank(w, j), 0.0, k_ex(w, j), ALU.max,
                                                         ALU.add).then_inc(kfeat, 1)
                            dve.wait_ge(kv_used, n * TT + TT + 1)
                            kv = ps[:, 0, 0:4 * VW].rearrange("p (x f) -> p x f", x=4)
                            dve.tensor_copy(table[:, 0:2, lo], kv[:, 0:2, 0:HD])
                            dve.tensor_copy(table[:, 2:4, hi], kv[:, 2:4, 0:HD])
                            for x in range(4):
                                ins = dve.tensor_scalar(table[:, x, hi if x < 2 else lo], ones[:, 0:HD],
                                                        kv[:, x, HD:VW], None, ALU.mult)
                            ins.then_inc(tables, 1)
                            dve.wait_ge(stored[p], i * 16 + 16)
                            for x in range(PIECES):
                                dve.wait_ge(outs, n * PIECES + max(x - 3, 0) + 1)
                                dve.wait_ge(exped, n * ACTS + TT + x + 1)
                                dve.scalar_tensor_tensor(qf[:, x % 4, :], ps[:, q_bank(x), 0:CH], 0.0,
                                                         ex[:, x % 3, 0:CH], ALU.max, ALU.add).then_inc(qfeat, 1)
                                if x % 4 == 1 and x > 4:
                                    divide(n, p, x // 4 - 1)
                            divide(n, p, 2)

        def gating():
            name = "gate"
            ws = spare["gate"][:, 0:KT * NEXP]
            bs = spare["gate"][:, KT * NEXP:(KT + TT) * NEXP].rearrange("p (j e) -> p j e", j=TT)
            ws_h, ws_l = (spare["gate_halves"][:, KT * NEXP * n:KT * NEXP * (n + 1)] for n in range(2))
            work = tmp[:, 0, :]

            def grid(n):
                return work[:, TT * NEXP * n:TT * NEXP * (n + 1)].rearrange("p (j e) -> p j e", j=TT)

            logits, is_top, first, second, rank = (grid(n) for n in range(5))
            t0 = TT * NEXP * 5
            top1, top2, pick, e2, total = (work[:, t0 + TT * n:t0 + TT * n + TT].rearrange("p (j o) -> p j o", o=1)
                                           for n in range(5))
            high = spare["gate_halves"][:, 2 * KT * NEXP:(2 * KT + TT) * NEXP].rearrange("p (j e) -> p j e", j=TT)
            both = tmp[:, 3, 0:40 * TT].rearrange("p (j e) -> p j e", j=TT)
            loaded, halves, products, gap, ratio = (sem(name + x) for x in
                                                    ("_loaded", "_halves", "_logits", "_gap", "_ratio"))
            ready, turned, placed = sem(name + "_ready"), sem(name + "_turned"), sem(name + "_placed")
            def sync(sp):
                sp.dma_start(ws, a["Ws"]).then_inc(loaded, 16)
                sp.dma_start(bs, a["bs"].rearrange("p (j e) -> p j e", j=TT)).then_inc(loaded, 16)

            def tensor(pe):
                pe.wait_ge(halves, 1)
                for j in range(TT):
                    nodes = slice(P * j, P * j + P)
                    for k in range(KT):
                        e = slice(NEXP * k, NEXP * k + NEXP)
                        out = ps[:, 0, NEXP * j:NEXP * j + NEXP]
                        for n, (l, r) in enumerate(((rh, ws_h), (rh, ws_l), (rl, ws_h))):
                            last = pe.matmul(out, l[:, k, nodes], r[:, e], start=(j == 0 and k == 0 and n == 0),
                                             stop=(k == KT - 1 and n == 2), skip_group_check=True)
                last.then_inc(products, 1)
                pe.wait_ge(ready, 1)
                for j in range(TT):
                    last = pe.transpose(ps[0:40, 3 + j // 4, P * (j % 4):P * (j % 4) + P], both[:, j, :], ident)
                last.then_inc(turned, 1)

            def vector(dve):
                link = Chain(dve, name + "_chain")

                def wide(fn, out, full, narrow, *ops):
                    f, n = bass.broadcast_tensor_aps(full, narrow)
                    return fn(out, f, n, *ops)

                iota8 = cst[:, C_IOTA8:C_IOTA8 + NEXP].rearrange("p (o e) -> p o e", o=1)
                dve.wait_ge(loaded, 32)
                dve.memset(both, 0.0)
                link(dve.tensor_copy(ws_h, ws))
                dve.tensor_tensor(ws_l, ws, ws_h.bitcast(F32), ALU.subtract).then_inc(halves, 1)
                dve.wait_ge(products, 1)
                link(dve.tensor_tensor(logits, ps[:, 0, 0:TT * NEXP].rearrange("p (j e) -> p j e", j=TT), bs, ALU.add))

                def choose(one_hot, top, best):
                    link(dve.tensor_reduce(top, logits, AX.X, ALU.max))
                    link(wide(dve.tensor_tensor, is_top, logits, top, ALU.is_equal))
                    link(wide(dve.tensor_tensor, rank, is_top, iota8, ALU.mult))
                    link(dve.tensor_reduce(best, rank, AX.X, ALU.max))
                    link(wide(dve.tensor_tensor, one_hot, rank, best, ALU.is_equal))

                choose(first, top1, pick)
                big = float(np.finfo(np.float32).max)
                link(dve.tensor_scalar(is_top, first, -2.0, 1.0, ALU.mult, ALU.add))
                link(dve.scalar_tensor_tensor(logits, is_top, big, logits, ALU.mult, ALU.min))
                choose(second, top2, pick)
                dve.tensor_tensor(e2, top2, top1, ALU.subtract).then_inc(gap, 1)
                dve.wait_ge(ratio, 1)
                link(dve.tensor_scalar(total, e2, 1.0, None, ALU.add))
                link(dve.reciprocal(total, total))
                link(dve.tensor_tensor(e2, e2, total, ALU.mult))
                link(wide(dve.tensor_tensor, first, first, total, ALU.mult))
                link(wide(dve.tensor_tensor, second, second, e2, ALU.mult))
                link(dve.tensor_tensor(first, first, second, ALU.add))
                link(dve.tensor_copy(high, first))
                dve.tensor_copy(both[:, :, 0:NEXP], high.bitcast(F32))
                dve.tensor_tensor(both[:, :, 32:32 + NEXP], first, high.bitcast(F32), ALU.subtract).then_inc(ready, 1)
                dve.wait_ge(turned, 1)
                dve.tensor_copy(wh[0:40, 3, 0:512], ps[0:40, 3, :])
                dve.tensor_copy(wh[0:40, 3, 512:2 * CH], ps[0:40, 4, 0:2 * CH - 512])
                dve.tensor_copy(wl[0:40, 3, 0:D - 2 * CH], ps[0:40, 4, 2 * CH - 512:512])
                dve.tensor_copy(wl[0:40, 3, D - 2 * CH:CH], ps[0:40, 5, 0:NT - D]).then_inc(placed, 1)

            def scalar(act):
                act.wait_ge(gap, 1)
                act.activation(e2, e2, ACT.Exp).then_inc(ratio, 1)
            return Stage(vector=vector, scalar=scalar, tensor=tensor, sync=sync, done=placed)

        def experts(*before):
            name = "moe"
            raw_in = [sem(f"{name}_raw{s}") for s in range(2)]
            split, used, sel_in, sel_set = (sem(name + x) for x in ("_split", "_items_used", "_sel_in", "_selector"))
            wide, gated, weighed, hidden = (sem(name + x) for x in ("_wide", "_gated", "_weighed", "_hidden"))
            high, low, y_done, added = (sem(name + x) for x in ("_high", "_low", "_y_products", "_y_added"))
            sel = wl[0:40, 3, 512:512 + 2 * P]
            sel_raw = raw_extra[0:40, :]
            STEPS, YS = FT // 2, 2 * KT

            def weights_of(c):
                return wh[0:40, 3, CH * c:CH * c + CH] if c < 2 else wl[0:40, 3, 0:CH]

            with nc.Block(name) as block:
                @block.sync
                def _(sp):
                    for stage in before:
                        stage.run("sync", sp)
                    stream_load(sp, a["moe"], 6 * STEPS, ITEM, raw_in, split, 6)

                @block.gpsimd
                def _(pool):
                    stream_split(pool, name, 6 * STEPS, ITEM, raw_in, split, used, lambda i, q: i * 6 + q + 1, 6, slots=3,
                                 before=before)

                @block.tensor
                def _(pe):
                    pe.sem_inc(used, 3)
                    for stage in before:
                        stage.run("tensor", pe)
                        if stage.done is not None:
                            pe.wait_ge(stage.done, KT if stage.programs.get("gpsimd") else 1)

                    def gemm(area, slot, c):
                        for k in range(KT):
                            f, t = slice(P * k, P * k + P), slice(CH * c, CH * c + CH)
                            last = mm3(pe, area[:, c, :], wh[:, slot, f], wl[:, slot, f], rh[:, k, t], rl[:, k, t],
                                       k == 0, k == KT - 1)
                        return last

                    def spread(x, c):
                        pe.matmul(ps[:, 6 + c % 2, 0:CH], sel[:, P * x:P * x + P], weights_of(c), start=True, stop=True)\
                          .then_inc(wide, 1)

                    with pe.Fori(0, STEPS) as i:
                        for x in range(2):
                            pe.wait_ge(split, i * 6 + 2 * x + 1 + LEAD)
                            if x == 0:
                                pe.wait_ge(added, i * YS + 1)
                            else:
                                pe.wait_ge(gated, i * 2 + 1)
                            gemm(setA, 2 * x % 3, 0)
                            gemm(setA, 2 * x % 3, 1)
                            gemm(setA, 2 * x % 3, 2).then_inc(used, 1)
                            pe.wait_ge(sel_set, i + 1 + 1)
                            pe.wait_ge(weighed, i * 6 + 3 * x + 1)
                            spread(x, 0)
                            spread(x, 1)
                            pe.wait_ge(split, i * 6 + 2 * x + 2 + LEAD)
                            if x == 0:
                                pe.wait_ge(added, i * YS + 2)
                            else:
                                pe.wait_ge(hidden, i * 2 + 1 + 1)
                            gemm(setB, (2 * x + 1) % 3, 0)
                            gemm(setB, (2 * x + 1) % 3, 1)
                            pe.wait_ge(weighed, i * 6 + 3 * x + 1 + 1)
                            spread(x, 2)
                            gemm(setB, (2 * x + 1) % 3, 2).then_inc(used, 1)
                        for n in range(YS):
                            x, m = n // KT, n % KT
                            if m == 0:
                                pe.wait_ge(split, i * 6 + 5 + x + LEAD)
                                pe.wait_ge(low, i * 2 + x + 1 + 1)
                            if n == 0:
                                pe.wait_ge(gated, i * 2 + 2)
                            elif n == 1:
                                pe.wait_ge(hidden, i * 2 + 2 + 1)
                            else:
                                pe.wait_ge(added, i * YS + n + 1)
                            for c in range(3):
                                f, t = slice(P * m, P * m + P), slice(CH * c, CH * c + CH)
                                last = mm3(pe, bank_sets(m)[:, c, :], wh[:, 1 + x, f], wl[:, 1 + x, f],
                                           high_of(KT + x)[:, t], low_of(KT + x)[:, t], True, True)
                            last.then_inc(y_done, 1)
                            if m == KT - 1:
                                pe.wait_ge(y_done, i * YS + n + 1)
                                pe.sem_inc(used, 1)

                @block.scalar
                def _(act):
                    for stage in before:
                        stage.run("scalar", act)
                    act.sem_inc(sel_set, 1)
                    with act.Fori(0, STEPS) as i:
                        act.wait_ge(sel_set, i + 1)
                        act.dma_start(sel_raw, a["sel"][ds(i, 1)].rearrange("a p f -> (a p) f")).then_inc(sel_in, 16)
                        act.wait_ge(sel_in, i * 16 + 16)
                        act.wait_ge(weighed, i * 6 + 1)
                        act.copy(sel, sel_raw).then_inc(sel_set, 1)
                        for x in range(2):
                            act.wait_ge(used, i * 6 + 2 * x + 1 + 3)
                            act.wait_ge(low, i * 2 + x + 1)
                            act.activation(rows(tmp[:, x, :]), setA, ACT.Silu).then_inc(gated, 1)
                            act.wait_ge(hidden, i * 2 + x + 1 + 1)
                            act.copy(high_of(KT + x), tmp[:, 2 + x, :]).then_inc(high, 1)

                @block.vector
                def _(dve):
                    for stage in before:
                        stage.run("vector", dve)
                    dve.sem_inc(low, 1)
                    dve.sem_inc(hidden, 1)
                    dve.sem_inc(weighed, 1)
                    dve.sem_inc(added, 2)
                    with dve.Fori(0, STEPS) as i:
                        def low_half(x):
                            dve.wait_ge(high, i * 2 + x + 1)
                            dve.tensor_tensor(low_of(KT + x), tmp[:, 2 + x, :], high_of(KT + x).bitcast(F32),
                                              ALU.subtract).then_inc(low, 1)

                        def add(n):
                            dve.wait_ge(y_done, i * YS + n + 1)
                            xm = rows(x_t[:, n % KT, :])
                            dve.tensor_tensor(xm, bank_sets(n), xm, ALU.add).then_inc(added, 1)

                        for x in range(2):
                            dve.wait_ge(gated, i * 2 + x + 1)
                            for c in range(3):
                                s = tmp[:, x, CH * c:CH * c + CH]
                                dve.wait_ge(wide, i * 6 + 3 * x + c + 1)
                                dve.tensor_tensor(s, s, ps[:, 6 + c % 2, 0:CH], ALU.mult).then_inc(weighed, 1)
                            dve.wait_ge(used, i * 6 + 2 * x + 2 + 3)
                            dve.wait_ge(weighed, i * 6 + 3 * x + 3 + 1)
                            dve.tensor_tensor(rows(tmp[:, 2 + x, :]), rows(tmp[:, x, :]), setB, ALU.mult)\
                               .then_inc(hidden, 1)
                            if x:
                                add(0)
                            low_half(x)
                        for n in range(1, YS):
                            add(n)

        def finish():
            stored = sem("out_stored")
            with nc.Block("finish") as block:
                @block.sync
                def _(sp):
                    sp.dma_start(out, x_t).then_inc(stored, 16)
                    sp.wait_ge(stored, 16)

        raw_extra = sb("bias_rows", [P, 256], F32)
        v_all = xres[:, 0:TT * H * VW].rearrange("p (j f) -> p j f", j=TT)
        kvt = xres[:, 5200:5200 + 8 * 256].rearrange("p (m f) -> p m f", m=8)
        setup()
        end_phase()
        with_scratch("graph", lambda: (graph(), end_phase(), linear_kv(layernorm("ln0", sums_at=spare["plain"][:, NT:2 * NT]))), 6260)
        end_phase()
        linear_out()
        end_phase()
        with_kept_rows(lambda: (product("sparse", wg_s, 0, load=a["x_t"], fetch=KT), end_phase(), product("out0", a["l0_o"], 1, prep=FromAttention("out0_prep", KT), sums=True)))
        end_phase()
        with_scratch("ffn8", lambda: int8_product(layernorm("ln1", quantise=True)))
        end_phase()
        with_scratch("vh", lambda: node_major(layernorm("ln2")))
        end_phase()
        with_scratch("fa", feature_attention, 6260)
        end_phase()
        with_two_more_tiles("gcn", lambda: product("gcn", h_s, None, k_tiles=TT, per=5 * P, parts=2, load=x2_s, fetch=4, prep=FromCounts("gcn_prep")))
        end_phase()
        product("out1", a["l1_o"], 4, prep=FromAttention("out1_prep", 4), sums=True)
        end_phase()
        with_gate(lambda: experts(layernorm("ln3"), gating()))
        end_phase()
        finish()
        end_phase()


def layout(v):
    f = np.float32
    x_t = np.zeros((P, KT, NT), f)
    x_t[:, :, :N] = v["x"].T.reshape(KT, P, N).transpose(1, 0, 2)

    def stat(w):
        k, m = w.shape
        return np.ascontiguousarray(w.reshape(k // P, P, m // P, P).transpose(2, 1, 0, 3)).reshape(m // P, P, k)

    def mov(w):
        k, m = w.shape
        return np.ascontiguousarray(w.reshape(2, 4, P, m // 256, 256).transpose(3, 0, 2, 1, 4)).reshape(-1, P, ITEM)

    def bc(b):
        return b.reshape(-1, P).T

    consts = np.zeros((P, C_ALL), f)
    consts[:, C_ID:C_ID + P] = np.eye(P)
    consts[:, C_ONE:C_ONE + P] = 1
    consts[:64, C_MASK:C_MASK + 64] = 1
    consts[64:, C_MASK + 64:C_MASK + P] = 1
    consts[:, C_IOTA8:C_IOTA8 + 8] = 8 - np.arange(8)
    bias_cols = np.zeros((P, 8, KT), f)
    for n, name in enumerate(["L0_gnn_bias", "L0_mix_bo", "L1_mix_bk", "L1_mix_bq", "L1_mix_bo"]):
        bias_cols[:, n, :] = bc(v[name])
    o = {
        "consts": consts, "bias_cols": bias_cols, "x_t": x_t,
        "iota": np.tile(np.arange(NR, dtype=f), (P, 1)), 
        "src": np.ascontiguousarray(v["src"].reshape(ET, EP).T), "dst": np.ascontiguousarray(v["dst"].reshape(ET, EP).T),
        "edge_w": np.ascontiguousarray(v["edge_weight"].reshape(ET, EP).T),
    }
    def pairs(*ws):
        return np.ascontiguousarray(np.stack([w.reshape(4, -1, P, ITEM) for w in ws], 1)).reshape(-1, P, ITEM)

    o["l0_kv"] = pairs(mov(v["L0_mix_Wk"]), mov(v["L0_mix_Wv"]))
    o["l0_q"] = stat(v["L0_mix_Wq"])
    o["l0_o"] = stat(v["L0_mix_Wo"])
    o["ffn_rhs"] = stat(v["L0_ffn_rhs"])
    o["l1_vh"] = np.concatenate([mov(np.ascontiguousarray(v["L1_gnn_W"].T)), mov(v["L1_mix_Wv"])])
    vh = np.concatenate([v["L1_gnn_b"], v["L1_mix_bv"]]).reshape(8, 1, 256)
    o["l1_vh_bias"] = np.ascontiguousarray(np.broadcast_to(vh, (8, P, 256)))
    kq = np.stack([stat(v["L1_mix_Wk"]), stat(v["L1_mix_Wq"])], 1)
    o["l1_kq"] = np.ascontiguousarray(kq).reshape(2 * KT, P, ITEM)
    o["l1_o"] = stat(v["L1_mix_Wo"])
    ws = v["L1_ffn_Ws"].reshape(KT, P, NEXP).transpose(1, 0, 2)
    o["Ws"] = np.ascontiguousarray(ws).reshape(P, KT * NEXP)
    o["bs"] = np.tile(v["L1_ffn_bs"], (P, TT))
    hid = NEXP * FF
    gu = np.zeros((2, D, FT * P), f)
    gu[0, :, :hid] = v["L1_ffn_Wg"].transpose(1, 0, 2).reshape(D, hid)
    gu[1, :, :hid] = v["L1_ffn_Wu"].transpose(1, 0, 2).reshape(D, hid)
    down = np.zeros((FT * P, D), f)
    down[:hid] = v["L1_ffn_Wd"].reshape(hid, D)
    moe = np.zeros((FT // 2, 6, P, ITEM), f)
    moe[:, 0:4:2] = stat(gu[0]).reshape(FT // 2, 2, P, ITEM)
    moe[:, 1:4:2] = stat(gu[1]).reshape(FT // 2, 2, P, ITEM)
    moe[:, 4:6] = down.reshape(FT // 2, 2, P, ITEM)
    o["moe"] = moe.reshape(-1, P, ITEM)
    owner = (np.arange(FT * P) // FF).reshape(FT // 2, 1, 2 * P)
    sel = np.zeros((FT // 2, 40, 2 * P), f)
    sel[:, 0:NEXP] = sel[:, 32:32 + NEXP] = owner == np.arange(NEXP).reshape(1, NEXP, 1)
    o["sel"] = sel
    o["rm"] = np.tile(v["L1_mix_random_matrix"], (2, 1))
    return o


def kernel(**inputs):
    from concourse import bacc
    from concourse.bass_utils import run_bass_kernel_spmd

    arrays = layout({k: np.asarray(v) for k, v in inputs.items()})
    nc = bacc.Bacc("TRN2", target_bir_lowering=False, num_devices=1)
    a = {k: nc.dram_tensor(k, v.shape, mybir.dt.from_np(v.dtype), kind="ExternalInput").ap() for k, v in arrays.items()}
    out = nc.dram_tensor("out", (P, KT, NT), F32, kind="ExternalOutput").ap()
    gps_kernel(nc, a, out)
    got = run_bass_kernel_spmd(nc, [arrays], core_ids=[0]).results[0]["out"]
    return np.ascontiguousarray(got.transpose(1, 0, 2).reshape(D, NT)[:, :N].T)
```

```python
from contextlib import ExitStack

import numpy as np
import concourse.bass as bass
from concourse import mybir

F32, F32R, I32 = mybir.dt.float32, mybir.dt.float32r, mybir.dt.int32
ALU, ACT, AX = mybir.AluOpType, mybir.ActivationFunctionType, mybir.AxisListType
ds = bass.ds

P = 128
N = 1250
D = 1024
KT = D // P
CH = 418
NT = 3 * CH
TT = 10
NR = TT * P
E = 20000
EP = 125
ET = E // EP
H, HD = 16, 64
M = 256
NEXP, FF = 8, 344
FT = 22
ITEM = 1024
TOKS = [P] * 9 + [N - 9 * P]
VW = HD + 1
MAGIC = 1.5 * 2.0 ** 23

C_ID = 0
C_ONE = C_ID + P
C_MASK = C_ONE + P
C_MEAN = C_MASK + P
C_IOTA8 = C_MEAN + P
C_ALL = C_IOTA8 + 8


def cuts(j):
    lo, hi, out = P * j, min(P * (j + 1), NT), []
    while lo < hi:
        b = lo // CH
        end = min(hi, CH * (b + 1))
        out.append((b, lo - CH * b, lo - P * j, end - P * j))
        lo = end
    return out


def mm3(pe, out, lh, ll, rh, rl, first, last):
    pe.matmul(out, lh, rh, start=first, stop=False)
    pe.matmul(out, lh, rl, start=False, stop=False)
    return pe.matmul(out, ll, rh, start=False, stop=last)


def gps_kernel(nc, a, out):
    ctx = ExitStack()

    def sb(name, shape, dt):
        return ctx.enter_context(nc.sbuf_tensor(name, shape, dt))

    carried = {"items": 0, "next": 0}
    phase_sems = []

    def sem(name):
        phase_sems.append(nc.alloc_semaphore(name))
        return phase_sems[-1]

    def end_phase():
        nc.clear_and_free_semaphores(list(phase_sems))
        nc.all_engine_barrier()
        phase_sems.clear()
        carried["items"], carried["next"] = carried["next"], 0

    def dram(name, shape):
        return nc.dram_tensor(name, shape, F32, kind="Internal").ap()

    with ctx:
        rh = sb("rh", [P, KT, NR], F32R)
        rl = sb("rl", [P, KT, NR], F32R)
        xres = sb("xres", [P, 10400], F32)
        raw = sb("raw", [P, 2, ITEM], F32)
        wh = sb("wh", [P, 4, ITEM], F32R)
        wl = sb("wl", [P, 4, ITEM], F32R)
        tmp = sb("tmp", [P, 4, NT], F32)
        cst = sb("cst", [P, C_ALL], F32)
        col = sb("col", [P, 6, TT], F32)
        bcol = sb("bcol", [P, 8, KT], F32)
        dcolq = sb("dcolq", [P, TT], F32)
        dcol = sb("dcol", [P, TT], F32)
        ps = ctx.enter_context(nc.psum_tensor("ps", [P, 8, 512], F32))
        x_t = xres[:, 0:KT * NT].rearrange("p (k t) -> p k t", k=KT)
        ident, ones, mask2 = cst[:, C_ID:C_ID + P], cst[:, C_ONE:C_ONE + P], cst[:, C_MASK:C_MASK + P]
        mean_of = cst[:, C_MEAN:C_MEAN + P]
        setA, setB = ps[:, 0:3, 0:CH], ps[:, 3:6, 0:CH]

        def rows(t):
            return t.rearrange("p (c t) -> p c t", c=3)

        cnt_s = dram("cnt_s", [TT, P, NT])
        wg_s = dram("wg_s", [KT, P, ITEM])
        att_s = dram("att_s", [KT, P, NT])
        x2_s = dram("x2_s", [P, KT, NT])
        h_s = dram("h_s", [KT * 2, P, 5 * P])

        consts_in = ctx.enter_context(nc.semaphore("consts_in"))

        spare = {}

        def high_of(k):
            return rh[:, k, 0:NT] if k < KT else spare["high"][:, k - KT, :]

        def low_of(k):
            return rl[:, k, 0:NT] if k < KT else spare["low"][:, k - KT, :]

        def with_two_more_tiles(name, phase):
            with nc.sbuf_tensor(name + "_more_high", [P, 2, NT], F32R) as spare["high"], \
                    nc.sbuf_tensor(name + "_more_low", [P, 2, NT], F32R) as spare["low"]:
                phase()

        def with_scratch(name, phase, size=5120):
            with nc.sbuf_tensor(name + "_scratch", [P, size], F32) as spare["plain"]:
                phase()

        def with_gate(phase):
            with nc.sbuf_tensor("gate", [P, (KT + TT) * NEXP], F32) as spare["gate"], \
                    nc.sbuf_tensor("gate_halves", [P, (4 * KT + TT) * NEXP], F32R) as spare["gate_halves"], \
                    nc.sbuf_tensor("gate_work", [P, TT * (5 * NEXP + 5)], F32) as spare["gate_work"]:
                with_two_more_tiles("moe", phase)

        def with_kept_rows(phases):
            with nc.sbuf_tensor("kept_rows", [P, 4, NT], F32) as spare["kept"]:
                phases()

        def setup():
            with nc.Block("setup") as block:
                @block.sync
                def _(sp):
                    sp.dma_start(cst[:, :], a["consts"]).then_inc(consts_in, 16)
                    sp.dma_start(bcol[:, :, :], a["bias_cols"]).then_inc(consts_in, 16)
                    sp.wait_ge(consts_in, 32)

                @block.vector
                def _(dve):
                    dve.memset(col[:, :, :], 1.0)
                    dve.memset(dcolq[:, :], 1.0)
                    dve.memset(dcol[:, :], 1.0)
                    dve.memset(rh[:, :, NT:NR].bitcast(F32), 0.0)
                    dve.memset(rl[:, :, NT:NR].bitcast(F32), 0.0)

        def graph():
            onehot_src = rh[0:EP, 0:2, 0:NT]
            zeros = rl[:, 4, 0:512]
            onehot_dst = [rl[0:EP, s, 0:P] for s in range(2)]
            w_hi_dst = [rl[0:EP, s, P:2 * P] for s in range(2)]
            w_lo_dst = [rl[0:EP, s, 2 * P:3 * P] for s in range(2)]
            ident_r = rl[:, 2, 0:P]
            w_hi = rl[0:EP, 3, 0:ET]
            w_lo = rl[0:EP, 3, ET:2 * ET]
            pieces = spare["plain"][:, 2 * NT:]

            def piece(size, at=[0]):
                at[0] += size
                return pieces[:, at[0] - size:at[0]]

            def thin(row, size):
                return tmp[0:1, row:row + 2, :].rearrange("p a b -> p (a b)")[:, 0:size]

            hit = piece(TT * ET)[0:EP, :]
            dloc_all = hit
            srcf, dstf, dtile, wraw = (piece(ET)[0:EP, :] for _ in range(4))
            src_l = pieces[0:EP, TT * ET:(TT + 2) * ET]
            iota = piece(NR)
            idx = raw[0:EP, 0, 0:2 * ET].bitcast(I32)
            rng_i, rng = piece(2 * TT)[0:1, :].bitcast(I32), piece(4 * TT)[0:1, :]
            steps = dtile[0:1, :]
            tile_i = idx[:, ET:2 * ET]
            range_f, first_rev = thin(0, TT * ET), thin(2, TT * ET)
            got, prep, hits_up, ranges = sem("g_loads"), sem("g_prep"), sem("g_hits_counted"), sem("g_ranges")
            slot_free, onehots = sem("g_slot_free"), sem("g_onehots")
            tile_done, tile_out = sem("g_tile_done"), sem("g_tile_out")
            counts_out = [sem(f"g_counts_stored{s}") for s in range(2)]
            weights_out = [sem(f"g_weights_stored{s}") for s in range(2)]
            chain = sem("g_dve_chain")
            cnt_copied, deg_sqrt = sem("g_counts_copied"), sem("g_deg_sqrt")
            deg_seen = sem("g_degree_products")

            col_sums = ps[:, 0, :]
            total = spare["plain"][:, 0:NT]
            x_sum, x_in, x_added = spare["plain"][:, NT:2 * NT], sem("g_x_in"), sem("g_x_added")
            added = sem("g_counts_added")

            def counts_area(j):
                return setA if j % 2 == 0 else ps[:, 5:8, 0:CH]

            def span(eng, j):
                first = eng.value_load(rng_i[0:1, 2 * j:2 * j + 1], min_val=0, max_val=ET // 2 - 1)
                count = eng.value_load(rng_i[0:1, 2 * j + 1:2 * j + 2], min_val=1, max_val=ET // 2)
                return first, count

            with nc.Block("graph") as block:
                @block.sync
                def _(sp):
                    sp.dma_start(iota, a["iota"]).then_inc(got, 16)
                    sp.dma_start(idx[:, 0:ET], a["src"]).then_inc(got, 16)
                    sp.dma_start(idx[:, ET:2 * ET], a["dst"]).then_inc(got, 16)
                    sp.dma_start(wraw, a["edge_w"]).then_inc(got, 16)
                    sp.dma_start(x_t, a["x_t"]).then_inc(x_in, 16)
                    sp.wait_ge(x_in, 16)

                @block.vector
                def _(dve):
                    link_n = [0]

                    def link(ins):
                        link_n[0] += 1
                        ins.then_inc(chain, 1)
                        dve.wait_ge(chain, link_n[0])

                    dve.wait_ge(got, 64)
                    dve.memset(total, 0.0).then_inc(added, 1)
                    dve.memset(zeros.bitcast(F32), 0.0).then_inc(prep, 1)
                    dve.tensor_copy(ident_r, ident).then_inc(prep, 1)
                    dve.tensor_copy(srcf, idx[:, 0:ET])
                    link(dve.tensor_copy(w_hi, wraw))
                    dve.tensor_tensor(w_lo, wraw, w_hi.bitcast(F32), ALU.subtract)
                    link(dve.tensor_copy(dstf, idx[:, ET:2 * ET]))
                    link(dve.tensor_scalar(tile_i, idx[:, ET:2 * ET], 7, None, ALU.logical_shift_right))
                    link(dve.tensor_copy(dtile, tile_i))
                    for j in range(TT):
                        last = dve.tensor_scalar(hit[:, ET * j:ET * j + ET], dtile, float(j), None, ALU.is_equal)
                    last.then_inc(prep, 1)
                    dve.wait_ge(prep, 3)
                    dve.wait_ge(hits_up, 1)
                    dve.tensor_scalar(steps, iota[0:1, 0:ET], 1.0, None, ALU.add)
                    for j in range(TT):
                        dve.tensor_scalar(dloc_all[:, ET * j:ET * j + ET], dstf, float(-P * j), None, ALU.add)
                    link(dve.tensor_scalar(range_f.rearrange("p (b n) -> p b n", b=4), ps[0:1, 0:4, 0:400],
                                           1.0, None, ALU.min))
                    r3 = range_f.rearrange("p (j t) -> p j t", j=TT)
                    f3 = first_rev.rearrange("p (j t) -> p j t", j=TT)
                    for j in range(TT):
                        last = dve.scalar_tensor_tensor(f3[:, j, :], steps, -1.0, r3[:, j, :], ALU.mult, ALU.mult)
                    link(last)
                    link(dve.scalar_tensor_tensor(first_rev, range_f, float(ET + 1), first_rev, ALU.mult, ALU.add))
                    for j in range(TT):
                        last = dve.tensor_tensor(r3[:, j, :], r3[:, j, :], steps, ALU.mult)
                    link(last)
                    link(dve.tensor_reduce(rng[:, 0:TT], f3, AX.X, ALU.max))
                    link(dve.tensor_reduce(rng[:, TT:2 * TT], r3, AX.X, ALU.max))
                    link(dve.tensor_scalar(rng[:, 0:TT], rng[:, 0:TT], -1.0, float(ET), ALU.mult, ALU.add))
                    link(dve.tensor_scalar(rng[:, 0:TT], rng[:, 0:TT], float(ET - 2), None, ALU.min))
                    link(dve.tensor_scalar(rng[:, TT:2 * TT], rng[:, TT:2 * TT], 1.0, None, ALU.add))
                    pairs = rng_i.rearrange("p (j c) -> p c j", c=2)
                    for c in range(2):
                        link(dve.tensor_copy(pairs[:, c, :], rng[:, c * TT:c * TT + TT]))
                    link(dve.tensor_scalar(rng_i, rng_i, 1, None, ALU.logical_shift_right))
                    link(dve.tensor_copy(rng.rearrange("p (a j c) -> p a c j", a=2, c=2)[:, 0], pairs))
                    f = rng[:, 0:2 * TT].rearrange("p (j c) -> p c j", c=2)
                    g = rng[:, 2 * TT:3 * TT]
                    link(dve.tensor_scalar(g, f[:, 0, :], 1.0, None, ALU.add))
                    link(dve.tensor_tensor(g, g, f[:, 1, :], ALU.max))
                    link(dve.tensor_tensor(g, g, f[:, 0, :], ALU.subtract))
                    dve.tensor_copy(pairs[:, 1, :], g).then_inc(ranges, 1)
                    dve.wait_ge(ranges, 1)
                    base = 0
                    for j in range(TT):
                        first, count = span(dve, j)
                        dloc = pieces[0:EP, ET * j:ET * j + 2 * ET]
                        w_hi_l, w_lo_l = rl[0:EP, 3, 0:2 * ET], rl[0:EP, 3, ET:3 * ET]
                        with dve.Fori(0, count) as i:
                            for s in range(2):
                                n = base + i * 2 + s
                                t = ds((first + i) * 2 + s, 1)
                                dve.wait_ge(slot_free, n + 1)
                                dve.tensor_scalar(onehot_src[:, s, :], iota[0:EP, 0:NT], src_l[:, t], None,
                                                  ALU.is_equal)
                                ins = dve.tensor_scalar(onehot_dst[s], iota[0:EP, 0:P], dloc[:, t], None, ALU.is_equal)
                                if j >= KT:
                                    ins.then_inc(onehots, 1)
                                if j < KT:
                                    dve.tensor_scalar(w_hi_dst[s], iota[0:EP, 0:P], dloc[:, t],
                                                      w_hi_l[:, t].bitcast(F32), ALU.is_equal, ALU.mult)
                                    dve.tensor_scalar(w_lo_dst[s], iota[0:EP, 0:P], dloc[:, t],
                                                      w_lo_l[:, t].bitcast(F32), ALU.is_equal,
                                                      ALU.mult).then_inc(onehots, 1)
                        base = dve.snap(base + count * 2)
                    deg, y, v = col[:, 0, :], col[:, 1, :], col[:, 2, :]
                    dve.wait_ge(deg_sqrt, 1)
                    dve.tensor_copy(deg[:, 0:TT - 1], col_sums[:, 0:TT - 1])
                    link(dve.tensor_copy(deg[0:NT - 9 * P, TT - 1:TT], col_sums[0:NT - 9 * P, TT - 1:TT]))
                    link(dve.reciprocal(y, col[:, 3, :]))
                    newton(dve, link, y, deg, v)
                    link(dve.tensor_copy(dcol[:, :], y))

                @block.tensor
                def _(pe):
                    pe.sem_inc(slot_free, 2)
                    pe.wait_ge(prep, 3)
                    for b in range(4):
                        last = pe.matmul(ps[0:1, b, 0:400], ones[0:EP, 0:1], hit[:, 400 * b:400 * b + 400],
                                         start=True, stop=True)
                    last.then_inc(hits_up, 1)
                    pe.wait_ge(ranges, 1)
                    base = 0
                    for j in range(TT):
                        _, count = span(pe, j)
                        if j >= 2:
                            pe.wait_ge(cnt_copied, j - 1)
                        for n in range(3):
                            pe.matmul(counts_area(j)[:, n, :], zeros[:, 0:P], zeros[:, 0:CH], start=True, stop=False)
                        for b, c, lo, hi in cuts(j):
                            pe.matmul(counts_area(j)[:, b, c:c + hi - lo], ident_r, ident_r[:, lo:hi], start=False, stop=False)
                        if 1 <= j < KT:
                            pe.wait_ge(tile_out, j)
                        if j < KT:
                            for n in range(2):
                                pe.matmul(ps[:, 3 + n, :], zeros[:, 0:P], zeros, start=True, stop=False)
                        with pe.Fori(0, count) as i:
                            for s in range(2):
                                pe.wait_ge(onehots, base + i * 2 + s + 1)
                                for n in range(3):
                                    last = pe.matmul(counts_area(j)[:, n, :], onehot_dst[s],
                                                     onehot_src[:, s, CH * n:CH * n + CH], start=False, stop=False)
                                if j < KT:
                                    for part in (w_hi_dst[s], w_lo_dst[s]):
                                        for n in range(2):
                                            last = pe.matmul(ps[:, 3 + n, :], part,
                                                             onehot_src[:, s, 512 * n:512 * n + 512],
                                                             start=False, stop=False)
                                last.then_inc(slot_free, 1)
                        base = pe.snap(base + count * 2)
                        for n in range(3):
                            last = pe.matmul(counts_area(j)[:, n, :], zeros[:, 0:P], zeros[:, 0:CH], start=False, stop=True)
                        if j < KT:
                            for n in range(2):
                                last = pe.matmul(ps[:, 3 + n, :], zeros[:, 0:P], zeros, start=False, stop=True)
                        last.then_inc(tile_done, 1)
                    pe.wait_ge(added, TT + 1)
                    node_sums(pe, 0, total).then_inc(deg_seen, 1)

                @block.gpsimd
                def _(pool):
                    pool.wait_ge(x_in, 16)
                    pool.tensor_tensor(x_sum, x_t[:, 0, :], x_t[:, 1, :], ALU.add).then_inc(x_added, 1)
                    for k in range(2, KT):
                        pool.wait_ge(x_added, k - 1)
                        pool.tensor_tensor(x_sum, x_sum, x_t[:, k, :], ALU.add).then_inc(x_added, 1)
                    for j in range(TT):
                        pool.wait_ge(cnt_copied, j + 1)
                        pool.wait_ge(added, j + 1)
                        pool.tensor_tensor(total, total, tmp[:, j % 2, :], ALU.add).then_inc(added, 1)

                @block.scalar
                def _(act):
                    for j in range(TT):
                        act.wait_ge(tile_done, j + 1)
                        if j >= 2:
                            act.wait_ge(counts_out[j % 2], 16 * (j // 2))
                            act.wait_ge(added, j)
                        if 2 <= j < KT:
                            act.wait_ge(weights_out[j % 2], 16 * (j // 2))
                        if j < KT:
                            act.copy(tmp[:, 2 + j % 2, 0:D].rearrange("p (c t) -> p c t", c=2),
                                     ps[:, 3:5, :]).then_inc(tile_out, 1)
                        act.copy(rows(tmp[:, j % 2, :]), counts_area(j)).then_inc(cnt_copied, 1)
                        act.wait_ge(cnt_copied, j + 1)
                        act.dma_start(cnt_s[j], tmp[:, j % 2, :]).then_inc(counts_out[j % 2], 16)
                        if j < KT:
                            act.wait_ge(tile_out, j + 1)
                            act.dma_start(wg_s[:, :, P * j:P * j + P].rearrange("m p f -> p m f"),
                                          tmp[:, 2 + j % 2, 0:D].rearrange("p (m f) -> p m f", m=KT))\
                               .then_inc(weights_out[j % 2], 16)
                    act.wait_ge(deg_seen, 1)
                    act.activation(col[:, 3, 0:TT - 1], col_sums[:, 0:TT - 1], ACT.Sqrt)
                    act.activation(col[0:NT - 9 * P, 3, TT - 1:TT], col_sums[0:NT - 9 * P, TT - 1:TT],
                                   ACT.Sqrt).then_inc(deg_sqrt, 1)
                    for s in range(2):
                        act.wait_ge(counts_out[s], 16 * TT // 2)
                        act.wait_ge(weights_out[s], 16 * KT // 2)

        def newton(dve, link, y, v, t):
            link(dve.tensor_tensor(t, y, y, ALU.mult))
            link(dve.tensor_tensor(t, t, v, ALU.mult))
            link(dve.tensor_scalar(t, t, -0.5, 1.5, ALU.mult, ALU.add))
            link(dve.tensor_tensor(y, y, t, ALU.mult))

        LEAD = 2
        TILE_BANKS = (6, 7, 0, 3)
        SLOTS = 4

        class Chain:

            def __init__(self, eng, name, per=0):
                self.eng, self.sem, self.n, self.off, self.per = eng, sem(name), 0, 0, per

            def __call__(self, ins):
                self.n += 1
                ins.then_inc(self.sem, 1)
                self.eng.wait_ge(self.sem, self.off + self.n)

        def stream_load(sp, items, count, width, raw_in, split, unroll, then=None):
            def load(n, q, source, size):
                sp.wait_ge(split, n + 1)
                sp.dma_start(raw[:, q % 2, 0:size], source.rearrange("a p f -> (a p) f")).then_inc(raw_in[q % 2], 16)

            ahead = carried["items"]
            if ahead:
                for q in range(ahead):
                    sp.sem_inc(raw_in[q], 16)
                for q in range(ahead, unroll):
                    load(q, q, items[q:q + 1], width)
            with sp.Fori(1 if ahead else 0, count // unroll) as i:
                for q in range(unroll):
                    n = i * unroll + q
                    load(n, q, items[ds(n, 1)], width)
            if then is not None:
                for q in range(2):
                    load(count + q, q, then[0][q:q + 1], then[1])

        def stream_split(pool, name, count, width, raw_in, split, used, used_of, unroll, slots=4, before=(), then=None):
            halves, claimed = sem(name + "_high_half"), sem(name + "_slot_claimed")

            def one(n, q, loads, free, size):
                pool.wait_ge(raw_in[q % 2], loads * 16)
                pool.wait_ge(used, free)
                pool.sem_inc(claimed, 1)
                pool.tensor_copy(wh[:, q % slots, 0:size], raw[:, q % 2, 0:size]).then_inc(halves, 1)
                pool.wait_ge(halves, n + 1)
                pool.tensor_tensor(wl[:, q % slots, 0:size], raw[:, q % 2, 0:size],
                                   wh[:, q % slots, 0:size].bitcast(F32), ALU.subtract).then_inc(split, 1)

            ahead = carried["items"]
            pool.sem_inc(split, LEAD + ahead)
            if ahead:
                pool.sem_inc(halves, ahead)
            start = 0
            if before or ahead:
                start = 1
                for q in range(ahead, unroll):
                    if q == slots - 1:
                        for stage in before:
                            stage.run("gpsimd", pool)
                    one(q, q, q // 2 + 1, used_of(0, q), width)
            with pool.Fori(start, count // unroll) as i:
                for q in range(unroll):
                    one(i * unroll + q, q, i * (unroll // 2) + q // 2 + 1, used_of(i, q), width)
            if then is not None:
                carried["next"] = 2
                for q in range(2):
                    one(count + q, q, count // 2 + 1, then[2][q], then[1])

        def bank_sets(q):
            return setA if q % 2 == 0 else setB

        def broadcast_cols(pe, area, v):
            last = None
            for j in range(TT):
                _, column = bass.broadcast_tensor_aps(ident, v[:, j:j + 1])
                for b, c, lo, hi in cuts(j):
                    last = pe.matmul(area[:, b, c:c + hi - lo], column, ident[:, lo:hi], start=True, stop=True)
            return last

        def node_sums(pe, bank, src, first=True, only=True):
            last = None
            for j in range(TT):
                w = min(P, NT - P * j)
                last = pe.matmul(ps[0:w, bank, j:j + 1], src[:, P * j:P * j + w], ones[:, 0:1],
                                 start=(first and j == 0), stop=only, skip_group_check=True)
            return last

        def node_cols(eng_op, dst, bank):
            eng_op(dst[:, 0:TT - 1], ps[:, bank, 0:TT - 1])
            w = NT - 9 * P
            return eng_op(dst[0:w, TT - 1:TT], ps[0:w, bank, TT - 1:TT])

        class Stage:

            def __init__(self, done, **programs):
                self.done, self.programs = done, programs

            def wait_nodes(self, pe, j):
                pe.wait_ge(self.done, KT * ((min(P * (j + 1), NT) - 1) // CH + 1))

            def run(self, name, eng):
                if self.programs.get(name) is not None:
                    self.programs[name](eng)

        sum_row = tmp[:, 2, :]

        def layernorm(name, sums_at=None, quantise=False, unsummed=()):
            var, rstd, std, t = (col[:, n, :] for n in range(1, 5))
            scale, shifted = dcolq[:, :], sem(name + "_shifted")
            pieces = [(c, k, slice(CH * c, CH * c + CH)) for c in range(3) for k in range(KT)]
            top = spare["plain"][:, 3 * P:3 * P + NT] if quantise else None
            rstd_in, wide = sem(name + "_rstd"), sem(name + "_broadcast")
            centred, squared, sq_used = sem(name + "_centred"), sem(name + "_squared"), sem(name + "_squares_summed")
            rooted, var_in, paired = sem(name + "_std"), sem(name + "_var"), sem(name + "_paired")
            normed, high, low = sem(name + "_normed"), sem(name + "_high"), sem(name + "_low")
            turned, top_done = sem(name + "_turned"), sem(name + "_top_done")
            def vector(dve):
                link = Chain(dve, name + "_chain")
                if quantise:
                    link(dve.memset(top, 0.0))
                dve.wait_ge(wide, 1)
                def pair(g):
                    dve.wait_ge(squared, 2 * g + 2)
                    dve.tensor_tensor(tmp[:, 2, :], tmp[:, 2, :], tmp[:, 3, :], ALU.add).then_inc(paired, 1)

                for k in range(KT):
                    if k >= 2:
                        dve.wait_ge(squared, k - 1)
                    dve.tensor_tensor(rows(tmp[:, k % 2, :]), rows(x_t[:, k, :]), setA, ALU.subtract)\
                       .then_inc(centred, 1)
                    if k % 2 == 0 and k:
                        pair(k // 2 - 1)
                    if quantise:
                        dve.wait_ge(centred, k + 1)
                        link(dve.tensor_tensor(top, tmp[:, k % 2, :], top, ALU.max))
                        link(dve.scalar_tensor_tensor(top, tmp[:, k % 2, :], -1.0, top, ALU.mult, ALU.max))
                pair(KT // 2 - 1)
                if quantise:
                    dve.sem_inc(top_done, 1)
                dve.wait_ge(sq_used, KT // 2)
                node_cols(lambda o, i: dve.tensor_scalar(o, i, 1.0 / D, 1e-5, ALU.mult, ALU.add), var, 7)\
                    .then_inc(var_in, 1)
                dve.wait_ge(rooted, 1)
                link(dve.reciprocal(rstd, std))
                newton(dve, link, rstd, var, t)
                if quantise:
                    dve.wait_ge(turned, 1)
                    for b in range(3):
                        n = min(4, 9 - 4 * b)
                        dve.tensor_reduce(scale[:, 4 * b:4 * b + n],
                                          ps[:, 3 + b, 0:P * n].rearrange("p (j c) -> p j c", c=P), AX.X, ALU.max)
                    w = NT - 9 * P
                    link(dve.tensor_reduce(scale[0:w, 9:10], ps[0:w, 5, P:2 * P], AX.X, ALU.max))
                    link(dve.tensor_tensor(scale, scale, rstd, ALU.mult))
                    link(dve.tensor_scalar(scale, scale, 1e-12, 1.0 / 127.0, ALU.max, ALU.mult))
                    link(dve.reciprocal(t, scale))
                    link(dve.tensor_tensor(rstd, rstd, t, ALU.mult))
                dve.sem_inc(rstd_in, 1)
                dve.wait_ge(wide, 2)
                if quantise:
                    for k in range(KT):
                        s = k % 3
                        link(dve.tensor_tensor(rows(tmp[:, s, :]), rows(x_t[:, k, :]), setA, ALU.subtract))
                        link(dve.tensor_tensor(rows(tmp[:, s, :]), rows(tmp[:, s, :]), setB, ALU.mult))
                        dve.tensor_scalar(rh[:, k, 0:NT], tmp[:, s, :], MAGIC, -MAGIC, ALU.add, ALU.add)
                    return
                for n, (c, k, cols) in enumerate(pieces):
                    if k >= 4:
                        dve.wait_ge(low, n - 3)
                    dve.tensor_tensor(tmp[:, k % 4, cols], x_t[:, k, cols], setA[:, c, :], ALU.subtract)\
                       .then_inc(shifted, 1)
                    if n:
                        scale_piece(dve, n - 1)
                scale_piece(dve, len(pieces) - 1)

            def scale_piece(dve, n):
                c, k, cols = pieces[n]
                dve.wait_ge(shifted, n + 1)
                dve.tensor_tensor(tmp[:, k % 4, cols], tmp[:, k % 4, cols], setB[:, c, :], ALU.mult).then_inc(normed, 1)

            def scalar(act):
                for k in range(KT):
                    act.wait_ge(centred, k + 1)
                    if k < 2:
                        act.wait_ge(wide, 1)
                    elif k % 2 == 0:
                        act.wait_ge(sq_used, k // 2)
                    act.activation(tmp[:, 2 + k % 2, :], tmp[:, k % 2, :], ACT.Square).then_inc(squared, 1)
                act.wait_ge(var_in, 1)
                act.activation(std, var, ACT.Sqrt).then_inc(rooted, 1)
                if not quantise:
                    for n, (c, k, cols) in enumerate(pieces):
                        act.wait_ge(normed, n + 1)
                        act.copy(rh[:, k, cols], tmp[:, k % 4, cols]).then_inc(high, 1)

            if not quantise:
                def gpsimd(pool):
                    for n, (c, k, cols) in enumerate(pieces):
                        pool.wait_ge(high, n + 1)
                        pool.tensor_tensor(rl[:, k, cols], tmp[:, k % 4, cols], rh[:, k, cols].bitcast(F32),
                                           ALU.subtract).then_inc(low, 1)

            def tensor(pe):
                sources = [sum_row if sums_at is None else sums_at] + [x_t[:, k, :] for k in unsummed]
                for c in range(3):
                    for n, source in enumerate(sources):
                        last = pe.matmul(setA[:, c, :], mean_of, source[:, CH * c:CH * c + CH],
                                         start=(n == 0), stop=(n == len(sources) - 1))
                last.then_inc(wide, 1)
                for g in range(KT // 2):
                    pe.wait_ge(paired, g + 1)
                    node_sums(pe, 7, tmp[:, 2, :], first=(g == 0), only=(g == KT // 2 - 1)).then_inc(sq_used, 1)
                if quantise:
                    pe.wait_ge(centred, KT)
                    pe.wait_ge(top_done, 1)
                    for j in range(TT):
                        w = min(P, NT - P * j)
                        last = pe.transpose(ps[0:w, 3 + j // 4, P * (j % 4):P * (j % 4) + P],
                                            top[:, P * j:P * j + w], ident)
                    last.then_inc(turned, 1)
                pe.wait_ge(rstd_in, 1)
                broadcast_cols(pe, ps[:, 3:6, :], rstd).then_inc(wide, 1)
            return Stage(vector=vector, scalar=scalar, tensor=tensor, gpsimd=None if quantise else gpsimd,
                         done=None if quantise else low)

        def linear_kv(*before):
            name = "lkv"
            then = (a["l0_q"], ITEM, (90, 90))
            kc = xres[:, 0:TT * 256].rearrange("p (j f) -> p j f", j=TT)
            vc = xres[:, 2560:2560 + TT * 260].rearrange("p (j h f) -> p j h f", j=TT, h=2)
            ex = xres[:, 7400:7912].rearrange("p (s f) -> p s f", s=2)
            raw_in = [sem(f"{name}_raw{s}") for s in range(2)]
            split, tiles = sem(name + "_split"), sem(name + "_tiles")
            freed, exped, k_in, v_in = sem(name + "_banks_free"), sem(name + "_exp"), sem(name + "_k"), sem(name + "_v")
            kv_done, kv_out, relued = sem(name + "_kv"), sem(name + "_kv_out"), sem(name + "_relu")
            v_ones = sem(name + "_ones")
            with nc.Block(name) as block:
                @block.sync
                def _(sp):
                    for stage in before:
                        stage.run("sync", sp)
                    stream_load(sp, a["l0_kv"], 16, ITEM, raw_in, split, 4, then)

                @block.gpsimd
                def _(pool):
                    stream_split(pool, name, 16, ITEM, raw_in, split, tiles, lambda i, q: i * 20 + (q // 2) * 10 + 10, 4,
                                 before=before, then=then)

                @block.tensor
                def _(pe):
                    pe.sem_inc(kv_done, 1)
                    pe.sem_inc(tiles, 2 * TT)
                    for stage in before:
                        stage.run("tensor", pe)
                    with pe.Fori(0, 4) as i:
                        for half in range(2):
                            pe.wait_ge(split, i * 4 + 2 * half + 2 + LEAD)
                            for j in range(TT):
                                t = TT * half + j
                                pe.wait_ge(freed, i * 20 + t + 1)
                                before[0].wait_nodes(pe, j)
                                for k in range(KT):
                                    s, c = 2 * half + k // 4, 256 * (k % 4)
                                    nodes = slice(P * j, P * j + P)
                                    last = mm3(pe, ps[:, TILE_BANKS[t % 4], 0:256], rh[:, k, nodes], rl[:, k, nodes],
                                               wh[:, s, c:c + 256], wl[:, s, c:c + 256], k == 0, k == KT - 1)
                                last.then_inc(tiles, 1)
                        pe.wait_ge(v_ones, 1)
                        pe.wait_ge(k_in, i * 10 + 10 + 1)
                        pe.wait_ge(v_in, i * 10 + 10)
                        pe.wait_ge(kv_out, i * 4 + 1)
                        for p in range(2):
                            for j in range(TT):
                                w = TOKS[j]
                                last = pe.matmul(ps[:, 4 + p, 0:P + 1], kc[0:w, j, P * p:P * p + P],
                                                 vc[0:w, j, p, 0:P + 1], start=(j == 0), stop=(j == TT - 1))
                            last.then_inc(kv_done, 1)

                @block.scalar
                def _(act):
                    for stage in before:
                        stage.run("scalar", act)
                    with act.Fori(0, 4) as i:
                        for j in range(TT):
                            act.wait_ge(consts_in, 32)
                            act.wait_ge(k_in, i * 10 + j + 1)
                            act.wait_ge(tiles, i * 20 + j + 1 + 2 * TT)
                            act.activation(ex[:, j % 2, :], ps[:, TILE_BANKS[j % 4], 0:256], ACT.Relu, scale=-1.0).then_inc(relued, 1)
                            act.wait_ge(consts_in, 32)
                            act.wait_ge(relued, i * 10 + j + 1)
                            act.activation(ex[:, j % 2, :], ex[:, j % 2, :], ACT.Exp, scale=-1.0).then_inc(exped, 1)
                        for j in range(TT):
                            act.wait_ge(kv_done, i * 2 + 1)
                            act.wait_ge(tiles, i * 20 + TT + j + 1 + 2 * TT)
                            act.copy(vc[:, j, :, 0:P], ps[:, TILE_BANKS[(TT + j) % 4], 0:256].rearrange("p (h f) -> p h f", h=2))\
                               .then_inc(v_in, 1)

                @block.vector
                def _(dve):
                    dve.sem_inc(freed, 4)
                    for stage in before:
                        stage.run("vector", dve)
                    dve.sem_inc(k_in, 1)
                    dve.memset(vc[:, :, :, P:P + 2], 1.0).then_inc(v_ones, 1)
                    dve.sem_inc(kv_out, 1)
                    with dve.Fori(0, 4) as i:
                        for j in range(TT):
                            dve.wait_ge(kv_done, i * 2 + 1)
                            dve.wait_ge(exped, i * 10 + j + 1)
                            dve.scalar_tensor_tensor(kc[:, j, :], ps[:, TILE_BANKS[j % 4], 0:256], 0.0, ex[:, j % 2, :],
                                                     ALU.max, ALU.add).then_inc(k_in, 1)
                            dve.wait_ge(k_in, i * 10 + j + 1 + 1)
                            dve.sem_inc(freed, 1)
                        for j in range(TT):
                            dve.wait_ge(v_in, i * 10 + j + 1)
                            dve.sem_inc(freed, 1)
                        for p in range(2):
                            dve.wait_ge(kv_done, i * 2 + p + 1 + 1)
                            dve.tensor_tensor(kvt[:, ds(2 * i + p, 1), 0:P].rearrange("p a f -> p (a f)"),
                                              ps[:, 4 + p, 0:P], mask2, ALU.mult).then_inc(kv_out, 1)
                            dve.tensor_scalar(kvt[:, ds(2 * i + p, 1), P:2 * P].rearrange("p a f -> p (a f)"),
                                              mask2, ps[:, 4 + p, P:P + 1], None, ALU.mult).then_inc(kv_out, 1)

        def linear_out():
            name = "lout"
            then = (wg_s, ITEM, (9, 10))
            ex = xres[:, 7400:7400 + NT]
            zt = xres[:, 8700:8700 + 2 * CH].rearrange("p (s f) -> p s f", s=2)
            numer = xres[:, 0:2 * CH].rearrange("p (s f) -> p s f", s=2)
            taken = sem(name + "_taken")
            stage = xres[:, 9600:9600 + 512].rearrange("p (s f) -> p s f", s=2)
            raw_in = [sem(f"{name}_raw{s}") for s in range(2)]
            store2 = [sem(f"{name}_rows_stored{s}") for s in range(2)]
            split, used, freed = sem(name + "_split"), sem(name + "_items_used"), sem(name + "_sets_free")
            staged, relued, exped, q_in = (sem(name + x) for x in ("_staged", "_relu", "_exp", "_q"))
            num, z_in, recip, att, stored = (sem(name + x) for x in ("_num", "_z", "_recip", "_att", "_stored"))
            with nc.Block(name) as block:
                @block.sync
                def _(sp):
                    stream_load(sp, a["l0_q"], 8, ITEM, raw_in, split, 2, then)

                @block.gpsimd
                def _(pool):
                    stream_split(pool, name, 8, ITEM, raw_in, split, used, lambda i, q: i * 2 + q + 1, 2, slots=2, then=then)

                @block.tensor
                def _(pe):
                    pe.sem_inc(used, 2)

                    def attend(n, q, c):
                        cols = slice(CH * c, CH * c + CH)
                        if c == 0:
                            pe.wait_ge(q_in, n + 1 + 1)
                            pe.wait_ge(staged, n + 1)
                        pe.wait_ge(taken, n * 3 + c + 1)
                        pe.matmul(ps[:, 7, 0:CH], stage[:, q % 2, P:2 * P], tmp[:, q % 2, cols], start=True, stop=True)
                        pe.matmul(ps[:, 6, 0:CH], stage[:, q % 2, 0:P], tmp[:, q % 2, cols], start=True, stop=True)\
                          .then_inc(num, 1)

                    AFTER = (9, 12, 16)

                    def gemm(n, q, attends):
                        pe.wait_ge(split, n + 1 + LEAD)
                        pe.wait_ge(freed, n + 1)
                        for c in range(3):
                            for k in range(KT):
                                f, t = slice(P * k, P * k + P), slice(CH * c, CH * c + CH)
                                last = mm3(pe, bank_sets(q)[:, c, :], wh[:, q, f], wl[:, q, f], rh[:, k, t], rl[:, k, t],
                                           k == 0, k == KT - 1)
                                if c == 2 and k == KT - 1:
                                    last.then_inc(used, 1)
                                if attends and c * KT + k + 1 in AFTER:
                                    attend(n - 1, 1 - q, AFTER.index(c * KT + k + 1))

                    gemm(0, 0, False)
                    with pe.Fori(0, KT // 2 - 1) as i:
                        gemm(i * 2 + 1, 1, True)
                        gemm(i * 2 + 2, 0, True)
                    gemm(KT - 1, 1, True)
                    for c in range(3):
                        attend(KT - 1, 1, c)

                @block.scalar
                def _(act):
                    act.sem_inc(taken, 1)
                    for s in range(2):
                        act.sem_inc(store2[s], 16)
                    with act.Fori(0, 2) as i:
                        for q in range(4):
                            n = i * 4 + q
                            act.wait_ge(att, (i * 12 + (3 * (q - 1) if q else 0)) + 1)
                            act.copy(stage[:, q % 2, :], kvt[:, ds(n, 1), :].rearrange("p a f -> p (a f)")).then_inc(staged, 1)
                            act.wait_ge(consts_in, 32)
                            act.wait_ge(q_in, n + 1)
                            act.wait_ge(used, n + 1 + 2)
                            act.activation(rows(ex), bank_sets(q), ACT.Relu, scale=-1.0).then_inc(relued, 1)
                            act.wait_ge(consts_in, 32)
                            act.wait_ge(relued, n + 1)
                            act.activation(ex, ex, ACT.Exp, scale=-1.0).then_inc(exped, 1)
                            for c in range(3):
                                act.wait_ge(consts_in, 32)
                                act.wait_ge(num, n * 3 + c + 1)
                                act.wait_ge(att, n * 3 + c if q or c else i * 12 + 1)
                                act.activation(zt[:, (q * 3 + c) % 2, :], ps[:, 7, 0:CH], ACT.Copy, bias=1e-6)\
                                   .then_inc(z_in, 1)
                                act.copy(numer[:, (q * 3 + c) % 2, :], ps[:, 6, 0:CH]).then_inc(taken, 1)
                            act.wait_ge(att, n * 3 + 3 + 1)
                            act.dma_start(att_s[ds(n, 1)].rearrange("a p f -> (a p) f"), tmp[:, 2 + q % 2, :])\
                               .then_inc(store2[q % 2], 16)
                    for s in range(2):
                        act.wait_ge(store2[s], 64 + 16)

                @block.vector
                def _(dve):
                    dve.sem_inc(q_in, 1)
                    dve.sem_inc(att, 1)
                    dve.sem_inc(freed, LEAD)
                    with dve.Fori(0, 2) as i:
                        for q in range(4):
                            n = i * 4 + q
                            dve.wait_ge(exped, n + 1)
                            dve.scalar_tensor_tensor(rows(tmp[:, q % 2, :]), bank_sets(q), 0.0, rows(ex),
                                                     ALU.max, ALU.add).then_inc(q_in, 1)
                            dve.wait_ge(q_in, n + 1 + 1)
                            dve.sem_inc(freed, 1)
                            dve.wait_ge(store2[q % 2], i * 32 + (q // 2) * 16 + 16)
                            for c in range(3):
                                zs = zt[:, (q * 3 + c) % 2, :]
                                dve.wait_ge(z_in, n * 3 + c + 1)
                                dve.reciprocal(zs, zs).then_inc(recip, 1)
                                dve.wait_ge(recip, n * 3 + c + 1)
                                dve.wait_ge(taken, n * 3 + c + 2)
                                dve.tensor_tensor(tmp[:, 2 + q % 2, CH * c:CH * c + CH], numer[:, (q * 3 + c) % 2, :], zs, ALU.mult)\
                                   .then_inc(att, 1)

        def att_row(k, early):
            return spare["kept"][:, k - 4, :] if early == KT and k >= 4 else tmp[:, k % 4, :]

        def product(name, items, bias, k_tiles=KT, per=ITEM, parts=1, load=None, prep=None,
                    fetch=0, sums=False, following=None):
            raw_in = [sem(f"{name}_raw{s}") for s in range(2)]
            split, used, freed = sem(name + "_split"), sem(name + "_items_used"), sem(name + "_sets_free")
            ready, x_in, fetched = sem(name + "_resident"), sem(name + "_x_in"), sem(name + "_rows_fetched")
            summed = sem(name + "_summed")
            kp, count = k_tiles // parts, KT * parts
            then = (following, ITEM, (count - 3 + SLOTS, count - 2 + SLOTS)) if following is not None else None
            if prep is not None:
                prep.begin(ready)
            with nc.Block(name) as block:
                @block.sync
                def _(sp):
                    stream_load(sp, items, count, per, raw_in, split, 4, then)

                @block.gpsimd
                def _(pool):
                    stream_split(pool, name, count, per, raw_in, split, used, lambda i, q: i * 4 + q + 1, 4,
                                 then=then)

                if prep is not None or load is not None:
                    @block.scalar
                    def _(act):
                        if prep is not None:
                            prep.scalar(act)
                        if load is not None:
                            act.wait_ge(split, 2 + LEAD)
                            act.dma_start(x_t, load).then_inc(x_in, 16)
                        if fetch:
                            if prep is not None:
                                act.wait_ge(ready, k_tiles)
                            for k in range(fetch):
                                act.dma_start(att_row(k, fetch), att_s[k]).then_inc(fetched, 16)
                            act.wait_ge(fetched, 16 * fetch)

                @block.tensor
                def _(pe):
                    if prep is not None:
                        prep.tensor(pe)
                    pe.sem_inc(used, SLOTS)
                    with pe.Fori(0, count // 4) as i:
                        for q in range(4):
                            n = i * 4 + q
                            pe.wait_ge(split, n + 1 + LEAD)
                            m, part = q // parts, q % parts
                            if part == 0:
                                pe.wait_ge(freed, i * (4 // parts) + m + 1)
                            for k in range(kp):
                                kk = part * kp + k
                                if prep is not None:
                                    pe.wait_ge(ready, kk + 1)
                                for c in range(3):
                                    f, t = slice(P * k, P * k + P), slice(CH * c, CH * c + CH)
                                    last = mm3(pe, bank_sets(m)[:, c, :], wh[:, q, f], wl[:, q, f],
                                               high_of(kk)[:, t], low_of(kk)[:, t], kk == 0, kk == k_tiles - 1)
                            last.then_inc(used, 1)

                @block.vector
                def _(dve):
                    dve.sem_inc(freed, 1)
                    if prep is not None:
                        prep.vector(dve)
                    dve.sem_inc(freed, 1)
                    if load is not None:
                        dve.wait_ge(x_in, 16)
                    if sums:
                        dve.wait_ge(ready, k_tiles)
                        dve.memset(sum_row, 0.0).then_inc(summed, 1)
                    with dve.Fori(0, count // 4) as i:
                        for m in range(4 // parts):
                            n = i * (4 // parts) + m
                            xm = x_t[:, ds(n, 1), :].rearrange("p a (c t) -> p (a c) t", c=3)
                            dve.wait_ge(used, i * 4 + (m + 1) * parts + SLOTS)
                            if bias is None:
                                ins = dve.tensor_tensor(xm, bank_sets(m), xm, ALU.add)
                            else:
                                ins = dve.scalar_tensor_tensor(xm, bank_sets(m), bcol[:, bias, ds(n, 1)], xm,
                                                               ALU.add, ALU.add)
                            ins.then_inc(freed, 1)
                            if sums:
                                dve.wait_ge(freed, n + 1 + LEAD)
                                dve.wait_ge(summed, n + 1)
                                dve.tensor_tensor(rows(sum_row), rows(sum_row), xm, ALU.add).then_inc(summed, 1)

        class FromAttention:

            def __init__(self, name, early):
                self.name, self.early = name, early

            def begin(self, ready):
                self.got = [sem(f"{self.name}_rows{s}") for s in range(4)]
                self.high, self.low = sem(self.name + "_high"), ready

            def scalar(self, act):
                for k in range(KT):
                    if k >= self.early:
                        act.wait_ge(self.got[k % 4], 16)
                    act.copy(rh[:, k, 0:NT], att_row(k, self.early)).then_inc(self.high, 1)
                    if 1 <= k and k + 3 >= self.early and k + 3 < KT:
                        act.wait_ge(self.low, k)
                        act.dma_start(att_row(k + 3, self.early), att_s[k + 3]).then_inc(self.got[(k + 3) % 4], 16)

            def vector(self, dve):
                for k in range(KT):
                    dve.wait_ge(self.high, k + 1)
                    dve.tensor_tensor(rl[:, k, 0:NT], att_row(k, self.early), rh[:, k, 0:NT].bitcast(F32),
                                      ALU.subtract).then_inc(self.low, 1)

            def tensor(self, pe):
                pass

        class FromCounts:

            def __init__(self, name):
                self.name = name

            def begin(self, ready):
                self.got = [sem(f"{self.name}_rows{s}") for s in range(3)]
                self.high, self.wide, self.scaled = (sem(self.name + x) for x in ("_high", "_wide", "_scaled"))
                self.low = ready

            def scalar(self, act):
                for k in range(3):
                    act.dma_start(tmp[:, k, :], cnt_s[k]).then_inc(self.got[k], 16)
                for k in range(TT):
                    act.wait_ge(self.scaled, k + 1)
                    act.copy(high_of(k), tmp[:, k % 3, :]).then_inc(self.high, 1)
                    if 1 <= k <= TT - 3:
                        act.wait_ge(self.low, k)
                        act.dma_start(tmp[:, (k + 2) % 3, :], cnt_s[k + 2]).then_inc(self.got[(k + 2) % 3], 16)

            def tensor(self, pe):
                broadcast_cols(pe, ps[:, 3:6, :], dcol).then_inc(self.wide, 1)

            def vector(self, dve):
                dve.wait_ge(self.wide, 1)
                for k in range(TT + 1):
                    if k < TT:
                        dve.wait_ge(self.got[k % 3], 16 * (k // 3 + 1))
                        dve.scalar_tensor_tensor(rows(tmp[:, k % 3, :]), rows(tmp[:, k % 3, :]), dcol[:, k:k + 1],
                                                 setB, ALU.mult, ALU.mult).then_inc(self.scaled, 1)
                    if k >= 1:
                        j = k - 1
                        dve.wait_ge(self.high, j + 1)
                        dve.tensor_tensor(low_of(j), tmp[:, j % 3, :], high_of(j).bitcast(F32),
                                          ALU.subtract).then_inc(self.low, 1)

        def int8_product(*before):
            name = "ffn8"
            raw_in = [sem(f"{name}_raw{s}") for s in range(2)]
            wide, slb = sem(name + "_scale_wide"), sem(name + "_scale_rows")
            topped, turned, colmax = sem(name + "_top"), sem(name + "_turned"), sem(name + "_colmax")
            inv_wide, quant, done, freed = (sem(name + x) for x in ("_inv_wide", "_quantised", "_products", "_free"))
            inv_diag, scaled, freed2 = sem(name + "_inv_diag"), sem(name + "_scaled"), sem(name + "_rows_added")
            lhs_done = sem(name + "_lhs_done")
            by_node, cleared, sum_added = sem(name + "_scaled_by_node"), sem(name + "_sums_cleared"), sem(name + "_sum_added")
            scale_row, srow = tmp[:, 3, :], bcol[:, 7, :]
            part, dg, least = (spare["plain"][:, P * n:P * n + P] for n in range(3))
            with nc.Block(name) as block:
                @block.sync
                def _(sp):
                    for stage in before:
                        stage.run("sync", sp)
                    for m in range(KT):
                        if m >= 2:
                            sp.wait_ge(quant, m - 1)
                        sp.dma_start(raw[:, m % 2, :], a["ffn_rhs"][m]).then_inc(raw_in[m % 2], 16)

                @block.vector
                def _(dve):
                    for stage in before:
                        stage.run("vector", dve)
                    link = Chain(dve, name + "_chain")
                    dve.sem_inc(lhs_done, 1)
                    dve.memset(sum_row, 0.0).then_inc(cleared, 1)
                    for m in range(KT + 3):
                        if m < KT:
                            w3 = raw[:, m % 2, :].rearrange("p (k f) -> p f k", k=KT)
                            wk = raw[:, m % 2, :].rearrange("p (k f) -> p k f", k=KT)
                            dve.wait_ge(raw_in[m % 2], 16 * (m // 2 + 1))
                            dve.tensor_reduce(part, w3, AX.X, ALU.max)
                            link(dve.tensor_reduce(least, w3, AX.X, ALU.min))
                            link(dve.scalar_tensor_tensor(part, least, -1.0, part, ALU.mult, ALU.max))
                            dve.sem_inc(topped, 1)
                            dve.wait_ge(turned, m + 1)
                            sc = srow[:, m:m + 1]
                            link(dve.tensor_reduce(sc, ps[:, 6, 0:P], AX.X, ALU.max))
                            link(dve.tensor_scalar(sc, sc, 1e-12, 1.0 / 127.0, ALU.max, ALU.mult))
                            link(dve.reciprocal(col[:, 0, 0:1], sc))
                            link(dve.tensor_scalar(dg, ident, col[:, 0, 0:1], None, ALU.mult))
                            dve.sem_inc(inv_diag, 1)
                            dve.wait_ge(inv_wide, m + 1)
                            full, inv = bass.broadcast_tensor_aps(wk, ps[:, 7, 0:P].rearrange("p (o f) -> p o f", o=1))
                            link(dve.tensor_tensor(wk, full, inv, ALU.mult))
                            dve.tensor_scalar(wh[:, m % 4, :], raw[:, m % 2, :], MAGIC, -MAGIC, ALU.add, ALU.add)\
                               .then_inc(quant, 1)
                        if m >= 3:
                            j = m - 3
                            dve.wait_ge(by_node, j + 1)
                            dve.tensor_tensor(x_t[:, j, :], x_t[:, j, :], tmp[:, j % 2, :], ALU.add).then_inc(freed2, 1)

                @block.gpsimd
                def _(pool):
                    pool.wait_ge(slb, 1)
                    pool.wait_ge(cleared, 1)
                    for m in range(KT):
                        pool.wait_ge(scaled, m + 1)
                        pool.tensor_tensor(tmp[:, m % 2, :], tmp[:, m % 2, :], scale_row, ALU.mult).then_inc(by_node, 1)
                        if 1 <= m < KT - 1:
                            pool.wait_ge(freed2, m)
                            if m > 1:
                                pool.wait_ge(sum_added, m - 1)
                            pool.tensor_tensor(sum_row, sum_row, x_t[:, m - 1, :], ALU.add).then_inc(sum_added, 1)

                @block.scalar
                def _(act):
                    for stage in before:
                        stage.run("scalar", act)
                    act.wait_ge(wide, 1)
                    act.copy(rows(scale_row), setB).then_inc(slb, 1)
                    for m in range(KT):
                        act.wait_ge(done, m + 1)
                        if m >= 2:
                            act.wait_ge(freed2, m - 1)
                        act.activation(rows(tmp[:, m % 2, :]), bank_sets(m), ACT.Copy, scale=srow[:, m:m + 1])\
                           .then_inc(scaled, 1)

                @block.tensor
                def _(pe):
                    for stage in before:
                        stage.run("tensor", pe)
                    pe.wait_ge(lhs_done, 1)
                    broadcast_cols(pe, ps[:, 3:6, :], dcolq).then_inc(wide, 1)
                    for m in range(KT + 1):
                        if m < KT:
                            pe.wait_ge(topped, m + 1)
                            pe.transpose(ps[:, 6, 0:P], part, ident).then_inc(turned, 1)
                            pe.wait_ge(inv_diag, m + 1)
                            pe.matmul(ps[:, 7, 0:P], ones, dg, start=True, stop=True).then_inc(inv_wide, 1)
                        if m >= 1:
                            j = m - 1
                            pe.wait_ge(quant, j + 1)
                            if j == 1:
                                pe.wait_ge(slb, 1)
                            if j >= 2:
                                pe.wait_ge(scaled, j - 1)
                            for c in range(3):
                                for k in range(KT):
                                    last = pe.matmul(bank_sets(j)[:, c, :], wh[:, j % 4, P * k:P * k + P],
                                                     rh[:, k, CH * c:CH * c + CH], start=(k == 0), stop=(k == KT - 1))
                            last.then_inc(done, 1)

        def node_major(*before):
            name = "vh"
            then = (a["l1_kq"], ITEM, (90, 90))
            v4 = v_all.rearrange("p j (h f) -> p j h f", h=H)
            biases = spare["plain"][:, 0:2 * D].rearrange("p (g f) -> p g f", f=256)
            raw_in = [sem(f"{name}_raw{s}") for s in range(2)]
            split, tiles, freed = sem(name + "_split"), sem(name + "_tiles"), sem(name + "_banks_free")
            bias_in, h_ready, x_out = sem(name + "_bias"), sem(name + "_h_ready"), sem(name + "_x_out")
            h_out = [sem(f"{name}_h_stored{s}") for s in range(2)]
            hbuf = tmp[:, :, :].rearrange("p a b -> p (a b)")[:, 0:2560].rearrange("p (j f) -> p j f", j=TT)
            hbufs = (spare["plain"][:, 2 * D:2 * D + 2560].rearrange("p (j f) -> p j f", j=TT), hbuf)
            with nc.Block(name) as block:
                @block.sync
                def _(sp):
                    for stage in before:
                        stage.run("sync", sp)
                    stream_load(sp, a["l1_vh"], 16, ITEM, raw_in, split, 4, then)

                @block.gpsimd
                def _(pool):
                    stream_split(pool, name, 16, ITEM, raw_in, split, tiles, lambda i, q: i * 20 + (q // 2) * 10 + 10, 4,
                                 before=before, then=then)

                @block.tensor
                def _(pe):
                    pe.sem_inc(tiles, 2 * TT)
                    for stage in before:
                        stage.run("tensor", pe)
                    with pe.Fori(0, 4) as i:
                        for half in range(2):
                            pe.wait_ge(split, i * 4 + 2 * half + 2 + LEAD)
                            for j in range(TT):
                                t = TT * half + j
                                pe.wait_ge(freed, i * 20 + t + 1)
                                before[0].wait_nodes(pe, j)
                                for k in range(KT):
                                    s, c = 2 * half + k // 4, 256 * (k % 4)
                                    nodes = slice(P * j, P * j + P)
                                    last = mm3(pe, ps[:, TILE_BANKS[t % 4], 0:256], rh[:, k, nodes], rl[:, k, nodes],
                                               wh[:, s, c:c + 256], wl[:, s, c:c + 256], k == 0, k == KT - 1)
                                last.then_inc(tiles, 1)

                @block.vector
                def _(dve):
                    dve.sem_inc(freed, 4)
                    for stage in before:
                        stage.run("vector", dve)
                    dve.wait_ge(bias_in, 16)
                    with dve.Fori(0, 2) as i:
                        for half in range(2):
                            dve.wait_ge(h_out[half], i * 64 + 16)
                            brow = biases[:, ds(i * 2 + half, 1), :].rearrange("p a f -> p (a f)")
                            for j in range(TT):
                                dve.wait_ge(tiles, (i * 2 + half) * TT + j + 1 + 2 * TT)
                                dve.tensor_tensor(hbufs[half][:, j, :], ps[:, TILE_BANKS[(TT * half + j) % 4], 0:256], brow,
                                                  ALU.add).then_inc(freed, 1)
                            dve.wait_ge(freed, (i * 2 + half) * TT + TT + 4)
                            dve.sem_inc(h_ready, 1)
                    dve.wait_ge(x_out, 16)
                    dve.memset(v4[:, :, :, HD:VW], 1.0)
                    with dve.Fori(0, 2) as i:
                        for half in range(2):
                            brow = biases[:, ds(i * 2 + half + 4, 1), :].rearrange("p a (h f) -> p (a h) f", h=4)
                            for j in range(TT):
                                dve.wait_ge(tiles, (i * 2 + half + 4) * TT + j + 1 + 2 * TT)
                                dve.tensor_tensor(v4[:, j, ds((i * 2 + half) * 4, 4), 0:HD],
                                                  ps[:, TILE_BANKS[(TT * half + j) % 4], 0:256].rearrange("p (h f) -> p h f", h=4),
                                                  brow, ALU.add).then_inc(freed, 1)

                @block.scalar
                def _(act):
                    for stage in before:
                        stage.run("scalar", act)
                    for half in range(2):
                        act.sem_inc(h_out[half], 16)
                    act.dma_start(biases, a["l1_vh_bias"].rearrange("g p f -> p g f")).then_inc(bias_in, 16)
                    act.wait_ge(split, 4 + LEAD)
                    act.dma_start(x2_s, x_t).then_inc(x_out, 16)
                    with act.Fori(0, 2) as i:
                        for half in range(2):
                            g = i * 2 + half
                            act.wait_ge(h_ready, g + 1)
                            for u in range(2):
                                for part in range(2):
                                    act.dma_start(h_s[ds(g * 4 + 2 * u + part, 1)].rearrange("a p (k f) -> (a p) k f", k=5),
                                                  hbufs[half][:, 5 * part:5 * part + 5, P * u:P * u + P])\
                                       .then_inc(h_out[half], 16)
                    for half in range(2):
                        act.wait_ge(h_out[half], 128 + 16)

        def feature_attention():
            name = "fa"
            then = (h_s, 5 * P, (16 - 3 + SLOTS, 16 - 2 + SLOTS))
            guard = float(np.float32(1e-6)) * M
            space_a, space_b = spare["plain"][:, 0:7 * 512], spare["plain"][:, 7 * 512:]
            kf = space_a[:, 0:3 * 512].rearrange("p (s f) -> p s f", s=3)
            ex = space_a[:, 3 * 512:6 * 512].rearrange("p (s f) -> p s f", s=3)
            table = space_a[:, 6 * 512:7 * 512].rearrange("p (x f) -> p x f", x=4)
            qf = space_b[:, 0:4 * CH].rearrange("p (s f) -> p s f", s=4)
            ez = space_b[:, 4 * CH:5 * CH]
            rm = raw_extra[:, :]
            k_t, q_t = tmp[:, 0, :], tmp[:, 1, :]
            v4 = v_all.rearrange("p j (h f) -> p j h f", h=H)
            raw_in = [sem(f"{name}_raw{s}") for s in range(2)]
            stored = [sem(f"{name}_stored{s}") for s in range(2)]
            rm_in, split, used, k_in, q_in = (sem(name + x) for x in ("_rm_in", "_split", "_items_used", "_k", "_q"))
            kproj, kfeat, kv_used, tables = (sem(name + x) for x in ("_k_projected", "_k_features", "_kv", "_tables"))
            qproj, qfeat, outs, att = (sem(name + x) for x in ("_q_projected", "_q_features", "_outs", "_att"))
            relued, exped, ez_in, recip = (sem(name + x) for x in ("_relu", "_exp", "_norm", "_recip"))
            PIECES = 12
            ACTS = TT + PIECES

            def out_bank(c, h):
                return (3 if c % 2 == 0 else 1) + h

            def k_bank(w, j):
                b = (6, 1, 3)[j % 3]
                return ps[0:w, b:b + 2, 0:M]

            def halves_of(t, w, j):
                return t[0:w, j % 3, :].rearrange("p (h f) -> p h f", h=2)

            def k_ex(w, j):
                return halves_of(ex, w, j)

            def q_bank(x):
                return ((6, 7), (0, 5))[x // 2 % 2][x % 2]

            with nc.Block(name) as block:
                @block.sync
                def _(sp):
                    sp.dma_start(rm, a["rm"]).then_inc(rm_in, 16)
                    stream_load(sp, a["l1_kq"], 16, ITEM, raw_in, split, 4, then)

                @block.gpsimd
                def _(pool):
                    stream_split(pool, name, 16, ITEM, raw_in, split, used, lambda i, q: i * 4 + q + 1, 4, then=then)

                @block.tensor
                def _(pe):
                    pe.sem_inc(outs, 1)
                    pe.sem_inc(kv_used, 1)
                    pe.sem_inc(used, SLOTS)
                    pe.wait_ge(rm_in, 16)

                    def gemm(area, slot):
                        for c in range(3):
                            for k in range(KT):
                                f, t = slice(P * k, P * k + P), slice(CH * c, CH * c + CH)
                                last = mm3(pe, area[:, c, :], wh[:, slot, f], wl[:, slot, f], rh[:, k, t], rl[:, k, t],
                                           k == 0, k == KT - 1)
                        last.then_inc(used, 1)

                    def kv_product(n, p, i, j):
                        w = TOKS[j]
                        pe.wait_ge(kfeat, n * TT + j + 1)
                        for x in range(4):
                            last = pe.matmul(ps[:, 0, VW * x:VW * x + VW], kf[0:w, j % 3, P * x:P * x + P],
                                             v4[0:w, j, ds(i * 4 + 2 * p + x // 2, 1), :].rearrange("p a f -> p (a f)"),
                                             start=(j == 0 and x == 0), stop=(j == TT - 1), skip_group_check=True)
                        last.then_inc(kv_used, 1)

                    def out_product(n, x):
                        c, mh, h = x // 4, x // 2 % 2, x % 2
                        pe.wait_ge(qfeat, n * PIECES + x + 1 + 1)
                        if x == 0:
                            pe.wait_ge(tables, n + 1 + 1)
                        if x == 8:
                            pe.wait_ge(att, n * 3 + 2 + 1)
                        pe.matmul(ps[:, out_bank(c, h), 0:CH], table[:, 2 * h + mh, :], qf[:, x % 4, :],
                                  start=(mh == 0), stop=(mh == 1)).then_inc(outs, 1)

                    with pe.Fori(0, 4) as i:
                        for p in range(2):
                            n = i * 2 + p
                            pe.wait_ge(split, i * 4 + 2 * p + 1 + LEAD)
                            pe.wait_ge(tables, n + 1)
                            pe.wait_ge(att, n * 3 + 1)
                            gemm(setA, 2 * p)
                            pe.wait_ge(split, i * 4 + 2 * p + 2 + LEAD)
                            pe.wait_ge(att, n * 3 + 1 + 1)
                            gemm(setB, 2 * p + 1)
                            pe.wait_ge(k_in, n + 1)
                            for j in range(TT):
                                w = TOKS[j]
                                if j == 2:
                                    pe.wait_ge(q_in, n + 1)
                                if j >= 3:
                                    pe.wait_ge(kfeat, n * TT + j - 2)
                                for h in range(2):
                                    r = slice(HD * h, HD * h + HD)
                                    last = pe.matmul(k_bank(w, j)[:, h, :], k_t[r, P * j:P * j + w],
                                                     rm[r, :], start=True, stop=True)
                                last.then_inc(kproj, 1)
                                if j >= 2:
                                    kv_product(n, p, i, j - 2)
                            kv_product(n, p, i, TT - 2)
                            kv_product(n, p, i, TT - 1)
                            pe.wait_ge(q_in, n + 1)
                            for y in range(PIECES // 2):
                                c, mh = y // 2, y % 2
                                if y == 1:
                                    pe.wait_ge(tables, n + 1 + 1)
                                if y >= 2:
                                    pe.wait_ge(qfeat, n * PIECES + 2 * y - 2 + 1)
                                for h in range(2):
                                    r = slice(HD * h, HD * h + HD)
                                    pe.matmul(ps[:, q_bank(2 * y + h), 0:CH], rm[r, P * mh:P * mh + P],
                                              q_t[r, CH * c:CH * c + CH], start=True, stop=True).then_inc(qproj, 1)
                                if y:
                                    out_product(n, 2 * y - 2)
                                    out_product(n, 2 * y - 1)
                            out_product(n, PIECES - 2)
                            out_product(n, PIECES - 1)

                @block.scalar
                def _(act):
                    for p in range(2):
                        act.sem_inc(stored[p], 16)
                    def relu_exp(dst, src, count):
                        act.activation(dst, src, ACT.Relu, scale=-1.0).then_inc(relued, 1)
                        act.wait_ge(relued, count)
                        act.activation(dst, dst, ACT.Exp, scale=-1.0).then_inc(exped, 1)

                    with act.Fori(0, 4) as i:
                        for p in range(2):
                            n = i * 2 + p
                            for j in range(TT):
                                w = TOKS[j]
                                if j < 3:
                                    act.wait_ge(qfeat, n * PIECES + 1)
                                else:
                                    act.wait_ge(kfeat, n * TT + j - 2)
                                act.wait_ge(kproj, n * TT + j + 1)
                                relu_exp(k_ex(w, j), k_bank(w, j), n * ACTS + j + 1)
                            for x in range(PIECES):
                                if x < 3:
                                    act.wait_ge(kfeat, n * TT + TT)
                                else:
                                    act.wait_ge(qfeat, n * PIECES + x - 2 + 1)
                                act.wait_ge(qproj, n * PIECES + x + 1)
                                relu_exp(ex[:, x % 3, 0:CH], ps[:, q_bank(x), 0:CH], n * ACTS + TT + x + 1)
                            act.wait_ge(att, n * 3 + 4 + 1)
                            act.dma_start(att_s[ds(n, 1)].rearrange("a p f -> (a p) f"), tmp[:, 2 + p, :])\
                               .then_inc(stored[p], 16)
                    for p in range(2):
                        act.wait_ge(stored[p], 64 + 16)

                @block.vector
                def _(dve):
                    dve.sem_inc(qfeat, 1)
                    dve.sem_inc(tables, 1)
                    dve.sem_inc(att, 2)
                    lo, hi = slice(0, HD), slice(HD, P)

                    def divide(n, p, c):
                        m, cols = n * 3 + c, slice(CH * c, CH * c + CH)
                        a_b, b_b = ps[:, out_bank(c, 0), 0:CH], ps[:, out_bank(c, 1), 0:CH]
                        dve.wait_ge(outs, n * PIECES + 4 * c + 4 + 1)
                        dve.wait_ge(att, m + 1 + 1)
                        dve.tensor_scalar(ez[lo, :], a_b[hi, :], guard, None, ALU.max).then_inc(ez_in, 1)
                        dve.tensor_scalar(ez[hi, :], b_b[lo, :], guard, None, ALU.max).then_inc(ez_in, 1)
                        dve.wait_ge(ez_in, m * 2 + 2)
                        dve.reciprocal(ez, ez).then_inc(recip, 1)
                        dve.wait_ge(recip, m + 1)
                        dve.tensor_tensor(tmp[lo, 2 + p, cols], a_b[lo, :], ez[lo, :], ALU.mult)
                        dve.tensor_tensor(tmp[hi, 2 + p, cols], b_b[hi, :], ez[hi, :], ALU.mult).then_inc(att, 1)

                    with dve.Fori(0, 4) as i:
                        for p in range(2):
                            n = i * 2 + p
                            for half, (area, dst, done, b) in enumerate(((setA, k_t, k_in, 2), (setB, q_t, q_in, 3))):
                                dve.wait_ge(used, i * 4 + 2 * p + half + 1 + SLOTS)
                                dve.tensor_scalar(rows(dst), area, bcol[:, b, ds(n, 1)], None, ALU.add)\
                                   .then_inc(done, 1)
                            for j in range(TT):
                                w = TOKS[j]
                                dve.wait_ge(kv_used, n * TT + max(j - 2, 0) + 1)
                                dve.wait_ge(exped, n * ACTS + j + 1)
                                dve.scalar_tensor_tensor(halves_of(kf, w, j), k_bank(w, j), 0.0, k_ex(w, j), ALU.max,
                                                         ALU.add).then_inc(kfeat, 1)
                            dve.wait_ge(kv_used, n * TT + TT + 1)
                            kv = ps[:, 0, 0:4 * VW].rearrange("p (x f) -> p x f", x=4)
                            dve.tensor_copy(table[:, 0:2, lo], kv[:, 0:2, 0:HD])
                            dve.tensor_copy(table[:, 2:4, hi], kv[:, 2:4, 0:HD])
                            for x in range(4):
                                ins = dve.tensor_scalar(table[:, x, hi if x < 2 else lo], ones[:, 0:HD],
                                                        kv[:, x, HD:VW], None, ALU.mult)
                            ins.then_inc(tables, 1)
                            dve.wait_ge(stored[p], i * 16 + 16)
                            for x in range(PIECES):
                                dve.wait_ge(outs, n * PIECES + max(x - 3, 0) + 1)
                                dve.wait_ge(exped, n * ACTS + TT + x + 1)
                                dve.scalar_tensor_tensor(qf[:, x % 4, :], ps[:, q_bank(x), 0:CH], 0.0,
                                                         ex[:, x % 3, 0:CH], ALU.max, ALU.add).then_inc(qfeat, 1)
                                if x % 4 == 1 and x > 4:
                                    divide(n, p, x // 4 - 1)
                            divide(n, p, 2)

        def gating(norm):
            name = "gate"
            ws = spare["gate"][:, 0:KT * NEXP]
            bs = spare["gate"][:, KT * NEXP:(KT + TT) * NEXP].rearrange("p (j e) -> p j e", j=TT)
            W2 = 2 * NEXP
            both_w, high_w = (spare["gate_halves"][:, KT * W2 * n:KT * W2 * (n + 1)].rearrange("p (k e) -> p k e", k=KT)
                              for n in range(2))
            ws3 = ws.rearrange("p (k e) -> p k e", k=KT)
            by_expert = tmp[:, 2:4, :].rearrange("p a b -> p (a b)")[0:W2, 0:NR]
            by_node = ps[:, 6, 0:TT * W2].rearrange("p (j e) -> p j e", j=TT)
            moved, across = sem(name + "_moved"), sem(name + "_across")
            work = spare["gate_work"]

            def grid(n):
                return work[:, TT * NEXP * n:TT * NEXP * (n + 1)].rearrange("p (j e) -> p j e", j=TT)

            logits, is_top, first, second, rank = (grid(n) for n in range(5))
            t0 = TT * NEXP * 5
            top1, top2, pick, e2, total = (work[:, t0 + TT * n:t0 + TT * n + TT].rearrange("p (j o) -> p j o", o=1)
                                           for n in range(5))
            high = spare["gate_halves"][:, 4 * KT * NEXP:(4 * KT + TT) * NEXP].rearrange("p (j e) -> p j e", j=TT)
            both = tmp[:, 3, 100:100 + 40 * TT].rearrange("p (j e) -> p j e", j=TT)
            loaded, halves, products, gap, ratio = (sem(name + x) for x in
                                                    ("_loaded", "_halves", "_logits", "_gap", "_ratio"))
            ready, turned, placed = sem(name + "_ready"), sem(name + "_turned"), sem(name + "_placed")
            def sync(sp):
                sp.dma_start(ws, a["Ws"]).then_inc(loaded, 16)
                sp.dma_start(bs, a["bs"].rearrange("p (j e) -> p j e", j=TT)).then_inc(loaded, 16)

            def tensor(pe):
                pe.wait_ge(halves, 1)
                for c in range(3):
                    cols = slice(CH * c, CH * c + CH)
                    pe.wait_ge(norm.done, KT * (c + 1))
                    for k in range(KT):
                        pe.matmul(setA[0:W2, c, :], both_w[:, k, :], rh[:, k, cols], start=(k == 0), stop=False)
                        last = pe.matmul(setA[0:W2, c, :], high_w[:, k, :], rl[:, k, cols], start=False, stop=(k == KT - 1))
                last.then_inc(products, 1)
                pe.wait_ge(moved, 1)
                pe.wait_ge(halves, 2)
                for j in range(TT):
                    last = pe.transpose(by_node[:, j, :], by_expert[:, P * j:P * j + P], ident[0:W2, 0:W2])
                last.then_inc(across, 1)

            def turn(pe):
                pe.wait_ge(ready, 1)
                for j in range(TT):
                    last = pe.transpose(ps[0:40, (6, 7, 0)[j // 4], P * (j % 4):P * (j % 4) + P], both[:, j, :], ident)
                last.then_inc(turned, 1)

            def vector(dve):
                link = Chain(dve, name + "_chain")

                def wide(fn, out, full, narrow, *ops):
                    f, n = bass.broadcast_tensor_aps(full, narrow)
                    return fn(out, f, n, *ops)

                iota8 = cst[:, C_IOTA8:C_IOTA8 + NEXP].rearrange("p (o e) -> p o e", o=1)
                dve.wait_ge(loaded, 32)
                dve.memset(high_w.bitcast(F32), 0.0)
                link(dve.tensor_copy(both_w[:, :, 0:NEXP], ws3))
                dve.tensor_copy(high_w[:, :, 0:NEXP], both_w[:, :, 0:NEXP].bitcast(F32))
                dve.tensor_tensor(both_w[:, :, NEXP:W2], ws3, both_w[:, :, 0:NEXP].bitcast(F32), ALU.subtract)\
                   .then_inc(halves, 1)
                dve.wait_ge(norm.done, KT * 3)
                dve.memset(both, 0.0)
                dve.memset(by_expert[:, NT:NR], 0.0).then_inc(halves, 1)
                dve.wait_ge(across, 1)
                link(dve.tensor_tensor(logits, by_node[:, :, 0:NEXP], bs, ALU.add))
                link(dve.tensor_tensor(logits, by_node[:, :, NEXP:W2], logits, ALU.add))

                def choose(one_hot, top, best):
                    link(dve.tensor_reduce(top, logits, AX.X, ALU.max))
                    link(wide(dve.tensor_tensor, is_top, logits, top, ALU.is_equal))
                    link(wide(dve.tensor_tensor, rank, is_top, iota8, ALU.mult))
                    link(dve.tensor_reduce(best, rank, AX.X, ALU.max))
                    link(wide(dve.tensor_tensor, one_hot, rank, best, ALU.is_equal))

                choose(first, top1, pick)
                big = float(np.finfo(np.float32).max)
                link(dve.tensor_scalar(is_top, first, -2.0, 1.0, ALU.mult, ALU.add))
                link(dve.scalar_tensor_tensor(logits, is_top, big, logits, ALU.mult, ALU.min))
                choose(second, top2, pick)
                dve.tensor_tensor(e2, top2, top1, ALU.subtract).then_inc(gap, 1)
                dve.wait_ge(ratio, 1)
                link(dve.tensor_scalar(total, e2, 1.0, None, ALU.add))
                link(dve.reciprocal(total, total))
                link(dve.tensor_tensor(e2, e2, total, ALU.mult))
                link(wide(dve.tensor_tensor, first, first, total, ALU.mult))
                link(wide(dve.tensor_tensor, second, second, e2, ALU.mult))
                link(dve.tensor_tensor(first, first, second, ALU.add))
                link(dve.tensor_copy(high, first))
                dve.tensor_copy(both[:, :, 0:NEXP], high.bitcast(F32))
                dve.tensor_tensor(both[:, :, 32:32 + NEXP], first, high.bitcast(F32), ALU.subtract).then_inc(ready, 1)
                dve.wait_ge(turned, 1)
                dve.tensor_copy(wh[0:40, 3, 0:512], ps[0:40, 6, :])
                dve.tensor_copy(wh[0:40, 3, 512:2 * CH], ps[0:40, 7, 0:2 * CH - 512])
                dve.tensor_copy(wl[0:40, 3, 0:D - 2 * CH], ps[0:40, 7, 2 * CH - 512:512])
                dve.tensor_copy(wl[0:40, 3, D - 2 * CH:CH], ps[0:40, 0, 0:NT - D]).then_inc(placed, 1)

            def scalar(act):
                act.wait_ge(products, 1)
                act.copy(by_expert[:, 0:NT].rearrange("p (c t) -> p c t", c=3), setA[0:W2]).then_inc(moved, 1)
                act.wait_ge(gap, 1)
                act.activation(e2, e2, ACT.Exp).then_inc(ratio, 1)
            return Stage(vector=vector, scalar=scalar, tensor=tensor, sync=sync, turn=turn, done=placed)

        def experts(*before):
            name = "moe"
            raw_in = [sem(f"{name}_raw{s}") for s in range(2)]
            split, used, sel_in, sel_set = (sem(name + x) for x in ("_split", "_items_used", "_sel_in", "_selector"))
            wide, gated, weighed, hidden = (sem(name + x) for x in ("_wide", "_gated", "_weighed", "_hidden"))
            high, low, y_done, added = (sem(name + x) for x in ("_high", "_low", "_y_products", "_y_added"))
            stored = sem("out_stored")
            sel = wl[0:40, 3, 512:512 + 2 * P]
            sel_raw = raw_extra[0:40, :]
            STEPS, YS = FT // 2, 2 * KT

            def weights_of(c):
                return wh[0:40, 3, CH * c:CH * c + CH] if c < 2 else wl[0:40, 3, 0:CH]

            with nc.Block(name) as block:
                @block.sync
                def _(sp):
                    for stage in before:
                        stage.run("sync", sp)
                    stream_load(sp, a["moe"], 6 * STEPS, ITEM, raw_in, split, 6)
                    for m in range(KT):
                        sp.wait_ge(added, (STEPS - 1) * YS + KT + m + 1 + 2)
                        sp.dma_start(out[:, m, :], x_t[:, m, :]).then_inc(stored, 16)
                    sp.wait_ge(stored, 16 * KT)

                @block.gpsimd
                def _(pool):
                    stream_split(pool, name, 6 * STEPS, ITEM, raw_in, split, used, lambda i, q: i * 6 + q + 1, 6, slots=3,
                                 before=before)

                @block.tensor
                def _(pe):
                    pe.sem_inc(used, 3)
                    for stage in before:
                        stage.run("tensor", pe)

                    def gemm(area, slot, c):
                        for k in range(KT):
                            f, t = slice(P * k, P * k + P), slice(CH * c, CH * c + CH)
                            last = mm3(pe, area[:, c, :], wh[:, slot, f], wl[:, slot, f], rh[:, k, t], rl[:, k, t],
                                       k == 0, k == KT - 1)
                        return last

                    def spread(x, c):
                        pe.matmul(ps[:, 6 + c % 2, 0:CH], sel[:, P * x:P * x + P], weights_of(c), start=True, stop=True)\
                          .then_inc(wide, 1)

                    def step(i, first):
                        for x in range(2):
                            pe.wait_ge(split, i * 6 + 2 * x + 1 + LEAD)
                            if x == 0:
                                pe.wait_ge(added, i * YS + 1)
                            else:
                                pe.wait_ge(gated, i * 2 + 1)
                            gemm(setA, 2 * x % 3, 0)
                            if x:
                                pe.wait_ge(weighed, i * 6 + 1 + 1)
                                spread(0, 2)
                            gemm(setA, 2 * x % 3, 1)
                            gemm(setA, 2 * x % 3, 2).then_inc(used, 1)
                            if x:
                                pe.wait_ge(weighed, i * 6 + 3 + 1)
                                spread(1, 0)
                                spread(1, 1)
                            pe.wait_ge(split, i * 6 + 2 * x + 2 + LEAD)
                            if x == 0:
                                pe.wait_ge(added, i * YS + 2)
                            else:
                                pe.wait_ge(hidden, i * 2 + 1 + 1)
                            gemm(setB, (2 * x + 1) % 3, 0)
                            gemm(setB, (2 * x + 1) % 3, 1)
                            if x:
                                pe.wait_ge(weighed, i * 6 + 3 + 1 + 1)
                                spread(1, 2)
                            gemm(setB, (2 * x + 1) % 3, 2).then_inc(used, 1)
                            if x == 0:
                                if first:
                                    pe.wait_ge(gated, 1)
                                    before[-1].programs["turn"](pe)
                                    pe.wait_ge(before[-1].done, 1)
                                pe.wait_ge(sel_set, i + 1 + 1)
                                pe.wait_ge(weighed, i * 6 + 1)
                                spread(0, 0)
                                spread(0, 1)
                        for n in range(YS):
                            x, m = n // KT, n % KT
                            if m == 0:
                                pe.wait_ge(split, i * 6 + 5 + x + LEAD)
                                pe.wait_ge(low, i * 2 + x + 1 + 1)
                            if n == 0:
                                pe.wait_ge(gated, i * 2 + 2)
                            elif n == 1:
                                pe.wait_ge(hidden, i * 2 + 2 + 1)
                            else:
                                pe.wait_ge(added, i * YS + n + 1)
                            for c in range(3):
                                f, t = slice(P * m, P * m + P), slice(CH * c, CH * c + CH)
                                last = mm3(pe, bank_sets(m)[:, c, :], wh[:, 1 + x, f], wl[:, 1 + x, f],
                                           high_of(KT + x)[:, t], low_of(KT + x)[:, t], True, True)
                            last.then_inc(y_done, 1)
                            if m == KT - 1:
                                pe.wait_ge(y_done, i * YS + n + 1)
                                pe.sem_inc(used, 1)

                    step(0, True)
                    with pe.Fori(1, STEPS) as i:
                        step(i, False)

                @block.scalar
                def _(act):
                    for stage in before:
                        stage.run("scalar", act)
                    act.sem_inc(sel_set, 1)
                    with act.Fori(0, STEPS) as i:
                        act.wait_ge(sel_set, i + 1)
                        act.dma_start(sel_raw, a["sel"][ds(i, 1)].rearrange("a p f -> (a p) f")).then_inc(sel_in, 16)
                        act.wait_ge(sel_in, i * 16 + 16)
                        act.wait_ge(weighed, i * 6 + 1)
                        act.copy(sel, sel_raw).then_inc(sel_set, 1)
                        for x in range(2):
                            act.wait_ge(used, i * 6 + 2 * x + 1 + 3)
                            act.wait_ge(low, i * 2 + x + 1)
                            act.activation(rows(tmp[:, x, :]), setA, ACT.Silu).then_inc(gated, 1)
                            act.wait_ge(hidden, i * 2 + x + 1 + 1)
                            act.copy(high_of(KT + x), tmp[:, 2 + x, :]).then_inc(high, 1)

                @block.vector
                def _(dve):
                    dve.sem_inc(low, 1)
                    dve.sem_inc(hidden, 1)
                    dve.sem_inc(weighed, 1)
                    dve.sem_inc(added, 2)
                    for stage in before:
                        stage.run("vector", dve)
                    with dve.Fori(0, STEPS) as i:
                        def low_half(x):
                            dve.wait_ge(high, i * 2 + x + 1)
                            dve.tensor_tensor(low_of(KT + x), tmp[:, 2 + x, :], high_of(KT + x).bitcast(F32),
                                              ALU.subtract).then_inc(low, 1)

                        def add(n):
                            dve.wait_ge(y_done, i * YS + n + 1)
                            xm = rows(x_t[:, n % KT, :])
                            dve.tensor_tensor(xm, bank_sets(n), xm, ALU.add).then_inc(added, 1)

                        for x in range(2):
                            dve.wait_ge(gated, i * 2 + x + 1)
                            for c in range(3):
                                s = tmp[:, x, CH * c:CH * c + CH]
                                dve.wait_ge(wide, i * 6 + 3 * x + c + 1)
                                dve.tensor_tensor(s, s, ps[:, 6 + c % 2, 0:CH], ALU.mult).then_inc(weighed, 1)
                            dve.wait_ge(used, i * 6 + 2 * x + 2 + 3)
                            dve.wait_ge(weighed, i * 6 + 3 * x + 3 + 1)
                            dve.tensor_tensor(rows(tmp[:, 2 + x, :]), rows(tmp[:, x, :]), setB, ALU.mult)\
                               .then_inc(hidden, 1)
                            if x:
                                add(0)
                            low_half(x)
                        for n in range(1, YS):
                            add(n)

        raw_extra = sb("bias_rows", [P, 256], F32)
        v_all = xres[:, 0:TT * H * VW].rearrange("p (j f) -> p j f", j=TT)
        kvt = xres[:, 5200:5200 + 8 * 256].rearrange("p (m f) -> p m f", m=8)
        setup()
        end_phase()
        with_scratch("graph", lambda: (graph(), end_phase(), linear_kv(layernorm("ln0", sums_at=spare["plain"][:, NT:2 * NT]))), 6120)
        end_phase()
        linear_out()
        end_phase()
        with_kept_rows(lambda: (product("sparse", wg_s, 0, load=a["x_t"], fetch=KT, following=a["l0_o"]), end_phase(), product("out0", a["l0_o"], 1, prep=FromAttention("out0_prep", KT), sums=True)))
        end_phase()
        with_scratch("ffn8", lambda: int8_product(layernorm("ln1", quantise=True)))
        end_phase()
        with_scratch("vh", lambda: node_major(layernorm("ln2", unsummed=(KT - 2, KT - 1))))
        end_phase()
        with_scratch("fa", feature_attention, 6120)
        end_phase()
        with_two_more_tiles("gcn", lambda: product("gcn", h_s, None, k_tiles=TT, per=5 * P, parts=2, load=x2_s, fetch=4, following=a["l1_o"], prep=FromCounts("gcn_prep")))
        end_phase()
        product("out1", a["l1_o"], 4, prep=FromAttention("out1_prep", 4), sums=True)
        end_phase()
        with_gate(lambda: (lambda norm: experts(norm, gating(norm)))(layernorm("ln3")))
        end_phase()


def layout(v):
    f = np.float32
    x_t = np.zeros((P, KT, NT), f)
    x_t[:, :, :N] = v["x"].T.reshape(KT, P, N).transpose(1, 0, 2)

    def stat(w):
        k, m = w.shape
        return np.ascontiguousarray(w.reshape(k // P, P, m // P, P).transpose(2, 1, 0, 3)).reshape(m // P, P, k)

    def mov(w):
        k, m = w.shape
        return np.ascontiguousarray(w.reshape(2, 4, P, m // 256, 256).transpose(3, 0, 2, 1, 4)).reshape(-1, P, ITEM)

    def bc(b):
        return b.reshape(-1, P).T

    consts = np.zeros((P, C_ALL), f)
    consts[:, C_ID:C_ID + P] = np.eye(P)
    consts[:, C_ONE:C_ONE + P] = 1
    consts[:, C_MEAN:C_MEAN + P] = 1.0 / D
    consts[:64, C_MASK:C_MASK + 64] = 1
    consts[64:, C_MASK + 64:C_MASK + P] = 1
    consts[:, C_IOTA8:C_IOTA8 + 8] = 8 - np.arange(8)
    bias_cols = np.zeros((P, 8, KT), f)
    for n, name in enumerate(["L0_gnn_bias", "L0_mix_bo", "L1_mix_bk", "L1_mix_bq", "L1_mix_bo"]):
        bias_cols[:, n, :] = bc(v[name])
    o = {
        "consts": consts, "bias_cols": bias_cols, "x_t": x_t,
        "iota": np.tile(np.arange(NR, dtype=f), (P, 1)), 
        "src": np.ascontiguousarray(v["src"].reshape(ET, EP).T), "dst": np.ascontiguousarray(v["dst"].reshape(ET, EP).T),
        "edge_w": np.ascontiguousarray(v["edge_weight"].reshape(ET, EP).T),
    }
    def pairs(*ws):
        return np.ascontiguousarray(np.stack([w.reshape(4, -1, P, ITEM) for w in ws], 1)).reshape(-1, P, ITEM)

    o["l0_kv"] = pairs(mov(v["L0_mix_Wk"]), mov(v["L0_mix_Wv"]))
    o["l0_q"] = stat(v["L0_mix_Wq"])
    o["l0_o"] = stat(v["L0_mix_Wo"])
    o["ffn_rhs"] = stat(v["L0_ffn_rhs"])
    o["l1_vh"] = np.concatenate([mov(np.ascontiguousarray(v["L1_gnn_W"].T)), mov(v["L1_mix_Wv"])])
    vh = np.concatenate([v["L1_gnn_b"], v["L1_mix_bv"]]).reshape(8, 1, 256)
    o["l1_vh_bias"] = np.ascontiguousarray(np.broadcast_to(vh, (8, P, 256)))
    kq = np.stack([stat(v["L1_mix_Wk"]), stat(v["L1_mix_Wq"])], 1)
    o["l1_kq"] = np.ascontiguousarray(kq).reshape(2 * KT, P, ITEM)
    o["l1_o"] = stat(v["L1_mix_Wo"])
    ws = v["L1_ffn_Ws"].reshape(KT, P, NEXP).transpose(1, 0, 2)
    o["Ws"] = np.ascontiguousarray(ws).reshape(P, KT * NEXP)
    o["bs"] = np.tile(v["L1_ffn_bs"], (P, TT))
    hid = NEXP * FF
    gu = np.zeros((2, D, FT * P), f)
    gu[0, :, :hid] = v["L1_ffn_Wg"].transpose(1, 0, 2).reshape(D, hid)
    gu[1, :, :hid] = v["L1_ffn_Wu"].transpose(1, 0, 2).reshape(D, hid)
    down = np.zeros((FT * P, D), f)
    down[:hid] = v["L1_ffn_Wd"].reshape(hid, D)
    moe = np.zeros((FT // 2, 6, P, ITEM), f)
    moe[:, 0:4:2] = stat(gu[0]).reshape(FT // 2, 2, P, ITEM)
    moe[:, 1:4:2] = stat(gu[1]).reshape(FT // 2, 2, P, ITEM)
    moe[:, 4:6] = down.reshape(FT // 2, 2, P, ITEM)
    o["moe"] = moe.reshape(-1, P, ITEM)
    owner = (np.arange(FT * P) // FF).reshape(FT // 2, 1, 2 * P)
    sel = np.zeros((FT // 2, 40, 2 * P), f)
    sel[:, 0:NEXP] = sel[:, 32:32 + NEXP] = owner == np.arange(NEXP).reshape(1, NEXP, 1)
    o["sel"] = sel
    o["rm"] = np.tile(v["L1_mix_random_matrix"], (2, 1))
    return o


def kernel(**inputs):
    from concourse import bacc
    from concourse.bass_utils import run_bass_kernel_spmd

    arrays = layout({k: np.asarray(v) for k, v in inputs.items()})
    nc = bacc.Bacc("TRN2", target_bir_lowering=False, num_devices=1)
    a = {k: nc.dram_tensor(k, v.shape, mybir.dt.from_np(v.dtype), kind="ExternalInput").ap() for k, v in arrays.items()}
    out = nc.dram_tensor("out", (P, KT, NT), F32, kind="ExternalOutput").ap()
    gps_kernel(nc, a, out)
    got = run_bass_kernel_spmd(nc, [arrays], core_ids=[0]).results[0]["out"]
    return np.ascontiguousarray(got.transpose(1, 0, 2).reshape(D, NT)[:, :N].T)
```
